# Optimizing a Trainium2 kernel written in Bass

```python
import numpy as np
import jax
import jax.numpy as jnp

def _softmax(x, axis=-1):
    return jax.nn.softmax(x, axis=axis)

def _gelu(x):
    return jax.nn.gelu(x, approximate=True)

def _silu(x):
    return jax.nn.silu(x)

def _sigmoid(x):
    return jax.nn.sigmoid(x)

def _layernorm(x, axis=-1, eps=1e-05):
    m = jnp.mean(x, axis=axis, keepdims=True)
    v = jnp.var(x, axis=axis, keepdims=True)
    return (x - m) / jnp.sqrt(v + eps)

def _scatter_add(tgt, idx, src, axis=0):
    return tgt.at[idx].add(src)

def _segment_sum(src, seg, n):
    return jax.ops.segment_sum(src, seg, n)
kernel_name = 'mk_gnn_resnorm_d4_gnn_r64_c64728'

def setup_inputs(seed: int=0):
    np.random.seed(seed)
    _w = jnp.asarray

    def _rec_inputs():
        import jax
        import jax.numpy as jnp
        _gk = jax.random.key(seed)
        x = -0.000202 + 1 * jax.random.normal(jax.random.fold_in(_gk, 1), (100000, 64), jnp.float32)
        src = jax.random.randint(jax.random.fold_in(_gk, 2), (25000,), 0, 100000, jnp.int32)
        dst = jnp.minimum((100000 * jax.random.uniform(jax.random.fold_in(_gk, 3), (25000,)) ** 2.0).astype(jnp.int32), 99999)
        _o = jnp.argsort(dst, stable=True)
        src = src[_o]
        dst = dst[_o]
        edge_attr_32 = -9.77346e-05 + 0.999888 * jax.random.normal(jax.random.fold_in(_gk, 12), (25000, 32), jnp.float32)
        edge_attr_8 = 0.000254156 + 0.999948 * jax.random.normal(jax.random.fold_in(_gk, 13), (25000, 8), jnp.float32)
        edge_type_16 = jax.random.randint(jax.random.fold_in(_gk, 15), (25000,), 0, 16, jnp.int32)
        edge_weight1 = jax.random.uniform(jax.random.fold_in(_gk, 16), (25000, 1), jnp.float32, 0.0, 0.999999)
        return (x, src, dst, edge_attr_32, edge_attr_8, edge_type_16, edge_weight1)
    x, src, dst, edge_attr_32, edge_attr_8, edge_type_16, edge_weight1 = _rec_inputs()

    def _L0_gnn_setup():
        import jax, jax.numpy as jnp
        import numpy as np
        N = 100000
        E = 25000
        IN = 64
        OUT = 64
        ED = 8
        H1 = OUT
        H2 = OUT // 2
        NEG_SLOPE = 0.01
        key = jax.random.key(seed)
        ks = jax.random.split(key, 16)
        s = 0.05
        x = jax.random.normal(ks[0], (N, IN), dtype=jnp.float32)
        edge_index = jax.random.randint(ks[1], (2, E), 0, N, dtype=jnp.int64)
        edge_attr = jax.random.normal(ks[2], (E, ED), dtype=jnp.float32)
        W_src = jax.random.normal(ks[3], (OUT, IN), dtype=jnp.float32) * s
        b_src = jnp.zeros((OUT,), jnp.float32)
        W_tgt = jax.random.normal(ks[4], (OUT, IN), dtype=jnp.float32) * s
        b_tgt = jnp.zeros((OUT,), jnp.float32)
        W_edge = jax.random.normal(ks[5], (OUT, ED), dtype=jnp.float32) * s
        b_edge = jnp.zeros((OUT,), jnp.float32)
        W1 = jax.random.normal(ks[6], (H1, 3 * OUT), dtype=jnp.float32) * s
        b1 = jnp.zeros((H1,), jnp.float32)
        W2 = jax.random.normal(ks[7], (H2, H1), dtype=jnp.float32) * s
        b2 = jnp.zeros((H2,), jnp.float32)
        W3 = jax.random.normal(ks[8], (1, H2), dtype=jnp.float32) * s
        b3 = jnp.zeros((1,), jnp.float32)
        return dict(x=x, edge_index=edge_index, edge_attr=edge_attr, W_src=W_src, b_src=b_src, W_tgt=W_tgt, b_tgt=b_tgt, W_edge=W_edge, b_edge=b_edge, W1=W1, b1=b1, W2=W2, b2=b2, W3=W3, b3=b3)
    _L0_gnn_all = _L0_gnn_setup()
    _L0_gnn_in = {k: v for k, v in _L0_gnn_all.items() if k in ('W_src', 'b_src', 'W_tgt', 'b_tgt', 'W_edge', 'b_edge', 'W1', 'b1', 'W2', 'b2', 'W3', 'b3')}
    del _L0_gnn_all

    def _L1_gnn_setup():
        import jax, jax.numpy as jnp
        import numpy as np
        N_NODES = 100000
        N_EDGES = 25000
        IN_FEAT = 64
        OUT_FEAT = 64
        key = jax.random.key(seed)
        ks = jax.random.split(key, 8)
        feature = jax.random.normal(ks[0], (N_NODES, IN_FEAT), dtype=jnp.float32)
        src = jax.random.randint(ks[1], (N_EDGES,), 0, N_NODES, dtype=jnp.int32)
        dst = jax.random.randint(ks[2], (N_EDGES,), 0, N_NODES, dtype=jnp.int32)
        W_out = jax.random.normal(ks[3], (IN_FEAT, OUT_FEAT), dtype=jnp.float32) / np.sqrt(IN_FEAT)
        b_out = jax.random.normal(ks[4], (OUT_FEAT,), dtype=jnp.float32) / np.sqrt(IN_FEAT)
        attn_w = jax.random.normal(ks[5], (2 * OUT_FEAT,), dtype=jnp.float32) / np.sqrt(2 * OUT_FEAT)
        res_W = jax.random.normal(ks[6], (IN_FEAT, OUT_FEAT), dtype=jnp.float32) / np.sqrt(IN_FEAT)
        res_b = jax.random.normal(ks[7], (OUT_FEAT,), dtype=jnp.float32) / np.sqrt(IN_FEAT)
        return {'feature': feature, 'src': src, 'dst': dst, 'W_out': W_out, 'b_out': b_out, 'attn_w': attn_w, 'res_W': res_W, 'res_b': res_b}
    _L1_gnn_all = _L1_gnn_setup()
    _L1_gnn_in = {k: v for k, v in _L1_gnn_all.items() if k in ('W_out', 'b_out', 'attn_w', 'res_W', 'res_b')}
    del _L1_gnn_all

    def _L2_gnn_setup():
        import jax, jax.numpy as jnp
        import numpy as np
        N_NODES = 100000
        N_EDGES = 25000
        NODE_IN = 64
        EDGE_DIM = 32
        NODE_OUT = 64
        key = jax.random.key(seed)
        ks = jax.random.split(key, 8)
        return {'nfeats': jax.random.normal(ks[0], (N_NODES, NODE_IN), dtype=jnp.float32), 'efeats': jax.random.normal(ks[1], (N_EDGES, EDGE_DIM), dtype=jnp.float32), 'src': jax.random.randint(ks[2], (N_EDGES,), 0, N_NODES, dtype=jnp.int32), 'dst': jax.random.randint(ks[3], (N_EDGES,), 0, N_NODES, dtype=jnp.int32), 'W_msg_w': jax.random.normal(ks[4], (NODE_IN + EDGE_DIM, NODE_OUT), dtype=jnp.float32) * 0.1, 'W_msg_b': jax.random.normal(ks[5], (NODE_OUT,), dtype=jnp.float32) * 0.1, 'W_apply_w': jax.random.normal(ks[6], (NODE_IN + NODE_OUT, NODE_OUT), dtype=jnp.float32) * 0.1, 'W_apply_b': jax.random.normal(ks[7], (NODE_OUT,), dtype=jnp.float32) * 0.1}
    _L2_gnn_all = _L2_gnn_setup()
    _L2_gnn_in = {k: v for k, v in _L2_gnn_all.items() if k in ('W_msg_w', 'W_msg_b', 'W_apply_w', 'W_apply_b')}
    del _L2_gnn_all

    def _L3_gnn_setup():
        import jax, jax.numpy as jnp
        import numpy as np
        N_NODES = 50000
        N_EDGES = 25000
        REL_NUM = 16
        D_IN = 64
        D_OUT = 64
        key = jax.random.key(seed)
        k_h, k_w, k_n, k_s, k_d, k_r = jax.random.split(key, 6)
        h = jax.random.normal(k_h, (N_NODES, D_IN), dtype=jnp.float32)
        limit = float(np.sqrt(6.0 / (D_IN + D_OUT)))
        weight = jax.random.uniform(k_w, (REL_NUM, D_IN, D_OUT), dtype=jnp.float32, minval=-limit, maxval=limit)
        norm = jax.random.uniform(k_n, (N_EDGES, 1), dtype=jnp.float32)
        src = jax.random.randint(k_s, (N_EDGES,), 0, N_NODES)
        dst = jax.random.randint(k_d, (N_EDGES,), 0, N_NODES)
        rel_type = jax.random.randint(k_r, (N_EDGES,), 0, REL_NUM)
        return {'h': h, 'weight': weight, 'norm': norm, 'src': src, 'dst': dst, 'rel_type': rel_type}
    _L3_gnn_all = _L3_gnn_setup()
    _L3_gnn_in = {k: v for k, v in _L3_gnn_all.items() if k in ('weight',)}
    del _L3_gnn_all
    return {'x': x, 'src': src, 'dst': dst, 'edge_attr_32': edge_attr_32, 'edge_attr_8': edge_attr_8, 'edge_type_16': edge_type_16, 'edge_weight1': edge_weight1, 'L0_gnn_W_src': _L0_gnn_in['W_src'], 'L0_gnn_b_src': _L0_gnn_in['b_src'], 'L0_gnn_W_tgt': _L0_gnn_in['W_tgt'], 'L0_gnn_b_tgt': _L0_gnn_in['b_tgt'], 'L0_gnn_W_edge': _L0_gnn_in['W_edge'], 'L0_gnn_b_edge': _L0_gnn_in['b_edge'], 'L0_gnn_W1': _L0_gnn_in['W1'], 'L0_gnn_b1': _L0_gnn_in['b1'], 'L0_gnn_W2': _L0_gnn_in['W2'], 'L0_gnn_b2': _L0_gnn_in['b2'], 'L0_gnn_W3': _L0_gnn_in['W3'], 'L0_gnn_b3': _L0_gnn_in['b3'], 'L1_gnn_W_out': _L1_gnn_in['W_out'], 'L1_gnn_b_out': _L1_gnn_in['b_out'], 'L1_gnn_attn_w': _L1_gnn_in['attn_w'], 'L1_gnn_res_W': _L1_gnn_in['res_W'], 'L1_gnn_res_b': _L1_gnn_in['res_b'], 'L2_gnn_W_msg_w': _L2_gnn_in['W_msg_w'], 'L2_gnn_W_msg_b': _L2_gnn_in['W_msg_b'], 'L2_gnn_W_apply_w': _L2_gnn_in['W_apply_w'], 'L2_gnn_W_apply_b': _L2_gnn_in['W_apply_b'], 'L3_gnn_weight': _L3_gnn_in['weight']}

def reference(x, src, dst, edge_attr_32, edge_attr_8, edge_type_16, edge_weight1, L0_gnn_W_src, L0_gnn_b_src, L0_gnn_W_tgt, L0_gnn_b_tgt, L0_gnn_W_edge, L0_gnn_b_edge, L0_gnn_W1, L0_gnn_b1, L0_gnn_W2, L0_gnn_b2, L0_gnn_W3, L0_gnn_b3, L1_gnn_W_out, L1_gnn_b_out, L1_gnn_attn_w, L1_gnn_res_W, L1_gnn_res_b, L2_gnn_W_msg_w, L2_gnn_W_msg_b, L2_gnn_W_apply_w, L2_gnn_W_apply_b, L3_gnn_weight):
    import jax
    import jax.numpy as jnp

    def _L0_gnn_ref(x, edge_index, edge_attr, W_src, b_src, W_tgt, b_tgt, W_edge, b_edge, W1, b1, W2, b2, W3, b3):
        import jax, jax.numpy as jnp
        import numpy as np
        N = 100000
        E = 25000
        IN = 64
        OUT = 64
        ED = 8
        H1 = OUT
        H2 = OUT // 2
        NEG_SLOPE = 0.01
        src, tgt = (edge_index[0], edge_index[1])
        x_source = x @ W_src.T + b_src
        x_target = x @ W_tgt.T + b_tgt
        edge_trans = edge_attr @ W_edge.T + b_edge
        combined = jnp.concatenate([x_source[src], x_target[tgt], edge_trans], axis=1)
        h = jax.nn.leaky_relu(combined @ W1.T + b1, NEG_SLOPE)
        h = jax.nn.leaky_relu(h @ W2.T + b2, NEG_SLOPE)
        e = (h @ W3.T + b3)[:, 0]
        e = jax.nn.relu(e)
        msg = e[:, None] * x_source[src]
        out = jax.ops.segment_sum(msg, tgt, num_segments=x.shape[0])
        return out + x_target

    def _L1_gnn_ref(feature, src, dst, W_out, b_out, attn_w, res_W, res_b):
        import jax, jax.numpy as jnp
        import numpy as np
        N_NODES = 100000
        N_EDGES = 25000
        IN_FEAT = 64
        OUT_FEAT = 64
        n = feature.shape[0]
        z = feature @ W_out + b_out
        d = z.shape[1]
        s_src = z @ attn_w[:d]
        s_dst = z @ attn_w[d:]
        e = jax.nn.gelu(s_src[src] + s_dst[dst], approximate=False)
        m = jax.ops.segment_max(e, dst, num_segments=n)
        m = jnp.where(jnp.isfinite(m), m, 0.0)
        ex = jnp.exp(e - m[dst])
        denom = jax.ops.segment_sum(ex, dst, num_segments=n)
        a = ex / jnp.maximum(denom[dst], 1e-20)
        h = jax.ops.segment_sum(a[:, None] * z[src], dst, num_segments=n)
        h = h + (feature @ res_W + res_b)
        return h

    def _L2_gnn_ref(nfeats, efeats, src, dst, W_msg_w, W_msg_b, W_apply_w, W_apply_b):
        import jax, jax.numpy as jnp
        import numpy as np
        N_NODES = 100000
        N_EDGES = 25000
        NODE_IN = 64
        EDGE_DIM = 32
        NODE_OUT = 64
        n_nodes = nfeats.shape[0]
        m = jnp.concatenate([nfeats[src], efeats], axis=-1) @ W_msg_w + W_msg_b
        s = jax.ops.segment_sum(m, dst, num_segments=n_nodes)
        cnt = jax.ops.segment_sum(jnp.ones((m.shape[0],), m.dtype), dst, num_segments=n_nodes)
        h_neigh = s / jnp.maximum(cnt, 1.0)[:, None]
        h = jnp.concatenate([nfeats, h_neigh], axis=-1) @ W_apply_w + W_apply_b
        return jax.nn.relu(h)

    def _L3_gnn_ref(h, weight, norm, src, dst, rel_type):
        import jax, jax.numpy as jnp
        import numpy as np
        N_NODES = 50000
        N_EDGES = 25000
        REL_NUM = 16
        D_IN = 64
        D_OUT = 64
        n_nodes = h.shape[0]
        transformed = jnp.einsum('nd,rdo->nro', h, weight)
        msg = transformed[src, rel_type] * norm
        agg = jax.ops.segment_sum(msg, dst, num_segments=n_nodes)
        return jax.nn.relu(agg)
    edge_index = jnp.stack([src, dst])
    x = _layernorm(x + _L0_gnn_ref(x, edge_index, edge_attr_8, L0_gnn_W_src, L0_gnn_b_src, L0_gnn_W_tgt, L0_gnn_b_tgt, L0_gnn_W_edge, L0_gnn_b_edge, L0_gnn_W1, L0_gnn_b1, L0_gnn_W2, L0_gnn_b2, L0_gnn_W3, L0_gnn_b3), axis=-1)
    x = _layernorm(x + _L1_gnn_ref(x, src, dst, L1_gnn_W_out, L1_gnn_b_out, L1_gnn_attn_w, L1_gnn_res_W, L1_gnn_res_b), axis=-1)
    x = _layernorm(x + _L2_gnn_ref(x, edge_attr_32, src, dst, L2_gnn_W_msg_w, L2_gnn_W_msg_b, L2_gnn_W_apply_w, L2_gnn_W_apply_b), axis=-1)
    x = _layernorm(x + _L3_gnn_ref(x, L3_gnn_weight, edge_weight1, src, dst, edge_type_16), axis=-1)
    return x

_drawn_inputs = setup_inputs


def setup_inputs(seed=0):
    import zlib

    import numpy as np

    out = dict(_drawn_inputs(seed))
    spreads = {'L0_gnn_b_src': (0.0, 0.8),
     'L0_gnn_b_tgt': (0.0, 0.1),
     'L0_gnn_b_edge': (0.0, 0.8),
     'L0_gnn_b1': (0.0, 0.8),
     'L0_gnn_b2': (0.0, 2.0)}
    factors = {'edge_attr_8': 8.0,
     'L0_gnn_W_src': 8.0,
     'L0_gnn_W_edge': 8.0,
     'L0_gnn_W1': 8.0,
     'L0_gnn_W2': 8.0,
     'L0_gnn_W3': 8.0,
     'L2_gnn_W_msg_b': 2.725}
    for name, (base, spread) in spreads.items():
        noise = np.random.default_rng([zlib.crc32(name.encode()), seed]).standard_normal(out[name].shape)
        drawn = base * np.exp(spread * noise) if base else spread * noise
        out[name] = jnp.asarray(drawn.astype(out[name].dtype))
    for name, factor in factors.items():
        out[name] = (out[name] * factor).astype(out[name].dtype)
    return out
```

```python
from contextlib import ExitStack

import concourse.bass as bass
from concourse import mybir

F32 = mybir.dt.float32
BF16 = mybir.dt.bfloat16
I32 = mybir.dt.int32
ALU = mybir.AluOpType
ACT = mybir.ActivationFunctionType
AX = mybir.AxisListType

N, E, F, P = 100000, 25000, 64, 128
REL = 16
CW = 512
CH = -(-E // (2 * CW))
SLOTS = CH * 2 * CW
TILES = SLOTS // P
TPC = TILES // CH
RP = TILES // 2
NB = 4 * CH
NPAD = NB * 2 * CW
EPS = 1e-5
SLOPE = 0.01
NO_ROW = 1 << 20
NEG = -1.0e30
LANES = 3
assert NPAD >= N and CH % 2 == 1

PIECES = ["eye", "cen", "w_src", "w_tgt", "w_srcT", "w1aT", "w1bT", "w1cT", "w2T", "w3rep",
          "res_wT", "w_outT", "w_tgtI", "attn_rep", "msg1", "app1", "app2", "w_edge", "msg2"]
COLS = ["b_src", "b_tgt", "b_edge", "b1", "b2", "b3", "res_b", "b_out", "msg_b", "app_b",
        "attn1_0", "attn1_1", "attn2_0", "attn2_1"]


ROWS = 16 * TPC
LN = {f"{what}{who}": 1 for what in ("sq", "ss", "sd", "rs") for who in "DS"}
BOTH = {"scan": 2, "carry": 2, "msg": 1, "cD": 1, "cS": 1, "D": 1, "S": 1, **LN}
STAGES = ["p0", "l0", "l1a", "l1b", "l2", "l3"]
PER_CHUNK = {
    "p0": {"rows0": ROWS, "rows1": ROWS, "idx": 1, "T": 1},
    "l0": {"rows0": ROWS, "rows1": ROWS, "idx": 1, "T": 1, "stream0": 48, "stream1": 48, "xsT": 1,
           "T2": 1, "DT": 1, **BOTH},
    "l1a": {"rows0": ROWS, "rows1": ROWS, "idx": 1, "T": 1, "stream0": 16, "stream1": 16, "copy": 1},
    "l1b": {"stream0": 64, "stream1": 64, "T2": 1, "DT": 1, **BOTH},
    "l2": {"rows0": ROWS, "rows1": ROWS, "idx": 1, "T": 1, "stream0": 64, "stream1": 64, "copy": 1,
           "xsT": 1, "rD": 1, **BOTH},
    "l3": {"rows0": ROWS, "rows1": ROWS, "idx": 1, "T": 2, "stream0": 48, "stream1": 48, "copy": 1,
           "rD": 1, "scan": 2, "carry": 2, "cD": 1, "D": 1, "sqD": 1, "ssD": 1, "sdD": 1, "rsD": 1},
}


def run_chunks(eng, body):
    for c in range(3):
        body(c, c % 2, c // 2)
    with eng.Fori(1, CH // 2) as i:
        body(i * 2 + 1, 1, i)
        body(i * 2 + 2, 0, i + 1)


def run_skewed(eng, front, back, mixed):
    front(0, 0, 0)
    mixed((1, 1, 0), (0, 0, 0))
    mixed((2, 0, 1), (1, 1, 0))
    with eng.Fori(1, CH // 2) as i:
        mixed((i * 2 + 1, 1, i), (i * 2, 0, i))
        mixed((i * 2 + 2, 0, i + 1), (i * 2 + 1, 1, i))
    back(CH - 1, 0, CH // 2)


def build(nc, x, xmap_in, xT, dst_col, nxt_col, src_col, row_col, dst_run, attr8T, attr32T,
          rel_flat, weight_col, wpack, cpack, relpack, out):
    with ExitStack() as ctx:
        def sb(name, shape, dt=F32):
            return ctx.enter_context(nc.sbuf_tensor(name, shape, dt))

        sems = {}

        def signal_of(name):
            stage, _, what = name.partition("_")
            if stage not in STAGES or what not in PER_CHUNK[stage]:
                return name, 0
            chunks = {"0": CH // 2 + 1, "1": CH // 2}.get(what[-1], CH)
            return what, sum(PER_CHUNK[s].get(what, 0) * chunks for s in STAGES[:STAGES.index(stage)])

        def sem(name):
            name = signal_of(name)[0]
            if name not in sems:
                sems[name] = ctx.enter_context(nc.semaphore(name))
            return sems[name]

        def upto(name, value):
            first = signal_of(name)[1]
            return max(value, 0) + first if isinstance(value, int) else value + first

        def some(name, value):
            at = upto(name, value)
            return not isinstance(at, int) or at > 0

        xmap = nc.dram_tensor("xmap", (N, F + 1), F32, kind="Internal").ap()
        dtab = [nc.dram_tensor(f"dtab{l}", (SLOTS, F), F32, kind="Internal").ap() for l in (1, 2, 3)]
        keep_flat = nc.dram_tensor("keep_flat", (SLOTS,), F32, kind="Internal").ap()
        inv_flat = nc.dram_tensor("inv_flat", (SLOTS,), F32, kind="Internal").ap()
        attn_flat = nc.dram_tensor("attn_flat", (SLOTS,), F32, kind="Internal").ap()
        xmap_cells = xmap.rearrange("n (f o) -> (n f) o", o=1)

        S = sb("S", [P, CH * CW])
        D = sb("D", [P, CH * CW])
        XR = sb("XR", [P, 2, TPC, F])
        idx_st = sb("idx_st", [P, 2, TPC], I32)
        row_st = sb("row_st", [P, 2, TPC])
        sidx_st = sb("sidx_st", [P, 2, TPC], I32)
        dstc = sb("dstc", [P, TILES], I32)
        srcc = sb("srcc", [P, TILES], I32)
        nxtc = sb("nxtc", [P, TILES], I32)
        rowc = sb("rowc", [P, TILES])
        qcol = sb("qcol", [P, TILES], I32)
        outc = sb("outc", [P, TILES], I32)
        cellc = sb("cellc", [P, TILES], I32)
        wcol = sb("wcol", [P, TILES])
        sc = sb("sc", [P, 2, TILES])
        stream = sb("stream", [P, 2, 2, CW])
        attr = sb("attr", [16, 2, CW])
        w = sb("w", [P, len(PIECES), P])
        cols = sb("cols", [P, len(COLS)])
        relw = sb("relw", [P, REL // 2, F])
        relid = sb("relid", [P, REL // 2])
        folded = sb("folded", [P, 5, P])
        edge1 = sb("edge1", [16, P])
        attn_w = sb("attn_w", [P, 4])
        fcol = sb("fcol", [P, 3])
        ones_b = sb("ones_b", [P, P], BF16)
        one = sb("one", [1, 1])
        epsc = sb("epsc", [P, 2])
        brow = sb("brow", [P, 3, CW], BF16)
        bres = sb("bres", [1, 2, P])
        AB = sb("AB", [P, LANES, 5, CW])
        dT = sb("dT", [P, 2, CW])
        EB = sb("EB", [P, 11, CW])
        small = sb("small", [P, 2, 3, 8])
        asmall = sb("asmall", [P, LANES, 3, 8])
        token = sb("token", [1, 3])
        carry = sb("carry", [P, 1])
        runs = sb("runs", [RP, 4, 2, P])
        rowbuf = sb("rowbuf", [1, 4, TILES + 2])
        ends = sb("ends", [RP, 4, 2])

        bank = [ctx.enter_context(nc.psum_tensor(f"bank{i}", [P, CW], F32)) for i in range(8)]

        def W(name, k=P, m=P):
            return w[0:k, PIECES.index(name), 0:m]

        def col(name, m=P):
            return cols[0:m, COLS.index(name):COLS.index(name) + 1]

        A1, B1, M0, M1, WOC = (folded[:, i, :] for i in range(5))
        eye = W("eye")
        cen = W("cen")

        def rows64(t):
            return t.rearrange("p (s f) -> p s f", f=F)

        def bcast8(t):
            return t.rearrange("p (s o) -> p s o", o=1).broadcast_to([P, 8, F])

        def cs(c):
            return bass.ds(c * CW, CW)

        def tc(c):
            return bass.ds(c * TPC, TPC)

        def half_stream(flat, c):
            v = flat[bass.ds(c * 2 * CW, 2 * CW)].rearrange("(h o n) -> h o n", h=2, o=1)
            return v.broadcast_to([2, F, CW])

        node_in, node_sq, node_x, node_xT, node_out = ([AB[:, u, i, :] for u in range(LANES)] for i in range(5))

        xsT, z1, h1 = [EB[:, i, :] for i in (0, 1)], EB[:, 2, :], EB[:, 3, :]
        h2, eg, msg = EB[:, 4, :], EB[:, 4, :], EB[:, 5, :]
        agg = EB[:, 6, :]
        sqD, sqS = EB[:, 7, :], EB[:, 8, :]
        dn = [EB[:, 9, :], EB[:, 10, :]]
        stream2 = [AB[:, 2, 0, :], AB[:, 2, 1, :]]
        rD, rS, cadd = AB[:, 2, 2, :], AB[:, 2, 3, :], AB[:, 2, 4, :]
        xw2 = AB[:, 2, 3:5, :].rearrange("p a n -> p (a n)")
        XM = AB[:, 2, 0:3, :].rearrange("p a n -> p (a n)")[:, 0:2 * TPC * (F + 1)].rearrange(
            "p (b s f) -> p b s f", b=2, s=TPC)

        def rt(i):
            return EB[0:RP, i, 0:2 * P].rearrange("p (g n) -> p g n", g=2)

        block = ctx.enter_context(nc.Block())

        @block.sync
        def _(sp):
            sp.dma_start(dstc[:, :], dst_col).then_inc(sem("dstc_in"), 16)
            sp.dma_start(xmap[:, :].rearrange("(a n) f -> a (n f)", a=16),
                         xmap_in[:, :].rearrange("(a n) f -> a (n f)", a=16)).then_inc(sem("xmap_init"), 16)
            sp.dma_start(w[:, :, :], wpack.rearrange("p (n m) -> p n m", m=P)).then_inc(sem("weights_in"), 16)
            sp.dma_start(cols[:, :], cpack).then_inc(sem("weights_in"), 16)
            sp.dma_start(relw[:, :, :], relpack[:, 0:REL // 2 * F].rearrange("p (k m) -> p k m", m=F)
                         ).then_inc(sem("weights_in"), 16)
            sp.dma_start(relid[:, :], relpack[:, REL // 2 * F:]).then_inc(sem("weights_in"), 16)
            sp.dma_start(nxtc[:, :], nxt_col).then_inc(sem("index_in"), 16)
            sp.dma_start(srcc[:, :], src_col).then_inc(sem("index_in"), 16)
            sp.dma_start(rowc[:, :], row_col).then_inc(sem("index_in"), 16)
            sp.dma_start(wcol[:, :], weight_col).then_inc(sem("index_in"), 16)
            for i in range(3):
                sp.dma_start(rt(i).bitcast(I32),
                             dst_run[i:i + SLOTS].rearrange("(g p n) -> p g n", g=2, n=P)
                             ).then_inc(sem("runs_in"), 16)

            def node_load(blk, u, n):
                if some(f"a{u}_c0", n):
                    sp.wait_ge(sem(f"a{u}_c0"), n)
                sp.dma_start(node_in[u], xT[:, cs(blk)]).then_inc(sem(f"a{u}_in"), 16)

            def node_store(blk, u, n):
                sp.wait_ge(sem(f"a{u}_o"), n + 1)
                sp.dma_start(out[bass.ds(blk * 1024, 1024), :].rearrange("(p s) f -> p (s f)", p=P),
                             node_out[u]).then_inc(sem(f"a{u}_stored"), 16)

            for u in range(LANES):
                node_load(u, u, 0)
            sp.wait_ge(sem("keep_run"), 1)
            sp.dma_start(keep_flat.rearrange("(g p n) -> p g n", g=2, n=P), runs[:, 0, :, :]
                         ).then_inc(sem("flat_out"), 16)
            sp.wait_ge(sem("inv_run"), 1)
            sp.dma_start(inv_flat.rearrange("(g p n) -> p g n", g=2, n=P), rt(3)
                         ).then_inc(sem("flat_out"), 16)

            with sp.Fori(0, CH - 1) as i:
                for u in range(LANES):
                    node_load(i * LANES + (LANES + u), u, i + 1)
                for u in range(LANES):
                    node_store(i * LANES + u, u, i)
            for u in range(2):
                node_load(LANES * CH + u, u, CH)
            for u in range(LANES):
                node_store((CH - 1) * LANES + u, u, CH - 1)

            sp.wait_ge(sem("flat_out"), 32)
            sp.wait_ge(sem("p0_D"), upto("p0_D", CH))

            def l0(c, b, k):
                if some("l0_cD", c - 1):
                    sp.wait_ge(sem("l0_cD"), upto("l0_cD", c - 1))
                sp.dma_start(dT[:, b, :], D[:, cs(c)]).then_inc(sem(f"l0_stream{b}"), 16)
                sp.dma_start(attr[:, b, :], attr8T[:, cs(c)]).then_inc(sem(f"l0_stream{b}"), 16)
                sp.dma_start(stream[:, 0, b, :], half_stream(keep_flat, c)).then_inc(sem(f"l0_stream{b}"), 16)
            run_chunks(sp, l0)

            base = LANES * CH

            def l1a_D(c, b):
                if some("l1a_s", c - 1):
                    sp.wait_ge(sem("l1a_s"), upto("l1a_s", c - 1))
                sp.dma_start(dT[:, b, :], D[:, cs(c)]).then_inc(sem(f"l1a_stream{b}"), 16)

            def l1a_io(c, b, k, ahead=2):
                if ahead:
                    l1a_D(c + 1, 1 - b)
                if ahead == 2:
                    node_load(c + (base + 2), b, k + (CH + 1))
                sp.wait_ge(sem("ring_clear"), 1)
                sp.wait_ge(sem("l1a_ST"), upto("l1a_ST", c + 1))
                sp.dma_start(S[:, cs(c)], xsT[b]).then_inc(sem(f"l1a_stored{b}"), 16)
                node_store(c + base, b, k + CH)

            sp.wait_ge(sem("l0_DT"), upto("l0_DT", CH))
            l1a_D(0, 0)
            l1a_io(0, 0, 0)
            l1a_io(1, 1, 0)
            with sp.Fori(1, (CH - 3) // 2) as i:
                l1a_io(i * 2, 0, i)
                l1a_io(i * 2 + 1, 1, i)
            l1a_io(CH - 3, 0, (CH - 3) // 2)
            l1a_io(CH - 2, 1, (CH - 3) // 2, ahead=1)
            l1a_io(CH - 1, 0, (CH - 1) // 2, ahead=0)
            sp.wait_ge(sem("l1a_stored0"), upto("l1a_stored0", 16 * (CH // 2 + 1)))
            sp.wait_ge(sem("l1a_stored1"), upto("l1a_stored1", 16 * (CH // 2)))

            sp.wait_ge(sem("attn_run"), 1)
            sp.dma_start(attn_flat.rearrange("(g p n) -> p g n", g=2, n=P), rt(3)
                         ).then_inc(sem("attn_out"), 16)
            sp.wait_ge(sem("attn_out"), 16)

            def l1b(c, b, k):
                if some("l1b_cD", c - 1):
                    sp.wait_ge(sem("l1b_cD"), upto("l1b_cD", c - 1))
                sp.dma_start(xsT[b], S[:, cs(c)]).then_inc(sem(f"l1b_stream{b}"), 16)
                sp.dma_start(dT[:, b, :], D[:, cs(c)]).then_inc(sem(f"l1b_stream{b}"), 16)
                sp.dma_start(stream[:, 1, b, :], half_stream(attn_flat, c)).then_inc(sem(f"l1b_stream{b}"), 16)
                sp.dma_start(stream[:, 0, b, :], half_stream(keep_flat, c)).then_inc(sem(f"l1b_stream{b}"), 16)
            run_chunks(sp, l1b)

            sp.wait_ge(sem("l1b_DT"), upto("l1b_DT", CH))

            def l2(c, b, k):
                if some("l2_cD", c - 1):
                    sp.wait_ge(sem("l2_cD"), upto("l2_cD", c - 1))
                sp.dma_start(stream2[b][0:F, :], attr32T[:, cs(c)]).then_inc(sem(f"l2_stream{b}"), 16)
                sp.dma_start(dT[:, b, :], D[:, cs(c)]).then_inc(sem(f"l2_stream{b}"), 16)
                sp.dma_start(stream[:, 1, b, :], half_stream(inv_flat, c)).then_inc(sem(f"l2_stream{b}"), 16)
                sp.dma_start(stream[:, 0, b, :], half_stream(keep_flat, c)).then_inc(sem(f"l2_stream{b}"), 16)
            run_chunks(sp, l2)

            def rel_half(c, h):
                v = rel_flat[bass.ds(c * 2 * CW + h * CW, CW)].rearrange("(o n) -> o n", o=1)
                return v.broadcast_to([P, CW])

            def l3(c, b, k):
                if some("l3_cD", c - 1):
                    sp.wait_ge(sem("l3_cD"), upto("l3_cD", c - 1))
                sp.dma_start(stream[:, 1, b, :].bitcast(I32), rel_half(c, 0)).then_inc(sem(f"l3_stream{b}"), 16)
                sp.dma_start(stream2[b].bitcast(I32), rel_half(c, 1)).then_inc(sem(f"l3_stream{b}"), 16)
                sp.dma_start(stream[:, 0, b, :], half_stream(keep_flat, c)).then_inc(sem(f"l3_stream{b}"), 16)
            run_chunks(sp, l3)
            for u in range(LANES):
                sp.wait_ge(sem(f"a{u}_stored"), 16 * (CH + (13 if u == 0 else 12 if u == 1 else 0)))
            sp.wait_ge(sem("final_st0"), 16 * TPC * (CH // 2 + 1))
            sp.wait_ge(sem("final_st1"), 16 * TPC * (CH // 2))

        @block.gpsimd
        def _(pool):
            last_node, last_row, last_cell = (pool.to_reg(v) for v in (N - 1, SLOTS - 1, N * (F + 1) - 1))
            pool.memset(token[:, :], 0.0).then_inc(sem("token"), 1)
            pool.wait_ge(sem("token"), 1)
            pool.memset(XR[:, :, :, :], 0.0).then_inc(sem("ring_clear"), 1)
            pool.memset(ones_b[:, :], 1.0).then_inc(sem("consts"), 1)
            pool.memset(one[:, :], 1.0).then_inc(sem("consts"), 1)
            pool.memset(epsc[:, 0:1], EPS).then_inc(sem("consts"), 1)
            pool.memset(epsc[:, 1:2], EPS * EPS).then_inc(sem("consts"), 1)
            pool.memset(brow[:, :, :], 0.0).then_inc(sem("consts"), 1)
            pool.memset(carry[:, :], 0.0).then_inc(sem("consts"), 1)

            def load_indices(stage, index, c, b, k):
                if some(f"{stage}_rows{b}", k * ROWS):
                    pool.wait_ge(sem(f"{stage}_rows{b}"), upto(f"{stage}_rows{b}", k * ROWS))
                pool.tensor_copy(idx_st[:, b, :], index[:, tc(c)]).then_inc(sem(f"{stage}_idx"), 1)
                pool.wait_ge(sem(f"{stage}_idx"), upto(f"{stage}_idx", c + 1))

            def gather(stage, table, bound, ring, b):
                for s in range(TPC):
                    pool.indirect_dma_start(
                        ring[:, b, s, :], None, table,
                        bass.IndirectOffsetOnAxis(ap=idx_st[:, b, s:s + 1], axis=0),
                        bounds_check=bound, oob_is_err=False).then_inc(sem(f"{stage}_rows{b}"), 16)

            def carry_waits():
                pool.tensor_tensor(token[:, 0:1], token[:, 1:2], token[:, 2:3], ALU.add)

            pool.wait_ge(sem("dstc_in"), 16)
            pool.wait_ge(sem("ring_clear"), 1)

            def p0(c, b, k):
                load_indices("p0", dstc, c, b, k)
                if some("p0_T", c - 1):
                    pool.wait_ge(sem("p0_T"), upto("p0_T", c - 1))
                carry_waits()
                gather("p0", x, last_node, XR, b)
            run_chunks(pool, p0)

            pool.wait_ge(sem("xmap_init"), 16)
            pool.wait_ge(sem("cells"), 1)
            pool.wait_ge(sem("index_in"), 64)

            def map_scatter(c, b, k):
                if some(f"map_st{b}", k * (16 * TPC)):
                    pool.wait_ge(sem(f"map_st{b}"), k * (16 * TPC))
                pool.tensor_copy(sidx_st[:, b, :], cellc[:, tc(c)]).then_inc(sem("map_idx"), 1)
                pool.tensor_copy(row_st[:, b, :], rowc[:, tc(c)]).then_inc(sem("map_idx"), 1)
                pool.wait_ge(sem("map_idx"), (c + 1) * 2)
                carry_waits()
                for s in range(TPC):
                    pool.indirect_dma_start(
                        xmap_cells, bass.IndirectOffsetOnAxis(ap=sidx_st[:, b, s:s + 1], axis=0),
                        row_st[:, b, s:s + 1], None,
                        bounds_check=last_cell, oob_is_err=False).then_inc(sem(f"map_st{b}"), 16)
            run_chunks(pool, map_scatter)
            pool.wait_ge(sem("map_st0"), 16 * TPC * (CH // 2 + 1))
            pool.wait_ge(sem("map_st1"), 16 * TPC * (CH // 2))

            pool.wait_ge(sem("p0_T"), upto("p0_T", CH))
            pool.wait_ge(sem("p0_rows0"), upto("p0_rows0", 16 * TPC * (CH // 2 + 1)))
            pool.wait_ge(sem("p0_rows1"), upto("p0_rows1", 16 * TPC * (CH // 2)))

            for u in range(LANES):
                pool.wait_ge(sem(f"a{u}_stored"), 16 * CH)


            def l0(c, b, k):
                load_indices("l0", srcc, c, b, k)
                if some("l0_dense", c - 1):
                    pool.wait_ge(sem("l0_dense"), upto("l0_dense", c - 1))
                if some("l0_q", c - 1):
                    pool.wait_ge(sem("l0_q"), upto("l0_q", c - 1))
                carry_waits()
                gather("l0", xmap, last_node, XM, b)
            run_chunks(pool, l0)

            def layer_gather(stage, l, prev):
                pool.wait_ge(sem("l0_q"), upto("l0_q", CH))
                pool.wait_ge(sem(f"{prev}_rows0"), upto(f"{prev}_rows0", 16 * TPC * (CH // 2 + 1)))
                pool.wait_ge(sem(f"{prev}_rows1"), upto(f"{prev}_rows1", 16 * TPC * (CH // 2)))
                pool.wait_ge(sem(f"tab{l}_st0"), 16 * (CH // 2 + 1))
                pool.wait_ge(sem(f"tab{l}_st1"), 16 * (CH // 2))

            layer_gather("l1a", 1, "l0")

            def l1a(c, b, k):
                load_indices("l1a", qcol, c, b, k)
                pool.wait_ge(sem("l1a_copy"), upto("l1a_copy", c + 1))
                carry_waits()
                gather("l1a", dtab[0], last_row, XR, b)
            run_chunks(pool, l1a)
            layer_gather("l2", 2, "l1a")

            def l2(c, b, k):
                load_indices("l2", qcol, c, b, k)
                pool.wait_ge(sem("l2_copy"), upto("l2_copy", c + 1))
                carry_waits()
                gather("l2", dtab[1], last_row, XR, b)
            run_chunks(pool, l2)
            layer_gather("l3", 3, "l2")
            pool.wait_ge(sem("a0_stored"), 16 * (CH + 13))
            pool.wait_ge(sem("a1_stored"), 16 * (CH + 12))
            pool.wait_ge(sem("a2_stored"), 16 * CH)
            pool.wait_ge(sem("map_st0"), 16 * TPC * (CH // 2 + 1))

            def l3_front(c, b, k):
                load_indices("l3", qcol, c, b, k)
                pool.wait_ge(sem("l3_copy"), upto("l3_copy", c + 1))
                carry_waits()
                gather("l3", dtab[2], last_row, XR, b)

            def final_scatter(c, b, k):
                if some(f"final_st{b}", k * (16 * TPC)):
                    pool.wait_ge(sem(f"final_st{b}"), k * (16 * TPC))
                pool.tensor_copy(sidx_st[:, b, :], outc[:, tc(c)]).then_inc(sem("final_idx"), 1)
                pool.wait_ge(sem("final_idx"), c + 1)
                pool.wait_ge(sem("l3_D"), upto("l3_D", c + 1))
                carry_waits()
                for s in range(TPC):
                    pool.indirect_dma_start(
                        out[:, :], bass.IndirectOffsetOnAxis(ap=sidx_st[:, b, s:s + 1], axis=0),
                        dn[b][:, s * F:(s + 1) * F], None,
                        bounds_check=last_node, oob_is_err=False).then_inc(sem(f"final_st{b}"), 16)

            def l3_mixed(f, g):
                l3_front(*f)
                final_scatter(*g)
            run_skewed(pool, l3_front, final_scatter, l3_mixed)

        @block.tensor
        def _(pe):
            pe.wait_ge(sem("weights_in"), 64)
            pe.wait_ge(sem("consts"), 6)
            pe.wait_ge(sem("eye_plus"), 2)
            fold = bank[6]
            pe.matmul(fold[:, 0:128], W("w_src"), W("w1aT"), start=True, stop=True)
            pe.matmul(fold[:, 128:256], W("w_tgt"), W("w1bT"), start=True, stop=True)
            pe.matmul(fold[:, 256:384], W("w_tgtI"), cen, start=True, stop=True)
            pe.matmul(fold[:, 384:512], W("res_wT"), cen, start=True, stop=True).then_inc(sem("fold"), 1)
            f2 = bank[7]
            pe.matmul(f2[:, 0:128], W("w_outT"), cen, start=True, stop=True)
            pe.matmul(f2[0:16, 128:256], W("w_edge", m=16), W("w1cT"), start=True, stop=True)
            pe.matmul(f2[:, 256:260], W("w_outT"), cols[:, COLS.index("attn1_0"):COLS.index("attn1_0") + 4],
                      start=True, stop=True)
            pe.matmul(f2[:, 260:261], W("w1aT"), col("b_src"), start=True, stop=False)
            pe.matmul(f2[:, 260:261], W("w1bT"), col("b_tgt"), start=False, stop=False)
            pe.matmul(f2[:, 260:261], W("w1cT"), col("b_edge"), start=False, stop=True)
            pe.matmul(f2[:, 261:262], W("app2"), col("msg_b"), start=True, stop=True)
            pe.matmul(f2[:, 262:263], W("attn_rep"), col("b_out"), start=True, stop=True).then_inc(sem("fold"), 1)
            f3 = bank[5]
            pe.matmul(f3[:, 0:128], col("b_tgt").broadcast_to([P, P]), cen, start=True, stop=True)
            pe.matmul(f3[:, 128:256], col("res_b").broadcast_to([P, P]), cen, start=True, stop=True)
            pe.matmul(f3[:, 256:384], col("b_out").broadcast_to([P, P]), cen, start=True, stop=True
                      ).then_inc(sem("fold"), 1)

            tls = [0]

            def two_level(loc, last, off, static=False):
                n = tls[0]
                tls[0] += 1
                pe.wait_ge(sem("tl_ends"), n + 1)
                row = bank[7][0:1, 0:TILES]
                for g in range(2):
                    mm = pe.matmul(bank[7][0:1, g * RP:(g + 1) * RP], loc[:, g, last:last + 1],
                                   eye[0:RP, 0:RP], start=True, stop=True)
                mm.then_inc(sem("tl_row"), 1)
                pe.wait_ge(sem("tl_carry"), n + 1)
                for g in range(2):
                    mm = pe.matmul(bank[7][0:RP, 256 + g:257 + g],
                                   rowbuf[0:1, 3, off + g * RP:off + (g + 1) * RP], one[:, :],
                                   start=True, stop=True)
                mm.then_inc(sem("tl_cin"), 1)

            def static_rows():
                pe.wait_ge(sem("ends_static"), 3)
                pe.wait_ge(sem("fold_used"), 7)
                for q in range(3):
                    if q:
                        if some("static_row", q):
                            pe.wait_ge(sem("static_row"), q)
                    for g in range(2):
                        mm = pe.matmul(bank[7][0:1, g * RP:(g + 1) * RP], ends[:, q, g:g + 1],
                                       eye[0:RP, 0:RP], start=True, stop=True)
                    mm.then_inc(sem("static_T"), 1)
                pe.wait_ge(sem("static_row"), 3)

            static_rows()
            two_level(rt(0), P - 1, 0)
            two_level(rt(2), 0, 2)

            def node_product(u, src, weight, bias, done):
                X = bank[2 * u]
                if bias is not None:
                    pe.matmul(X[:, :], ones_b[:, :], brow[:, bias, :], start=True, stop=True)
                for j in range(4):
                    mm = pe.matmul(X[:, j * P:(j + 1) * P], src[:, j * P:(j + 1) * P], weight,
                                   start=bias is None, stop=True, skip_group_check=True)
                mm.then_inc(sem(done), 1)

            def node_c0(u, n):
                pe.wait_ge(sem(f"a{u}_in"), n * 16 + 16)
                if some(f"a{u}_c2s", n):
                    pe.wait_ge(sem(f"a{u}_c2s"), n)
                node_product(u, node_in[u], M0, 0, f"a{u}_c0")

            def node_turn(u, n, m):
                pe.wait_ge(sem(f"a{u}_xn"), n * 2 + m)
                for j in range(4):
                    mm = pe.transpose(bank[2 * u + 1][:, j * P:(j + 1) * P], node_x[u][:, j * P:(j + 1) * P], eye)
                mm.then_inc(sem(f"a{u}_T"), 1)

            def node_c1(u, n):
                pe.wait_ge(sem(f"a{u}_xt"), n * 2 + 1)
                node_product(u, node_xT[u], M1, 1, f"a{u}_c1")

            def node_y(u, n):
                pe.wait_ge(sem(f"a{u}_xt"), n * 2 + 2)
                pe.matmul(bank[2 * u + 1][:, :], W("app1"), node_xT[u], start=True, stop=True
                          ).then_inc(sem(f"a{u}_y"), 1)

            def node_c2(u, n):
                pe.wait_ge(sem(f"a{u}_r"), n + 1)
                node_product(u, node_sq[u], cen, None, f"a{u}_c2")

            pe.wait_ge(sem("fold_used"), 7)
            pe.wait_ge(sem("brow"), 3)

            def transpose_rows(stage, rows, dest):
                for j in range(4):
                    mm = pe.transpose(dest[:, j * P:(j + 1) * P],
                                      rows[:, 2 * j:2 * j + 2, :].rearrange("p s f -> p (s f)"), eye)
                mm.then_inc(sem(f"{stage}_T"), 1)

            def stage1(c, b, k):
                for u in range(LANES):
                    node_c0(u, c)
                for u in range(LANES):
                    node_turn(u, c, 1)
                for u in range(LANES):
                    node_c1(u, c)
                for u in range(LANES):
                    node_turn(u, c, 2)
                for u in range(LANES):
                    node_y(u, c)
                for u in range(LANES):
                    node_c2(u, c)
                pe.wait_ge(sem(f"p0_rows{b}"), upto(f"p0_rows{b}", (k + 1) * ROWS))
                if some("p0_D", c):
                    pe.wait_ge(sem("p0_D"), upto("p0_D", c))
                transpose_rows("p0", XR[:, b, :, :], bank[6])
            run_chunks(pe, stage1)

            def tile_product(dest, terms, bias, done):
                if bias is not None:
                    pe.matmul(dest[:, :], ones_b[:, :], brow[:, bias, :], start=True, stop=True)
                for j in range(4):
                    for t, (src, weight) in enumerate(terms):
                        mm = pe.matmul(dest[:, j * P:(j + 1) * P], src(j), weight,
                                       start=bias is None and t == 0, stop=True,
                                       skip_group_check=True)
                mm.then_inc(sem(done), 1)

            def fixed(t):
                return lambda j: t[:, j * P:(j + 1) * P]

            def transpose_dn(stage, c, b):
                pe.wait_ge(sem(f"{stage}_D"), upto(f"{stage}_D", c + 1))
                if some(f"{stage}_DT", c):
                    pe.wait_ge(sem(f"{stage}_DT"), upto(f"{stage}_DT", c))
                for j in range(4):
                    mm = pe.transpose(bank[2][:, j * P:(j + 1) * P], dn[b][:, j * P:(j + 1) * P], eye)
                mm.then_inc(sem(f"{stage}_T2"), 1)

            pe.wait_ge(sem("p0_D"), upto("p0_D", CH))
            for u in range(LANES):
                pe.wait_ge(sem(f"a{u}_c2s"), CH)

            def l0_front(c, b, k):
                pe.wait_ge(sem("l0_dense"), upto("l0_dense", c + 1))
                if some("l0_xsT", c):
                    pe.wait_ge(sem("l0_xsT"), upto("l0_xsT", c))
                transpose_rows("l0", XR[:, b, :, :], bank[4])
                pe.wait_ge(sem("l0_xsT"), upto("l0_xsT", c + 1))
                pe.wait_ge(sem(f"l0_stream{b}"), upto(f"l0_stream{b}", (k + 1) * 48))
                if some("l0_eg", c):
                    pe.wait_ge(sem("l0_eg"), upto("l0_eg", c))
                pe.matmul(bank[5][:, :], B1, dT[:, b, :], start=True, stop=False)
                pe.matmul(bank[5][:, :], edge1[:, :], attr[:, b, :], start=False, stop=False)
                pe.matmul(bank[5][:, :], A1, xsT[b], start=False, stop=True).then_inc(sem("l0_z1"), 1)
                if some("l0_msg", c):
                    pe.wait_ge(sem("l0_msg"), upto("l0_msg", c))
                pe.matmul(bank[6][:, :], W("w_srcT"), xsT[b], start=True, stop=True).then_inc(sem("l0_xs"), 1)
                if some("l0_S", c):
                    pe.wait_ge(sem("l0_S"), upto("l0_S", c))
                tile_product(bank[1], [(fixed(xsT[b]), M0)], 0, "l0_cS")
                pe.wait_ge(sem("l0_h1"), upto("l0_h1", c + 1))
                pe.wait_ge(sem("l0_z1b"), upto("l0_z1b", c + 1))
                pe.matmul(bank[5][0:64, :], W("w2T", m=64), h1, start=True, stop=True).then_inc(sem("l0_z2"), 1)
                pe.wait_ge(sem("l0_h2"), upto("l0_h2", c + 1))
                pe.matmul(bank[5][:, :], W("w3rep", k=64), h2[0:64, :], start=True, stop=True
                          ).then_inc(sem("l0_e"), 1)

            def l0_back(c, b, k):
                pe.wait_ge(sem("l0_scan"), upto("l0_scan", c * 2 + 2))
                if some("l0_D", c):
                    pe.wait_ge(sem("l0_D"), upto("l0_D", c))
                tile_product(bank[0], [(fixed(dT[:, b, :]), M0), (fixed(agg), cen)], 0, "l0_cD")
                transpose_dn("l0", c, b)

            def l0(c, b, k):
                l0_front(c, b, k)
                l0_back(c, b, k)
            run_chunks(pe, l0)

            def l1a(c, b, k):
                n = k + CH
                node_c0(b, n)
                pe.wait_ge(sem(f"l1a_rows{b}"), upto(f"l1a_rows{b}", (k + 1) * ROWS))
                if some("l1a_ST", c):
                    pe.wait_ge(sem("l1a_ST"), upto("l1a_ST", c))
                transpose_rows("l1a", XR[:, b, :, :], bank[6])
                node_turn(b, n, 1)
                pe.wait_ge(sem("l1a_ST"), upto("l1a_ST", c + 1))
                if some("l1a_sc", c):
                    pe.wait_ge(sem("l1a_sc"), upto("l1a_sc", c))
                pe.wait_ge(sem(f"l1a_stream{b}"), upto(f"l1a_stream{b}", (k + 1) * 16))
                for j in range(4):
                    pe.matmul(bank[7][:, 2 * j:2 * j + 2], xsT[b][:, j * P:(j + 1) * P], attn_w[:, 0:2],
                              start=True, stop=True)
                for j in range(4):
                    mm = pe.matmul(bank[7][:, 8 + 2 * j:10 + 2 * j], dT[:, b, j * P:(j + 1) * P],
                                   attn_w[:, 2:4], start=True, stop=True)
                mm.then_inc(sem("l1a_s"), 1)
                node_c1(b, n)
                node_turn(b, n, 2)
                node_y(b, n)
                node_c2(b, n)
            pe.wait_ge(sem("l0_DT"), upto("l0_DT", CH))
            run_chunks(pe, l1a)

            pe.wait_ge(sem("l1_perm"), 2)
            pe.wait_ge(sem("l1a_ST"), upto("l1a_ST", CH))
            for q in range(2):
                for g in range(2):
                    mm = pe.transpose(bank[6][0:RP, (2 * q + g) * P:(2 * q + g + 1) * P],
                                      EB[:, 4 + q, g * RP:(g + 1) * RP], eye)
            mm.then_inc(sem("l1_run"), 1)
            two_level(rt(2), 0, 2)
            two_level(rt(0), P - 1, 0)
            two_level(rt(2), 0, 2)
            two_level(rt(0), P - 1, 0)
            two_level(rt(2), 0, 2)

            pe.wait_ge(sem("a0_c2s"), CH + 13)
            pe.wait_ge(sem("a1_c2s"), CH + 12)

            def l1b(c, b, k):
                if some("l1b_S", c):
                    pe.wait_ge(sem("l1b_S"), upto("l1b_S", c))
                pe.wait_ge(sem(f"l1b_stream{b}"), upto(f"l1b_stream{b}", (k + 1) * 64))
                tile_product(bank[1], [(fixed(xsT[b]), M1)], 1, "l1b_cS")
                pe.wait_ge(sem("l1b_scan"), upto("l1b_scan", c * 2 + 2))
                if some("l1b_D", c):
                    pe.wait_ge(sem("l1b_D"), upto("l1b_D", c))
                tile_product(bank[0], [(fixed(dT[:, b, :]), M1), (fixed(agg), WOC)], 2, "l1b_cD")
                transpose_dn("l1b", c, b)
            run_chunks(pe, l1b)
            pe.wait_ge(sem("l1b_DT"), upto("l1b_DT", CH))

            def l2(c, b, k):
                pe.wait_ge(sem(f"l2_rows{b}"), upto(f"l2_rows{b}", (k + 1) * ROWS))
                if some("l2_xsT", c):
                    pe.wait_ge(sem("l2_xsT"), upto("l2_xsT", c))
                transpose_rows("l2", XR[:, b, :, :], bank[4])
                pe.wait_ge(sem("l2_xsT"), upto("l2_xsT", c + 1))
                pe.wait_ge(sem(f"l2_stream{b}"), upto(f"l2_stream{b}", (k + 1) * 64))
                if some("l2_msg", c):
                    pe.wait_ge(sem("l2_msg"), upto("l2_msg", c))
                pe.matmul(bank[5][:, :], W("msg1"), xsT[b], start=True, stop=False)
                pe.matmul(bank[5][:, :], W("msg2", k=64), stream2[b][0:F, :], start=False, stop=True
                          ).then_inc(sem("l2_m"), 1)
                if some("l2_rS", c):
                    pe.wait_ge(sem("l2_rS"), upto("l2_rS", c))
                pe.matmul(bank[6][:, :], W("app1"), xsT[b], start=True, stop=True).then_inc(sem("l2_yS"), 1)
                pe.wait_ge(sem("l2_rS"), upto("l2_rS", c + 1))
                if some("l2_addS", c):
                    pe.wait_ge(sem("l2_addS"), upto("l2_addS", c))
                tile_product(bank[1], [(fixed(rS), cen)], None, "l2_cS")
                pe.wait_ge(sem("l2_scan"), upto("l2_scan", c * 2 + 2))
                if some("l2_rD", c):
                    pe.wait_ge(sem("l2_rD"), upto("l2_rD", c))
                pe.matmul(bank[7][:, :], W("app1"), dT[:, b, :], start=True, stop=False)
                pe.matmul(bank[7][:, :], W("app2"), agg, start=False, stop=True).then_inc(sem("l2_yD"), 1)
                pe.wait_ge(sem("l2_rD"), upto("l2_rD", c + 1))
                if some("l2_D", c):
                    pe.wait_ge(sem("l2_D"), upto("l2_D", c))
                tile_product(bank[0], [(fixed(dT[:, b, :]), cen), (fixed(rD), cen)], None, "l2_cD")
            run_chunks(pe, l2)

            pe.wait_ge(sem("l2_D"), upto("l2_D", CH))

            def l3(c, b, k):
                pe.wait_ge(sem("l3_xw"), upto("l3_xw", c + 1))
                if some("l3_xAB", c * 2):
                    pe.wait_ge(sem("l3_xAB"), upto("l3_xAB", c * 2))
                for h in range(2):
                    for j in range(4):
                        mm = pe.transpose(bank[4 + h][:, j * P:(j + 1) * P],
                                          xw2[:, (2 * j + h) * P:(2 * j + h + 1) * P], eye)
                    mm.then_inc(sem("l3_T"), 1)
                if some("l3_scan", c * 2):
                    pe.wait_ge(sem("l3_scan"), upto("l3_scan", c * 2))
                for q in range(REL // 2):
                    pe.wait_ge(sem("l3_mask"), upto("l3_mask", c * REL + (2 * q + 2)))
                    for h in range(2):
                        mm = pe.matmul(bank[6][h * F:(h + 1) * F, :], relw[:, q, :], AB[:, h, q % 4, :],
                                       start=q == 0, stop=q == REL // 2 - 1)
                    mm.then_inc(sem("l3_pair"), 1)
                pe.wait_ge(sem("l3_rD"), upto("l3_rD", c + 1))
                if some("l3_addD", c):
                    pe.wait_ge(sem("l3_addD"), upto("l3_addD", c))
                tile_product(bank[0], [(fixed(rD), cen)], None, "l3_cD")
            run_chunks(pe, l3)

        @block.scalar
        def _(act):
            act.wait_ge(sem("consts"), 6)

            def deviation(dest, ss, final, p=P):
                scale = (1.0 + EPS) / F if final else 1.0 / F
                return act.activation(dest, ss, ACT.Sqrt, bias=epsc[:, 1:2] if final else epsc[:, 0:1],
                                      scale=scale)

            def node_square(u, n, layer):
                act.wait_ge(sem(f"a{u}_" + ("c0", "c1", "c2s")[layer]), upto(f"a{u}_" + ("c0", "c1", "c2s")[layer], n + 1))
                act.activation(node_sq[u], node_out[u] if layer == 2 else bank[2 * u][:, :], ACT.Square
                               ).then_inc(sem(f"a{u}_sq"), 1)

            def node_deviation(u, n, layer):
                act.wait_ge(sem(f"a{u}_ss"), n * 3 + (layer + 1))
                deviation(asmall[:, u, 1, :], asmall[:, u, 0, :], layer == 2).then_inc(sem(f"a{u}_sd"), 1)

            def node_turned(u, n, m):
                act.wait_ge(sem(f"a{u}_T"), n * 2 + m)
                act.activation(node_xT[u], bank[2 * u + 1][:, :], ACT.Copy).then_inc(sem(f"a{u}_xt"), 1)

            def node_relu(u, n):
                act.wait_ge(sem(f"a{u}_y"), n + 1)
                act.activation(node_sq[u], bank[2 * u + 1][:, :], ACT.Relu, bias=col("app_b")
                               ).then_inc(sem(f"a{u}_r"), 1)

            act.wait_ge(sem("weights_in"), 64)

            def stage1(c, b, k):
                for layer in range(2):
                    for u in range(LANES):
                        node_square(u, c, layer)
                    for u in range(LANES):
                        node_deviation(u, c, layer)
                    for u in range(LANES):
                        node_turned(u, c, layer + 1)
                for u in range(LANES):
                    node_relu(u, c)
                for u in range(LANES):
                    node_square(u, c, 2)
                for u in range(LANES):
                    node_deviation(u, c, 2)
                act.wait_ge(sem("p0_T"), upto("p0_T", c + 1))
                act.activation(D[:, cs(c)], bank[6][:, :], ACT.Copy).then_inc(sem("p0_D"), 1)
            run_chunks(act, stage1)

            def ln_square(stage, who, src, dest, after, c):
                act.wait_ge(sem(after), upto(after, c + 1))
                if some(f"{stage}_ss{who}", c):
                    act.wait_ge(sem(f"{stage}_ss{who}"), upto(f"{stage}_ss{who}", c))
                act.activation(dest, src, ACT.Square).then_inc(sem(f"{stage}_sq{who}"), 1)

            def ln_dev(stage, who, c):
                act.wait_ge(sem(f"{stage}_ss{who}"), upto(f"{stage}_ss{who}", c + 1))
                if some(f"{stage}_rs{who}", c):
                    act.wait_ge(sem(f"{stage}_rs{who}"), upto(f"{stage}_rs{who}", c))
                i = "DS".index(who)
                deviation(small[:, i, 1, :], small[:, i, 0, :], False).then_inc(sem(f"{stage}_sd{who}"), 1)

            def store_tab(l, stage, c, b, k):
                act.wait_ge(sem(f"{stage}_D"), upto(f"{stage}_D", c + 1))
                act.dma_start(dtab[l - 1][bass.ds(c * 1024, 1024), :].rearrange("(p s) f -> p (s f)", p=P),
                              dn[b]).then_inc(sem(f"tab{l}_st{b}"), 16)

            def turn_D(stage, c):
                act.wait_ge(sem(f"{stage}_T2"), upto(f"{stage}_T2", c + 1))
                act.activation(D[:, cs(c)], bank[2][:, :], ACT.Copy).then_inc(sem(f"{stage}_DT"), 1)

            def l0(c, b, k):
                act.wait_ge(sem(f"l0_rows{b}"), upto(f"l0_rows{b}", (k + 1) * (16 * TPC)))
                if some("l0_T", c - 1):
                    act.wait_ge(sem("l0_T"), upto("l0_T", c - 1))
                act.activation(XR[:, b, :, :], XM[:, b, :, 0:F], ACT.Copy).then_inc(sem("l0_dense"), 1)
                act.wait_ge(sem("l0_T"), upto("l0_T", c + 1))
                if some("l0_cS", c - 1):
                    act.wait_ge(sem("l0_cS"), upto("l0_cS", c - 1))
                act.activation(xsT[b], bank[4][:, :], ACT.Copy).then_inc(sem("l0_xsT"), 1)
                act.wait_ge(sem("l0_z1"), upto("l0_z1", c + 1))
                if some("l0_h2", c):
                    act.wait_ge(sem("l0_h2"), upto("l0_h2", c))
                act.activation(z1, bank[5][:, :], ACT.Identity, bias=fcol[:, 0:1]).then_inc(sem("l0_z1b"), 1)
                ln_square("l0", "S", bank[1][:, :], sqS, "l0_cS", c)
                act.wait_ge(sem("l0_z2"), upto("l0_z2", c + 1))
                act.wait_ge(sem("l0_h1"), upto("l0_h1", c + 1))
                act.activation(z1[0:64, :], bank[5][0:64, :], ACT.Identity, bias=col("b2", 64)
                               ).then_inc(sem("l0_z2b"), 1)
                ln_dev("l0", "S", c)
                act.wait_ge(sem("l0_e"), upto("l0_e", c + 1))
                if some("l0_msg", c):
                    act.wait_ge(sem("l0_msg"), upto("l0_msg", c))
                act.activation(eg, bank[5][:, :], ACT.Relu, bias=col("b3")).then_inc(sem("l0_eg"), 1)
                ln_square("l0", "D", bank[0][:, :], sqD, "l0_cD", c)
                ln_dev("l0", "D", c)
                store_tab(1, "l0", c, b, k)
                turn_D("l0", c)
            act.wait_ge(sem("fold_used"), 7)
            run_chunks(act, l0)

            def copy_ring(stage, c, b):
                act.activation(XR[:, b, :, :], rows64(S[:, cs(c)]), ACT.Copy).then_inc(sem(f"{stage}_copy"), 1)

            def last(c):
                return isinstance(c, int) and c == CH - 1

            def l1a(c, b, k):
                n = k + CH
                node_square(b, n, 0)
                node_deviation(b, n, 0)
                if not last(c):
                    if some("l1a_T", c):
                        act.wait_ge(sem("l1a_T"), upto("l1a_T", c))
                    copy_ring("l1a", c + 1, 1 - b)
                act.wait_ge(sem("l1a_T"), upto("l1a_T", c + 1))
                if some(f"l1a_stored{b}", k * 16):
                    act.wait_ge(sem(f"l1a_stored{b}"), upto(f"l1a_stored{b}", k * 16))
                if some("l1a_s", c - 1):
                    act.wait_ge(sem("l1a_s"), upto("l1a_s", c - 1))
                act.activation(xsT[b], bank[6][:, :], ACT.Copy).then_inc(sem("l1a_ST"), 1)
                node_turned(b, n, 1)
                node_square(b, n, 1)
                node_deviation(b, n, 1)
                node_turned(b, n, 2)
                node_relu(b, n)
                node_square(b, n, 2)
                node_deviation(b, n, 2)

            def run_ahead(body):
                for c in range(3):
                    body(c, c % 2, c // 2)
                with act.Fori(1, CH // 2 - 1) as i:
                    body(i * 2 + 1, 1, i)
                    body(i * 2 + 2, 0, i + 1)
                body(CH - 2, 1, CH // 2 - 1)
                body(CH - 1, 0, CH // 2)
            act.wait_ge(sem("l0_T"), upto("l0_T", CH))
            act.wait_ge(sem("l0_q"), upto("l0_q", CH))
            act.wait_ge(sem("l0_S"), upto("l0_S", CH))
            copy_ring("l1a", 0, 0)
            run_ahead(l1a)

            act.wait_ge(sem("l1_dve"), 1)
            act.activation(rt(3), rt(3), ACT.Gelu, bias=fcol[0:RP, 2:3]).then_inc(sem("l1_act"), 1)
            act.wait_ge(sem("l1_dve"), 2)
            act.activation(rt(3), rt(3), ACT.Exp).then_inc(sem("l1_act"), 1)

            def l1b(c, b, k):
                ln_square("l1b", "S", bank[1][:, :], sqS, "l1b_cS", c)
                ln_dev("l1b", "S", c)
                ln_square("l1b", "D", bank[0][:, :], sqD, "l1b_cD", c)
                ln_dev("l1b", "D", c)
                store_tab(2, "l1b", c, b, k)
                turn_D("l1b", c)
            run_chunks(act, l1b)

            def l2(c, b, k):
                if not last(c):
                    if some("l2_T", c):
                        act.wait_ge(sem("l2_T"), upto("l2_T", c))
                    if some("l2_addS", c):
                        act.wait_ge(sem("l2_addS"), upto("l2_addS", c))
                    copy_ring("l2", c + 1, 1 - b)
                act.wait_ge(sem("l2_T"), upto("l2_T", c + 1))
                if some("l2_yS", c - 1):
                    act.wait_ge(sem("l2_yS"), upto("l2_yS", c - 1))
                act.activation(xsT[b], bank[4][:, :], ACT.Copy).then_inc(sem("l2_xsT"), 1)
                act.wait_ge(sem("l2_yS"), upto("l2_yS", c + 1))
                if some("l2_cS", c):
                    act.wait_ge(sem("l2_cS"), upto("l2_cS", c))
                act.activation(rS, bank[6][:, :], ACT.Relu, bias=col("app_b")).then_inc(sem("l2_rS"), 1)
                ln_square("l2", "S", cadd, sqS, "l2_addS", c)
                ln_dev("l2", "S", c)
                act.wait_ge(sem("l2_yD"), upto("l2_yD", c + 1))
                if some("l2_cD", c):
                    act.wait_ge(sem("l2_cD"), upto("l2_cD", c))
                act.activation(rD, bank[7][:, :], ACT.Relu, bias=fcol[:, 1:2]).then_inc(sem("l2_rD"), 1)
                ln_square("l2", "D", bank[0][:, :], sqD, "l2_cD", c)
                ln_dev("l2", "D", c)
                store_tab(3, "l2", c, b, k)
                act.wait_ge(sem("l2_cD"), upto("l2_cD", c + 1))
                act.activation(D[:, cs(c)], dn[b], ACT.Copy).then_inc(sem("l2_keepD"), 1)
            act.wait_ge(sem("l1b_S"), upto("l1b_S", CH))
            copy_ring("l2", 0, 0)
            run_ahead(l2)

            def l3(c, b, k):
                if not last(c):
                    if some("l3_xw", c):
                        act.wait_ge(sem("l3_xw"), upto("l3_xw", c))
                    copy_ring("l3", c + 1, 1 - b)
                for h in range(2):
                    act.wait_ge(sem("l3_T"), upto("l3_T", c * 2 + (h + 1)))
                    if some("l3_mask", c * REL):
                        act.wait_ge(sem("l3_mask"), upto("l3_mask", c * REL))
                    act.activation((z1, h1)[h], bank[4 + h][:, :], ACT.Copy).then_inc(sem("l3_xAB"), 1)
                act.wait_ge(sem("l3_scan"), upto("l3_scan", c * 2 + 2))
                if some("l3_cD", c):
                    act.wait_ge(sem("l3_cD"), upto("l3_cD", c))
                act.activation(rD, agg, ACT.Relu).then_inc(sem("l3_rD"), 1)
                ln_square("l3", "D", eg, sqD, "l3_addD", c)
                ln_dev("l3", "D", c)
            act.wait_ge(sem("l2_S"), upto("l2_S", CH))
            act.wait_ge(sem("l2_T"), upto("l2_T", CH))
            copy_ring("l3", 0, 0)
            run_ahead(l3)

        @block.vector
        def _(dve):
            dve.wait_ge(sem("weights_in"), 64)
            dve.tensor_tensor(W("w_tgtI"), W("w_tgt"), eye, ALU.add).then_inc(sem("eye_plus"), 1)
            dve.tensor_tensor(W("res_wT"), W("res_wT"), eye, ALU.add).then_inc(sem("eye_plus"), 1)
            fl = [sqD[:, 0:TILES], sqS[:, 0:TILES], dn[0][:, 0:TILES]]
            dve.wait_ge(sem("dstc_in"), 16)
            dve.wait_ge(sem("index_in"), 64)
            dve.tensor_tensor(fl[0], dstc[:, :], nxtc[:, :], ALU.is_equal).then_inc(sem("nm_flags"), 1)
            dve.wait_ge(sem("nm_flags"), 1)
            dve.scalar_tensor_tensor(fl[1], fl[0], float(NO_ROW), dstc[:, :], ALU.mult, ALU.add
                                     ).then_inc(sem("nm_flags"), 1)
            dve.wait_ge(sem("nm_flags"), 2)
            dve.tensor_copy(outc[:, :], fl[1]).then_inc(sem("nm_flags"), 1)
            dve.tensor_scalar(fl[2], dstc[:, :], float(F + 1), float(F), ALU.mult, ALU.add
                              ).then_inc(sem("nm_flags"), 1)
            dve.wait_ge(sem("nm_flags"), 4)
            dve.scalar_tensor_tensor(fl[2], fl[0], float(8 * NO_ROW), fl[2], ALU.mult, ALU.add
                                     ).then_inc(sem("nm_flags"), 1)
            dve.wait_ge(sem("nm_flags"), 5)
            dve.tensor_copy(cellc[:, :], fl[2]).then_inc(sem("cells"), 1)
            dve.wait_ge(sem("runs_in"), 48)
            keep, cont, rep, pen = (runs[:, i, :, :] for i in range(4))
            dve.tensor_tensor(keep, rt(1).bitcast(I32), rt(0).bitcast(I32), ALU.is_equal).then_inc(sem("keep_run"), 1)
            dve.tensor_tensor(cont, rt(1).bitcast(I32), rt(2).bitcast(I32), ALU.is_equal).then_inc(sem("flags"), 1)
            dve.wait_ge(sem("keep_run"), 1)
            dve.wait_ge(sem("flags"), 1)
            dve.tensor_scalar(rep, cont, -1.0, 1.0, ALU.mult, ALU.add).then_inc(sem("flags"), 1)
            dve.tensor_scalar(pen, keep, -NEG, NEG, ALU.mult, ALU.add).then_inc(sem("flags"), 1)
            dve.wait_ge(sem("flags"), 3)
            for q, a in enumerate((keep, cont, pen)):
                dve.tensor_reduce(ends[:, q, :], a, AX.X, ALU.min).then_inc(sem("ends_static"), 1)
            dve.wait_ge(sem("fold"), 3)
            dve.tensor_copy(folded[:, 0:4, :], bank[6][:, :].rearrange("p (n m) -> p n m", n=4)
                            ).then_inc(sem("fold_used"), 1)
            dve.tensor_copy(WOC, bank[7][:, 0:128]).then_inc(sem("fold_used"), 1)
            dve.tensor_copy(edge1[:, :], bank[7][0:16, 128:256]).then_inc(sem("fold_used"), 1)
            dve.tensor_copy(attn_w[:, :], bank[7][:, 256:260]).then_inc(sem("fold_used"), 1)
            dve.tensor_tensor(fcol[:, 0:1], bank[7][:, 260:261], col("b1"), ALU.add).then_inc(sem("fold_used"), 1)
            dve.tensor_tensor(fcol[:, 1:2], bank[7][:, 261:262], col("app_b"), ALU.add).then_inc(sem("fold_used"), 1)
            dve.tensor_copy(fcol[:, 2:3], bank[7][:, 262:263]).then_inc(sem("fold_used"), 1)
            full = msg[:, 0:3 * P].rearrange("p (n m) -> p n m", n=3)
            dve.wait_ge(sem("consts"), 6)
            dve.tensor_copy(full, bank[5][:, 0:3 * P].rearrange("p (n m) -> p n m", n=3)).then_inc(sem("bias_rows"), 1)
            dve.wait_ge(sem("bias_rows"), 1)
            dve.tensor_tensor(full[:, 2, :], full[:, 2, :], full[:, 1, :], ALU.add).then_inc(sem("bias_rows"), 1)
            for part in range(3):
                r0 = 32 * part
                dve.wait_ge(sem("bias_rows"), 2 + 2 * part)
                for rr in range(4):
                    dv = dve.tensor_copy(brow[r0:r0 + 1, :, rr * P:(rr + 1) * P], full[r0:r0 + 1, :, :])
                dv.then_inc(sem("brow"), 1)
                if part < 2:
                    dve.tensor_copy(parts_b := h2[:, 0:192].bitcast(BF16).rearrange("p (n m) -> p n m", n=3), full
                                    ).then_inc(sem("bias_rows"), 1)
                    dve.wait_ge(sem("bias_rows"), 3 + 2 * part)
                    dve.wait_ge(sem("brow"), part + 1)
                    dve.tensor_tensor(full, full, parts_b, ALU.subtract).then_inc(sem("bias_rows"), 1)

            for q in range(3):
                dve.wait_ge(sem("static_T"), q + 1)
                dve.tensor_copy(rowbuf[0:1, q, 0:TILES], bank[7][0:1, 0:TILES]).then_inc(sem("static_row"), 1)
            dve.wait_ge(sem("static_row"), 3)

            tls = [0]

            def two_level(a, d0, d1, op0, op1, start, coef, reverse):
                n = tls[0]
                tls[0] += 1

                def way(t):
                    return t[:, ::-1] if reverse else t[:, :]
                if n:
                    if some("tl_done", 2 * n):
                        dve.wait_ge(sem("tl_done"), 2 * n)
                dve.tensor_tensor_scan(way(a[:, 0, :]), way(d0[:, 0, :]), way(d1[:, 0, :]), start, op0, op1
                                       ).then_inc(sem("tl_loc"), 1)
                dve.tensor_tensor_scan(way(a[:, 1, :]), way(d0[:, 1, :]), way(d1[:, 1, :]), start, op0, op1
                                       ).then_inc(sem("tl_ends"), 1)
                dve.memset(rowbuf[0:1, 3, :], start).then_inc(sem("tl_init"), 1)
                dve.wait_ge(sem("tl_init"), n + 1)
                dve.wait_ge(sem("tl_row"), n + 1)
                dve.tensor_tensor_scan(way(rowbuf[0:1, 3, 1:TILES + 1]), way(rowbuf[0:1, coef, 0:TILES]),
                                       way(bank[7][0:1, 0:TILES]), start, op0, op1).then_inc(sem("tl_carry"), 1)
                dve.wait_ge(sem("tl_cin"), n + 1)
                dve.tensor_copy(ends[:, 3, :], bank[7][0:RP, 256:258]).then_inc(sem("tl_cin_sb"), 1)
                dve.wait_ge(sem("tl_cin_sb"), n + 1)
                for g in range(2):
                    dve.tensor_tensor_scan(way(a[:, g, :]), way(d0[:, g, :]), way(d1[:, g, :]),
                                           ends[:, 3, g:g + 1], op0, op1).then_inc(sem("tl_done"), 1)
                dve.wait_ge(sem("tl_done"), 2 * n + 2)

            lasts = [0]

            def last_to_run(dest, src, tmp):
                lasts[0] += 1
                dve.tensor_tensor(tmp, src, rep, ALU.mult).then_inc(sem("rep_only"), 1)
                if some("rep_only", lasts[0]):
                    dve.wait_ge(sem("rep_only"), lasts[0])
                two_level(dest, cont, tmp, ALU.mult, ALU.add, 0.0, 1, True)

            dve.memset(rt(1), 1.0).then_inc(sem("unit"), 1)
            dve.wait_ge(sem("unit"), 1)
            two_level(rt(0), keep, rt(1), ALU.mult, ALU.add, 0.0, 0, False)
            last_to_run(rt(2), rt(0), rt(1))
            dve.reciprocal(rt(3), rt(2)).then_inc(sem("inv_run"), 1)

            def ln_apply(dest, src, rs):
                return dve.tensor_tensor(rows64(dest), rows64(src), bcast8(rs), ALU.mult)

            def node_sum(u, n, layer):
                dve.wait_ge(sem(f"a{u}_sq"), n * 3 + (layer + 1))
                dve.tensor_reduce(asmall[:, u, 0, :], rows64(node_sq[u]), AX.X, ALU.add
                                  ).then_inc(sem(f"a{u}_ss"), 1)

            def node_normalize(u, n, layer):
                dve.wait_ge(sem(f"a{u}_sd"), n * 3 + (layer + 1))
                dve.reciprocal(asmall[:, u, 2, :], asmall[:, u, 1, :]).then_inc(sem(f"a{u}_rs"), 1)
                dve.wait_ge(sem(f"a{u}_rs"), n * 3 + (layer + 1))
                if layer == 2:
                    ln_apply(node_out[u], node_out[u], asmall[:, u, 2, :]).then_inc(sem(f"a{u}_o"), 1)
                else:
                    ln_apply(node_x[u], bank[2 * u][:, :], asmall[:, u, 2, :]).then_inc(sem(f"a{u}_xn"), 1)

            def node_add(u, n):
                dve.wait_ge(sem(f"a{u}_c2"), n + 1)
                if some(f"a{u}_stored", n * 16):
                    dve.wait_ge(sem(f"a{u}_stored"), n * 16)
                dve.tensor_tensor(node_out[u], bank[2 * u][:, :], node_x[u], ALU.add
                                  ).then_inc(sem(f"a{u}_c2s"), 1)

            def stage1(c, b, k):
                for layer in range(3):
                    if layer == 2:
                        for u in range(LANES):
                            node_add(u, c)
                    for u in range(LANES):
                        node_sum(u, c, layer)
                    for u in range(LANES):
                        node_normalize(u, c, layer)
            run_chunks(dve, stage1)

            def ln_reduce(stage, who, src, c):
                i = "DS".index(who)
                dve.wait_ge(sem(f"{stage}_sq{who}"), upto(f"{stage}_sq{who}", c + 1))
                dve.tensor_reduce(small[:, i, 0, :], rows64(src), AX.X, ALU.add).then_inc(sem(f"{stage}_ss{who}"), 1)

            def ln_inverse(stage, who, c):
                i = "DS".index(who)
                dve.wait_ge(sem(f"{stage}_sd{who}"), upto(f"{stage}_sd{who}", c + 1))
                dve.reciprocal(small[:, i, 2, :], small[:, i, 1, :]).then_inc(sem(f"{stage}_rs{who}"), 1)
                dve.wait_ge(sem(f"{stage}_rs{who}"), upto(f"{stage}_rs{who}", c + 1))

            def run_scan(stage, c, b, data):
                if not (isinstance(c, int) and c == 0):
                    if some(f"{stage}_carry", c * 2):
                        dve.wait_ge(sem(f"{stage}_carry"), upto(f"{stage}_carry", c * 2))
                for h in range(2):
                    a, z = h * F, (h + 1) * F
                    if h:
                        dve.wait_ge(sem(f"{stage}_carry"), upto(f"{stage}_carry", c * 2 + 1))
                    dve.tensor_tensor_scan(agg[a:z, :], stream[a:z, 0, b, :], data[a:z, :],
                                           carry[a:z, :], ALU.mult, ALU.add).then_inc(sem(f"{stage}_scan"), 1)
                    dve.wait_ge(sem(f"{stage}_scan"), upto(f"{stage}_scan", c * 2 + (h + 1)))
                    o = F - a
                    dve.tensor_copy(carry[o:o + F, :], agg[a:z, CW - 1:CW]).then_inc(sem(f"{stage}_carry"), 1)

            def l0(c, b, k):
                dve.wait_ge(sem(f"l0_rows{b}"), upto(f"l0_rows{b}", (k + 1) * (16 * TPC)))
                dve.tensor_copy(qcol[:, tc(c)].rearrange("p (s o) -> p s o", o=1), XM[:, b, :, F:F + 1]
                                ).then_inc(sem("l0_q"), 1)
                dve.wait_ge(sem("l0_z1b"), upto("l0_z1b", c + 1))
                dve.scalar_tensor_tensor(h1, z1, SLOPE, z1, ALU.mult, ALU.max).then_inc(sem("l0_h1"), 1)
                ln_reduce("l0", "S", sqS, c)
                dve.wait_ge(sem("l0_z2b"), upto("l0_z2b", c + 1))
                if some("l0_e", c):
                    dve.wait_ge(sem("l0_e"), upto("l0_e", c))
                dve.scalar_tensor_tensor(h2[0:64, :], z1[0:64, :], SLOPE, z1[0:64, :], ALU.mult, ALU.max
                                         ).then_inc(sem("l0_h2"), 1)
                ln_inverse("l0", "S", c)
                ln_apply(S[:, cs(c)], bank[1][:, :], small[:, 1, 2, :]).then_inc(sem("l0_S"), 1)
                dve.wait_ge(sem("l0_eg"), upto("l0_eg", c + 1))
                dve.wait_ge(sem("l0_xs"), upto("l0_xs", c + 1))
                if some("l0_scan", c * 2):
                    dve.wait_ge(sem("l0_scan"), upto("l0_scan", c * 2))
                dve.scalar_tensor_tensor(msg, bank[6][:, :], col("b_src"), eg, ALU.add, ALU.mult
                                         ).then_inc(sem("l0_msg"), 1)
                dve.wait_ge(sem("l0_msg"), upto("l0_msg", c + 1))
                dve.wait_ge(sem(f"l0_stream{b}"), upto(f"l0_stream{b}", (k + 1) * 48))
                if some("l0_cD", c):
                    dve.wait_ge(sem("l0_cD"), upto("l0_cD", c))
                run_scan("l0", c, b, msg)
                ln_reduce("l0", "D", sqD, c)
                ln_inverse("l0", "D", c)
                if some(f"tab1_st{b}", k * 16):
                    dve.wait_ge(sem(f"tab1_st{b}"), k * 16)
                ln_apply(dn[b], bank[0][:, :], small[:, 0, 2, :]).then_inc(sem("l0_D"), 1)
            run_chunks(dve, l0)

            def l1a(c, b, k):
                n = k + CH
                node_sum(b, n, 0)
                node_normalize(b, n, 0)
                dve.wait_ge(sem("l1a_s"), upto("l1a_s", c + 1))
                dve.tensor_copy(sc[:, :, tc(c)], bank[7][:, 0:16].rearrange("p (q s) -> p q s", q=2)
                                ).then_inc(sem("l1a_sc"), 1)
                node_sum(b, n, 1)
                node_normalize(b, n, 1)
                node_add(b, n)
                node_sum(b, n, 2)
                node_normalize(b, n, 2)
            run_chunks(dve, l1a)

            dve.wait_ge(sem("l1a_sc"), upto("l1a_sc", CH))
            dve.wait_ge(sem("l0_e"), upto("l0_e", CH))
            for q in range(2):
                dve.tensor_copy(EB[:, 4 + q, 0:TILES].rearrange("p (c h j) -> p c h j", h=2, j=4),
                                sc[:, q, :].rearrange("p (c j h) -> p c h j", h=2, j=4)).then_inc(sem("l1_perm"), 1)
            dve.wait_ge(sem("l1_run"), 1)
            dve.wait_ge(sem("l1a_stored0"), upto("l1a_stored0", 16 * (CH // 2 + 1)))
            dve.wait_ge(sem("l1a_stored1"), upto("l1a_stored1", 16 * (CH // 2)))
            dve.wait_ge(sem("tab1_st0"), 16)
            s_src = bank[6][0:RP, 0:2 * P].rearrange("p (g n) -> p g n", g=2)
            s_dst = bank[6][0:RP, 2 * P:4 * P].rearrange("p (g n) -> p g n", g=2)
            last_to_run(rt(2), s_dst, rt(1))
            dve.tensor_tensor(rt(3), s_src, rt(2), ALU.add).then_inc(sem("l1_dve"), 1)
            dve.wait_ge(sem("l1_act"), 1)
            two_level(rt(0), pen, rt(3), ALU.add, ALU.max, NEG, 2, False)
            last_to_run(rt(2), rt(0), rt(1))
            dve.tensor_tensor(rt(3), rt(3), rt(2), ALU.subtract).then_inc(sem("l1_dve"), 1)
            dve.wait_ge(sem("l1_act"), 2)
            two_level(rt(0), keep, rt(3), ALU.mult, ALU.add, 0.0, 0, False)
            last_to_run(rt(2), rt(0), rt(1))
            dve.tensor_scalar(rt(2), rt(2), 1e-20, None, ALU.max).then_inc(sem("l1_den"), 1)
            dve.wait_ge(sem("l1_den"), 1)
            dve.reciprocal(rt(1), rt(2)).then_inc(sem("l1_den"), 1)
            dve.wait_ge(sem("l1_den"), 2)
            dve.tensor_tensor(rt(3), rt(3), rt(1), ALU.mult).then_inc(sem("attn_run"), 1)

            dve.wait_ge(sem("l0_carry"), upto("l0_carry", CH * 2))
            dve.memset(carry[:, :], 0.0).then_inc(sem("carry_clear"), 1)
            dve.wait_ge(sem("carry_clear"), 1)

            def l1b(c, b, k):
                dve.wait_ge(sem(f"l1b_stream{b}"), upto(f"l1b_stream{b}", (k + 1) * 64))
                if some("l1b_scan", c * 2):
                    dve.wait_ge(sem("l1b_scan"), upto("l1b_scan", c * 2))
                dve.tensor_tensor(msg, xsT[b], stream[:, 1, b, :], ALU.mult).then_inc(sem("l1b_msg"), 1)
                dve.wait_ge(sem("l1b_msg"), upto("l1b_msg", c + 1))
                if some("l1b_cD", c):
                    dve.wait_ge(sem("l1b_cD"), upto("l1b_cD", c))
                run_scan("l1b", c, b, msg)
                ln_reduce("l1b", "S", sqS, c)
                ln_inverse("l1b", "S", c)
                ln_apply(S[:, cs(c)], bank[1][:, :], small[:, 1, 2, :]).then_inc(sem("l1b_S"), 1)
                ln_reduce("l1b", "D", sqD, c)
                ln_inverse("l1b", "D", c)
                if some(f"tab2_st{b}", k * 16):
                    dve.wait_ge(sem(f"tab2_st{b}"), k * 16)
                ln_apply(dn[b], bank[0][:, :], small[:, 0, 2, :]).then_inc(sem("l1b_D"), 1)
            dve.wait_ge(sem("attn_out"), 16)
            run_chunks(dve, l1b)

            dve.wait_ge(sem("l1b_carry"), upto("l1b_carry", CH * 2))
            dve.memset(carry[:, :], 0.0).then_inc(sem("carry_clear"), 1)
            dve.wait_ge(sem("carry_clear"), 2)

            def l2(c, b, k):
                dve.wait_ge(sem("l2_cS"), upto("l2_cS", c + 1))
                if some("l2_S", c):
                    dve.wait_ge(sem("l2_S"), upto("l2_S", c))
                dve.tensor_tensor(rows64(cadd), rows64(bank[1][:, :]), XR[:, b, :, :], ALU.add
                                  ).then_inc(sem("l2_addS"), 1)
                dve.wait_ge(sem("l2_m"), upto("l2_m", c + 1))
                dve.wait_ge(sem(f"l2_stream{b}"), upto(f"l2_stream{b}", (k + 1) * 64))
                if some("l2_scan", c * 2):
                    dve.wait_ge(sem("l2_scan"), upto("l2_scan", c * 2))
                dve.tensor_tensor(msg, bank[5][:, :], stream[:, 1, b, :], ALU.mult).then_inc(sem("l2_msg"), 1)
                dve.wait_ge(sem("l2_msg"), upto("l2_msg", c + 1))
                if some("l2_yD", c):
                    dve.wait_ge(sem("l2_yD"), upto("l2_yD", c))
                run_scan("l2", c, b, msg)
                ln_reduce("l2", "S", sqS, c)
                ln_inverse("l2", "S", c)
                ln_apply(S[:, cs(c)], cadd, small[:, 1, 2, :]).then_inc(sem("l2_S"), 1)
                ln_reduce("l2", "D", sqD, c)
                ln_inverse("l2", "D", c)
                if some(f"tab3_st{b}", k * 16):
                    dve.wait_ge(sem(f"tab3_st{b}"), k * 16)
                if some("l2_keepD", c - 1):
                    dve.wait_ge(sem("l2_keepD"), upto("l2_keepD", c - 1))
                ln_apply(dn[b], bank[0][:, :], small[:, 0, 2, :]).then_inc(sem("l2_D"), 1)
            dve.wait_ge(sem("tab2_st0"), 16 * (CH // 2 + 1))
            dve.wait_ge(sem("tab2_st1"), 16 * (CH // 2))
            dve.wait_ge(sem("l1b_T2"), upto("l1b_T2", CH))
            run_chunks(dve, l2)

            dve.wait_ge(sem("l2_carry"), upto("l2_carry", CH * 2))
            dve.memset(carry[:, :], 0.0).then_inc(sem("carry_clear"), 1)
            dve.wait_ge(sem("carry_clear"), 3)
            dve.wait_ge(sem("tab3_st0"), 16 * (CH // 2 + 1))
            dve.wait_ge(sem("tab3_st1"), 16 * (CH // 2))
            dve.wait_ge(sem("l2_keepD"), upto("l2_keepD", CH))

            def l3(c, b, k):
                dve.wait_ge(sem(f"l3_rows{b}"), upto(f"l3_rows{b}", (k + 1) * (16 * TPC)))
                if some("l3_T", c * 2):
                    dve.wait_ge(sem("l3_T"), upto("l3_T", c * 2))
                dve.tensor_tensor(xw2.rearrange("p (s d f) -> p s d f", d=2, f=F),
                                  XR[:, b, :, :].rearrange("p s (o f) -> p s o f", o=1).broadcast_to([P, TPC, 2, F]),
                                  wcol[:, tc(c)].rearrange("p (s o d) -> p s o d", o=1, d=1
                                                           ).broadcast_to([P, TPC, 2, F]),
                                  ALU.mult).then_inc(sem("l3_xw"), 1)
                dve.wait_ge(sem(f"l3_stream{b}"), upto(f"l3_stream{b}", (k + 1) * 48))
                for q in range(REL // 2):
                    for h in range(2):
                        if q == 0:
                            dve.wait_ge(sem("l3_xAB"), upto("l3_xAB", c * 2 + (h + 1)))
                        if h == 0:
                            if some("l3_pair", c * (REL // 2) + (q - 3)):
                                dve.wait_ge(sem("l3_pair"), upto("l3_pair", c * (REL // 2) + (q - 3)))
                        dve.scalar_tensor_tensor(AB[:, h, q % 4, :], (stream[:, 1, b, :], stream2[b])[h].bitcast(I32),
                                                 relid[:, q:q + 1], (z1, h1)[h], ALU.is_equal, ALU.mult
                                                 ).then_inc(sem("l3_mask"), 1)
                dve.wait_ge(sem("l3_pair"), upto("l3_pair", (c + 1) * (REL // 2)))
                if some("l3_rD", c):
                    dve.wait_ge(sem("l3_rD"), upto("l3_rD", c))
                run_scan("l3", c, b, bank[6])
                dve.wait_ge(sem("l3_cD"), upto("l3_cD", c + 1))
                if some("l3_D", c):
                    dve.wait_ge(sem("l3_D"), upto("l3_D", c))
                dve.tensor_tensor(eg, bank[0][:, :], D[:, cs(c)], ALU.add).then_inc(sem("l3_addD"), 1)
                ln_reduce("l3", "D", sqD, c)
                ln_inverse("l3", "D", c)
                if some(f"final_st{b}", k * ROWS):
                    dve.wait_ge(sem(f"final_st{b}"), k * ROWS)
                ln_apply(dn[b], eg, small[:, 0, 2, :]).then_inc(sem("l3_D"), 1)
            dve.wait_ge(sem("a0_stored"), 16 * (CH + 13))
            dve.wait_ge(sem("a1_stored"), 16 * (CH + 12))
            run_chunks(dve, l3)


def kernel(**inputs):
    import numpy as np
    import concourse.bacc as bacc
    from concourse import mybir as mb
    from concourse.bass_utils import run_bass_kernel_spmd as run

    g = {k: np.asarray(v) for k, v in inputs.items()}
    x, src, dst = g["x"], g["src"], g["dst"]
    H = F

    def pad_slots(a, fill):
        o = np.full((SLOTS,) + a.shape[1:], fill, a.dtype)
        o[:E] = a
        return o

    def node_cols(a):
        return np.ascontiguousarray(a.reshape(CH, 2, 4, P).transpose(3, 0, 2, 1).reshape(P, TILES))

    def feature_major(a):
        f = a.shape[1]
        return np.ascontiguousarray(a.reshape(CH, 2, CW, f).transpose(1, 3, 0, 2).reshape(2 * f, CH * CW))

    dst_p = pad_slots(dst, N)
    nxt = np.append(dst_p[1:], np.array([-1], dst.dtype))
    run_ = np.concatenate([np.array([-1], dst.dtype), dst_p, np.array([-1], dst.dtype)])
    rows = node_cols(np.arange(SLOTS)) * 0 + (
        (np.arange(CH)[None, :, None] * P + np.arange(P)[:, None, None]) * TPC
        + np.arange(TPC)[None, None, :]).reshape(P, TILES)
    xp = np.zeros((NPAD, F), x.dtype)
    xp[:N] = x
    xT = np.ascontiguousarray(xp.reshape(NB, P, 4, 2, F).transpose(3, 4, 0, 2, 1).reshape(P, NB * CW))

    def bd(a):
        k, m = a.shape
        o = np.zeros((P, P), np.float32)
        o[:k, :m] = a
        o[k:2 * k, m:2 * m] = a
        return o

    W1 = g["L0_gnn_W1"]
    aw = g["L1_gnn_attn_w"]
    Wm, Wa = g["L2_gnn_W_msg_w"], g["L2_gnn_W_apply_w"]
    w3 = np.zeros((P, P), np.float32)
    w3[0:32, 0:64] = g["L0_gnn_W3"].T
    w3[32:64, 64:128] = g["L0_gnn_W3"].T
    attn_rep = np.concatenate([np.repeat(aw[:64, None], P, 1), np.repeat(aw[64:, None], P, 1)])
    piece = {
        "eye": np.eye(P, dtype=np.float32),
        "cen": bd(np.eye(F, dtype=np.float32) - np.float32(1.0 / F)),
        "w_src": bd(g["L0_gnn_W_src"]), "w_tgt": bd(g["L0_gnn_W_tgt"]),
        "w_srcT": bd(g["L0_gnn_W_src"].T),
        "w1aT": bd(W1[:, :64].T), "w1bT": bd(W1[:, 64:128].T), "w1cT": bd(W1[:, 128:].T),
        "w2T": bd(g["L0_gnn_W2"].T), "w3rep": w3,
        "res_wT": bd(g["L1_gnn_res_W"].T), "w_outT": bd(g["L1_gnn_W_out"].T),
        "w_tgtI": np.zeros((P, P), np.float32), "attn_rep": attn_rep,
        "msg1": bd(Wm[:64]), "msg2": bd(Wm[64:]), "app1": bd(Wa[:64]), "app2": bd(Wa[64:]),
        "w_edge": bd(g["L0_gnn_W_edge"]),
    }
    wpack = np.concatenate([piece[n] for n in PIECES], 1)

    def st(v):
        o = np.zeros((P,), np.float32)
        o[:2 * len(v)] = np.concatenate([v, v])
        return o
    z = np.zeros(64, np.float32)
    column = {
        "b_src": st(g["L0_gnn_b_src"]), "b_tgt": st(g["L0_gnn_b_tgt"]), "b_edge": st(g["L0_gnn_b_edge"]),
        "b1": st(g["L0_gnn_b1"]), "b2": st(g["L0_gnn_b2"]), "b3": np.repeat(g["L0_gnn_b3"], P),
        "res_b": st(g["L1_gnn_res_b"]), "b_out": st(g["L1_gnn_b_out"]), "msg_b": st(g["L2_gnn_W_msg_b"]),
        "app_b": st(g["L2_gnn_W_apply_b"]),
        "attn1_0": np.concatenate([aw[:64], z]), "attn1_1": np.concatenate([z, aw[:64]]),
        "attn2_0": np.concatenate([aw[64:], z]), "attn2_1": np.concatenate([z, aw[64:]]),
    }
    cpack = np.ascontiguousarray(np.stack([column[n] for n in COLS], 1))
    rw = g["L3_gnn_weight"].reshape(REL // 2, 2 * F, F).transpose(1, 0, 2).reshape(P, -1)
    relid = (2 * np.arange(REL // 2)[None, :] + (np.arange(P)[:, None] >= F)).astype(np.float32)
    arrays = {
        "x": x,
        "xmap_in": np.concatenate([x, np.full((N, 1), NO_ROW, x.dtype)], 1),
        "xT": xT,
        "dst_col": node_cols(dst_p), "nxt_col": node_cols(nxt), "src_col": node_cols(pad_slots(src, 0)),
        "row_col": rows.astype(np.float32), "dst_run": run_,
        "attr8T": feature_major(pad_slots(g["edge_attr_8"], 0)),
        "attr32T": feature_major(pad_slots(g["edge_attr_32"], 0)),
        "rel_flat": pad_slots(g["edge_type_16"], 0),
        "weight_col": node_cols(pad_slots(g["edge_weight1"][:, 0], 0)),
        "wpack": wpack, "cpack": cpack, "relpack": np.concatenate([rw, relid], 1),
    }
    arrays = {k: np.ascontiguousarray(v) for k, v in arrays.items()}

    nc = bacc.Bacc("TRN2", target_bir_lowering=False, num_devices=1)
    aps = [nc.dram_tensor(f"in_{k}", v.shape, mb.dt.from_np(v.dtype), kind="ExternalInput").ap()
           for k, v in arrays.items()]
    o = nc.dram_tensor("out_0", (NPAD, F), F32, kind="ExternalOutput").ap()
    build(nc, *aps, o)
    r = run(nc, [{f"in_{k}": v for k, v in arrays.items()}], core_ids=[0])
    return r.results[0]["out_0"][:N]
```

```python
from contextlib import ExitStack

import concourse.bass as bass
from concourse import mybir

F32 = mybir.dt.float32
BF16 = mybir.dt.bfloat16
I32 = mybir.dt.int32
ALU = mybir.AluOpType
ACT = mybir.ActivationFunctionType
AX = mybir.AxisListType

N, E, F, P = 100000, 25000, 64, 128
REL = 16
CW = 512
CH = -(-E // (2 * CW))
SLOTS = CH * 2 * CW
TILES = SLOTS // P
TPC = TILES // CH
RP = TILES // 2
NB = 4 * CH
NPAD = NB * 2 * CW
EPS = 1e-5
SLOPE = 0.01
NO_ROW = 1 << 20
NEG = -1.0e30
NB1 = 3 * CH
assert NPAD >= N and CH % 2 == 1 and NB1 % 2 == 1

PIECES = ["eye", "cen", "w_src", "w_tgt", "w_srcT", "w1aT", "w1bT", "w1cT", "w2T", "w3rep",
          "res_wT", "w_outT", "w_tgtI", "attn_rep", "msg1", "app1", "app2", "w_edge", "msg2"]
COLS = ["b_src", "b_tgt", "b_edge", "b1", "b2", "b3", "res_b", "b_out", "msg_b", "app_b",
        "attn1_0", "attn1_1", "attn2_0", "attn2_1"]


ROWS = 16 * TPC
LN = {f"{what}{who}": 1 for what in ("sq", "ss", "sd", "rs") for who in "DS"}
BOTH = {"scan": 2, "carry": 2, "msg": 1, "cD": 1, "cS": 1, "D": 1, "S": 1, **LN}
STAGES = ["p0", "l0", "l1a", "l1b", "l2", "l3"]
PER_CHUNK = {
    "p0": {"rows0": ROWS, "rows1": ROWS, "idx": 1, "T": 1},
    "l0": {"rows0": ROWS, "rows1": ROWS, "idx": 1, "T": 1, "stream0": 32, "stream1": 32, "xsT": 1,
           "T2": 1, "DT": 1, **BOTH},
    "l1a": {"rows0": ROWS, "rows1": ROWS, "idx": 1, "T": 1, "stream0": 16, "stream1": 16, "copy": 1},
    "l1b": {"stream0": 64, "stream1": 64, "T2": 1, "DT": 1, **BOTH},
    "l2": {"rows0": ROWS, "rows1": ROWS, "idx": 1, "T": 1, "stream0": 32, "stream1": 32, "copy": 1,
           "keep0": 16, "keep1": 16, "xsT": 1, "rD": 1, **BOTH},
    "l3": {"rows0": ROWS, "rows1": ROWS, "idx": 1, "T": 2, "stream0": 32, "stream1": 32, "copy": 1,
           "keep0": 16, "keep1": 16,
           "rD": 1, "scan": 2, "carry": 2, "cD": 1, "D": 1, "sqD": 1, "ssD": 1, "sdD": 1, "rsD": 1},
}


def run_chunks(eng, body, tail=0):
    for c in range(3):
        body(c, c % 2, c // 2)
    with eng.Fori(1, (CH - tail) // 2) as i:
        body(i * 2 + 1, 1, i)
        body(i * 2 + 2, 0, i + 1)
    for c in range(CH - tail, CH):
        body(c, c % 2, c // 2)


def run_pipe(eng, body, depth):
    def step(t):
        body(*((t - p, (t - p) % 2, (t - p) // 2) if 0 <= t - p < CH else None for p in range(depth)))

    def loop_step(i, t):
        body(*((i * 2 + (t - p), (t - p) % 2, i + (t - p) // 2) for p in range(depth)))
    peeled = 2 * depth - 1
    for t in range(peeled):
        step(t)
    with eng.Fori(peeled // 2, CH // 2) as i:
        loop_step(i, 1)
        loop_step(i, 2)
    for t in range(CH, CH + depth - 1):
        step(t)


def node_phases(h, par, lo, hi):
    out = []
    for p in range(4):
        d = par - p
        blk, b, k = h * 2 + d, d % 2, h + d // 2
        out.append((blk, b, k) if not isinstance(h, int) or lo <= blk < hi else None)
    return out


def run_nodes_alone(eng, step):
    with eng.Fori(CH, (NB1 - 1) // 2) as h:
        step(h, 0, 0, NB1)
        step(h, 1, 0, NB1)
    for i in range((NB1 - 1) // 2 * 2, NB1 + 3):
        step(i // 2, i % 2, 0, NB1)


def nodes_beside(eng, step, c, b, k):
    step(k + (NB1 + b) // 2, (NB1 + b) % 2, NB1, NB)


def build(nc, x, xmap_in, xT, dst_col, nxt_col, src_col, row_col, dst_run, attr8T, attr32T,
          rel_flat, weight_col, wpack, cpack, relpack, out):
    with ExitStack() as ctx:
        def sb(name, shape, dt=F32):
            return ctx.enter_context(nc.sbuf_tensor(name, shape, dt))

        sems = {}

        def signal_of(name):
            stage, _, what = name.partition("_")
            if stage not in STAGES or what not in PER_CHUNK[stage]:
                return name, 0
            chunks = {"0": CH // 2 + 1, "1": CH // 2}.get(what[-1], CH)
            return what, sum(PER_CHUNK[s].get(what, 0) * chunks for s in STAGES[:STAGES.index(stage)])

        def sem(name):
            name = signal_of(name)[0]
            if name not in sems:
                sems[name] = ctx.enter_context(nc.semaphore(name))
            return sems[name]

        def upto(name, value):
            first = signal_of(name)[1]
            return max(value, 0) + first if isinstance(value, int) else value + first

        def some(name, value):
            at = upto(name, value)
            return not isinstance(at, int) or at > 0

        xmap = nc.dram_tensor("xmap", (N, F + 1), F32, kind="Internal").ap()
        dtab = [nc.dram_tensor(f"dtab{l}", (SLOTS, F), F32, kind="Internal").ap() for l in (1, 2, 3)]
        keep_flat = nc.dram_tensor("keep_flat", (SLOTS,), F32, kind="Internal").ap()
        inv_flat = nc.dram_tensor("inv_flat", (SLOTS,), F32, kind="Internal").ap()
        attn_flat = nc.dram_tensor("attn_flat", (SLOTS,), F32, kind="Internal").ap()
        xmap_cells = xmap.rearrange("n (f o) -> (n f) o", o=1)

        S = sb("S", [P, CH * CW])
        D = sb("D", [P, CH * CW])
        XR = sb("XR", [P, 2, TPC, F])
        idx_st = sb("idx_st", [P, 2, TPC], I32)
        row_st = sb("row_st", [P, 2, TPC])
        sidx_st = sb("sidx_st", [P, 2, TPC], I32)
        dstc = sb("dstc", [P, TILES], I32)
        srcc = sb("srcc", [P, TILES], I32)
        nxtc = sb("nxtc", [P, TILES], I32)
        rowc = sb("rowc", [P, TILES])
        qcol = sb("qcol", [P, TILES], I32)
        outc = sb("outc", [P, TILES], I32)
        cellc = sb("cellc", [P, TILES], I32)
        wcol = sb("wcol", [P, TILES])
        sc = sb("sc", [P, 2, TILES])
        stream = sb("stream", [P, 2, 2, CW])
        attr = sb("attr", [16, 2, CW])
        w = sb("w", [P, len(PIECES), P])
        cols = sb("cols", [P, len(COLS)])
        relw = sb("relw", [P, REL // 2, F])
        relid = sb("relid", [P, REL // 2])
        folded = sb("folded", [P, 5, P])
        edge1 = sb("edge1", [16, P])
        attn_w = sb("attn_w", [P, 4])
        fcol = sb("fcol", [P, 3])
        ones_b = sb("ones_b", [P, P], BF16)
        one = sb("one", [1, 1])
        epsc = sb("epsc", [P, 2])
        brow = sb("brow", [P, 3, CW], BF16)
        bres = sb("bres", [1, 2, P])
        NT = sb("NT", [P, 13, CW])
        dT = sb("dT", [P, 2, CW])
        EB = sb("EB", [P, 12, CW])
        small = sb("small", [P, 2, 3, 8])
        asmall = sb("asmall", [P, 3, 3, 8])
        token = sb("token", [1, 3])
        carry = sb("carry", [P, 1])
        runs = sb("runs", [RP, 4, 2, P])
        rowbuf = sb("rowbuf", [1, 4, TILES + 2])
        ends = sb("ends", [RP, 4, 2])

        bank = [ctx.enter_context(nc.psum_tensor(f"bank{i}", [P, CW], F32)) for i in range(8)]

        def W(name, k=P, m=P):
            return w[0:k, PIECES.index(name), 0:m]

        def col(name, m=P):
            return cols[0:m, COLS.index(name):COLS.index(name) + 1]

        A1, B1, M0, M1, WOC = (folded[:, i, :] for i in range(5))
        eye = W("eye")
        cen = W("cen")

        def rows64(t):
            return t.rearrange("p (s f) -> p s f", f=F)

        def bcast8(t):
            return t.rearrange("p (s o) -> p s o", o=1).broadcast_to([P, 8, F])

        def cs(c):
            return bass.ds(c * CW, CW)

        def tc(c):
            return bass.ds(c * TPC, TPC)

        def half_stream(flat, c):
            v = flat[bass.ds(c * 2 * CW, 2 * CW)].rearrange("(h o n) -> h o n", h=2, o=1)
            return v.broadcast_to([2, F, CW])

        node_in = [NT[:, 0, :], NT[:, 1, :]]
        node_sq = [NT[:, 2, :], NT[:, 3, :], NT[:, 4, :]]
        node_x1, node_x1T = NT[:, 5, :], NT[:, 6, :]
        node_x2, node_x2T = [NT[:, 7, :], NT[:, 8, :]], NT[:, 9, :]
        node_r, node_out = NT[:, 10, :], [NT[:, 11, :], NT[:, 12, :]]

        xsT, z1, h1 = [EB[:, i, :] for i in (0, 1)], EB[:, 2, :], EB[:, 3, :]
        h2, eg, msg = EB[:, 4, :], EB[:, 4, :], EB[:, 5, :]
        agg = EB[:, 6, :]
        sqD, sqS = EB[:, 7, :], EB[:, 8, :]
        dn = [EB[:, 9, :], EB[:, 10, :]]
        z2 = EB[:, 11, :]
        stream2 = [NT[:, 8, :], NT[:, 9, :]]
        rD, rS, cadd = NT[:, 10, :], NT[:, 11, :], NT[:, 12, :]
        xw2 = NT[:, 11:13, :].rearrange("p a n -> p (a n)")
        XM = NT[:, 0:3, :].rearrange("p a n -> p (a n)")[:, 0:2 * TPC * (F + 1)].rearrange(
            "p (b s f) -> p b s f", b=2, s=TPC)

        def rt(i):
            return EB[0:RP, i, 0:2 * P].rearrange("p (g n) -> p g n", g=2)

        block = ctx.enter_context(nc.Block())

        @block.sync
        def _(sp):
            sp.dma_start(dstc[:, :], dst_col).then_inc(sem("dstc_in"), 16)
            sp.dma_start(w[:, :, :], wpack.rearrange("p (n m) -> p n m", m=P)).then_inc(sem("weights_in"), 16)
            sp.dma_start(cols[:, :], cpack).then_inc(sem("weights_in"), 16)
            sp.dma_start(relw[:, :, :], relpack[:, 0:REL // 2 * F].rearrange("p (k m) -> p k m", m=F)
                         ).then_inc(sem("weights_in"), 16)
            sp.dma_start(relid[:, :], relpack[:, REL // 2 * F:]).then_inc(sem("weights_in"), 16)
            sp.dma_start(nxtc[:, :], nxt_col).then_inc(sem("index_in"), 16)
            sp.dma_start(srcc[:, :], src_col).then_inc(sem("index_in"), 16)
            sp.dma_start(rowc[:, :], row_col).then_inc(sem("index_in"), 16)
            sp.dma_start(wcol[:, :], weight_col).then_inc(sem("index_in"), 16)
            for i in range(3):
                sp.dma_start(rt(i).bitcast(I32),
                             dst_run[i:i + SLOTS].rearrange("(g p n) -> p g n", g=2, n=P)
                             ).then_inc(sem("runs_in"), 16)

            def node_load(blk, b, k):
                if not isinstance(blk, int) or blk > 1:
                    if some("a_c0", blk - 1):
                        sp.wait_ge(sem("a_c0"), blk - 1)
                sp.dma_start(node_in[b], xT[:, cs(blk)]).then_inc(sem(f"a_in{b}"), 16)

            def node_store(blk, b, k):
                sp.wait_ge(sem("a_out"), blk + 1)
                sp.dma_start(out[bass.ds(blk * 1024, 1024), :].rearrange("(p s) f -> p (s f)", p=P),
                             node_out[b]).then_inc(sem(f"a_stored{b}"), 16)

            def node_io(h, par, lo, hi):
                nxt = h * 2 + (par + 1)
                if not isinstance(h, int) or nxt < hi:
                    node_load(nxt, (par + 1) % 2, None)
                last = node_phases(h, par, lo, hi)[3]
                if last:
                    node_store(*last)

            node_load(0, 0, 0)
            sp.wait_ge(sem("keep_run"), 1)
            sp.dma_start(keep_flat.rearrange("(g p n) -> p g n", g=2, n=P), runs[:, 0, :, :]
                         ).then_inc(sem("flat_out"), 16)
            sp.wait_ge(sem("inv_run"), 1)
            sp.dma_start(inv_flat.rearrange("(g p n) -> p g n", g=2, n=P), rt(3)
                         ).then_inc(sem("flat_out"), 16)

            def stage1(c, b, k):
                node_io(c, 0, 0, NB1)
                sp.dma_start(xmap[bass.ds(c * (N // CH), N // CH), :].rearrange("(a n) f -> a (n f)", a=16),
                             xmap_in[bass.ds(c * (N // CH), N // CH), :].rearrange("(a n) f -> a (n f)", a=16)
                             ).then_inc(sem("xmap_init"), 16)
                node_io(c, 1, 0, NB1)
            run_chunks(sp, stage1)
            run_nodes_alone(sp, node_io)

            sp.wait_ge(sem("flat_out"), 32)
            sp.wait_ge(sem("p0_D"), upto("p0_D", CH))


            def l0(front, mid, back):
                if front:
                    c, b, k = front
                    if some("l0_z1", c - 1):
                        sp.wait_ge(sem("l0_z1"), upto("l0_z1", c - 1))
                    sp.dma_start(attr[:, b, :], attr8T[:, cs(c)]).then_inc(sem(f"l0_attr{b}"), 16)
                if mid:
                    c, b, k = mid
                    sp.wait_ge(sem("ring_clear"), 1)
                    if some("l0_cD", c - 1):
                        sp.wait_ge(sem("l0_cD"), upto("l0_cD", c - 1))
                    sp.dma_start(dT[:, b, :], D[:, cs(c)]).then_inc(sem(f"l0_stream{b}"), 16)
                    sp.dma_start(stream[:, 0, b, :], half_stream(keep_flat, c)).then_inc(sem(f"l0_stream{b}"), 16)
            run_pipe(sp, l0, 3)


            def l1a_D(c, b):
                if some("l1a_s", c - 1):
                    sp.wait_ge(sem("l1a_s"), upto("l1a_s", c - 1))
                sp.dma_start(dT[:, b, :], D[:, cs(c)]).then_inc(sem(f"l1a_stream{b}"), 16)

            def l1a(c, b, k):
                if not (isinstance(c, int) and c == CH - 1):
                    l1a_D(c + 1, 1 - b)
                sp.wait_ge(sem("ring_clear"), 1)
                sp.wait_ge(sem("l1a_ST"), upto("l1a_ST", c + 1))
                sp.dma_start(S[:, cs(c)], xsT[b]).then_inc(sem(f"l1a_stored{b}"), 16)
                nodes_beside(sp, node_io, c, b, k)

            sp.wait_ge(sem("l0_DT"), upto("l0_DT", CH))
            node_load(NB1, NB1 % 2, None)
            l1a_D(0, 0)
            run_chunks(sp, l1a, tail=2)
            for i in range(NB, NB + 3):
                node_io(i // 2, i % 2, NB1, NB)
            sp.wait_ge(sem("l1a_stored0"), upto("l1a_stored0", 16 * (CH // 2 + 1)))
            sp.wait_ge(sem("l1a_stored1"), upto("l1a_stored1", 16 * (CH // 2)))

            sp.wait_ge(sem("attn_run"), 1)
            sp.dma_start(attn_flat.rearrange("(g p n) -> p g n", g=2, n=P), rt(3)
                         ).then_inc(sem("attn_out"), 16)
            sp.wait_ge(sem("attn_out"), 16)

            def l1b(c, b, k):
                if some("l1b_cD", c - 1):
                    sp.wait_ge(sem("l1b_cD"), upto("l1b_cD", c - 1))
                sp.dma_start(dT[:, b, :], D[:, cs(c)]).then_inc(sem(f"l1b_stream{b}"), 16)
                sp.dma_start(xsT[b], S[:, cs(c)]).then_inc(sem(f"l1b_stream{b}"), 16)
                sp.dma_start(stream[:, 1, b, :], half_stream(attn_flat, c)).then_inc(sem(f"l1b_stream{b}"), 16)
                sp.dma_start(stream[:, 0, b, :], half_stream(keep_flat, c)).then_inc(sem(f"l1b_stream{b}"), 16)
            run_chunks(sp, l1b)

            sp.wait_ge(sem("l1b_DT"), upto("l1b_DT", CH))

            def l2(front, mid, back):
                if front:
                    c, b, k = front
                    if some("l2_msg", c - 1):
                        sp.wait_ge(sem("l2_msg"), upto("l2_msg", c - 1))
                    sp.dma_start(stream2[b][0:F, :], attr32T[:, cs(c)]).then_inc(sem(f"l2_stream{b}"), 16)
                    sp.dma_start(stream[:, 1, b, :], half_stream(inv_flat, c)).then_inc(sem(f"l2_stream{b}"), 16)
                    if some("l2_scan", (c - 1) * 2):
                        sp.wait_ge(sem("l2_scan"), upto("l2_scan", (c - 1) * 2))
                    sp.dma_start(stream[:, 0, b, :], half_stream(keep_flat, c)).then_inc(sem(f"l2_keep{b}"), 16)
                if mid:
                    c, b, k = mid
                    sp.wait_ge(sem("ring_clear"), 1)
                    if some("l2_cD", c - 1):
                        sp.wait_ge(sem("l2_cD"), upto("l2_cD", c - 1))
                    sp.dma_start(dT[:, b, :], D[:, cs(c)]).then_inc(sem(f"l2_dT{b}"), 16)
            run_pipe(sp, l2, 3)

            def rel_half(c, h):
                v = rel_flat[bass.ds(c * 2 * CW + h * CW, CW)].rearrange("(o n) -> o n", o=1)
                return v.broadcast_to([P, CW])

            sp.wait_ge(sem("l2_msg"), upto("l2_msg", CH))
            sp.wait_ge(sem("l2_scan"), upto("l2_scan", CH * 2))

            def l3(c, b, k):
                if some("l3_mask", (c - 1) * REL):
                    sp.wait_ge(sem("l3_mask"), upto("l3_mask", (c - 1) * REL))
                sp.dma_start(stream[:, 1, b, :].bitcast(I32), rel_half(c, 0)).then_inc(sem(f"l3_stream{b}"), 16)
                sp.dma_start(stream2[b].bitcast(I32), rel_half(c, 1)).then_inc(sem(f"l3_stream{b}"), 16)
                if some("l3_scan", (c - 1) * 2):
                    sp.wait_ge(sem("l3_scan"), upto("l3_scan", (c - 1) * 2))
                sp.dma_start(stream[:, 0, b, :], half_stream(keep_flat, c)).then_inc(sem(f"l3_keep{b}"), 16)
            run_chunks(sp, l3)
            sp.wait_ge(sem("a_stored0"), 16 * (NB // 2))
            sp.wait_ge(sem("a_stored1"), 16 * (NB // 2))
            sp.wait_ge(sem("final_st0"), 16 * TPC * (CH // 2 + 1))
            sp.wait_ge(sem("final_st1"), 16 * TPC * (CH // 2))

        @block.gpsimd
        def _(pool):
            last_node, last_row, last_cell = (pool.to_reg(v) for v in (N - 1, SLOTS - 1, N * (F + 1) - 1))
            pool.memset(token[:, :], 0.0).then_inc(sem("token"), 1)
            pool.wait_ge(sem("token"), 1)
            pool.memset(XR[:, :, :, :], 0.0).then_inc(sem("ring_clear"), 1)
            pool.memset(ones_b[:, :], 1.0).then_inc(sem("consts"), 1)
            pool.memset(one[:, :], 1.0).then_inc(sem("consts"), 1)
            pool.memset(epsc[:, 0:1], EPS).then_inc(sem("consts"), 1)
            pool.memset(epsc[:, 1:2], EPS * EPS).then_inc(sem("consts"), 1)
            pool.memset(brow[:, :, :], 0.0).then_inc(sem("consts"), 1)
            pool.memset(carry[:, :], 0.0).then_inc(sem("consts"), 1)

            def load_indices(stage, index, c, b, k):
                if some(f"{stage}_rows{b}", k * ROWS):
                    pool.wait_ge(sem(f"{stage}_rows{b}"), upto(f"{stage}_rows{b}", k * ROWS))
                pool.tensor_copy(idx_st[:, b, :], index[:, tc(c)]).then_inc(sem(f"{stage}_idx"), 1)
                pool.wait_ge(sem(f"{stage}_idx"), upto(f"{stage}_idx", c + 1))

            def gather(stage, table, bound, ring, b):
                for s in range(TPC):
                    pool.indirect_dma_start(
                        ring[:, b, s, :], None, table,
                        bass.IndirectOffsetOnAxis(ap=idx_st[:, b, s:s + 1], axis=0),
                        bounds_check=bound, oob_is_err=False).then_inc(sem(f"{stage}_rows{b}"), 16)

            def carry_waits():
                pool.tensor_tensor(token[:, 0:1], token[:, 1:2], token[:, 2:3], ALU.add)

            pool.wait_ge(sem("dstc_in"), 16)
            pool.wait_ge(sem("ring_clear"), 1)

            def p0(c, b, k):
                load_indices("p0", dstc, c, b, k)
                if some("p0_T", c - 1):
                    pool.wait_ge(sem("p0_T"), upto("p0_T", c - 1))
                carry_waits()
                gather("p0", x, last_node, XR, b)
            run_chunks(pool, p0)

            pool.wait_ge(sem("xmap_init"), 16 * CH)
            pool.wait_ge(sem("cells"), 1)
            pool.wait_ge(sem("index_in"), 64)

            def map_scatter(c, b, k):
                if some(f"map_st{b}", k * (16 * TPC)):
                    pool.wait_ge(sem(f"map_st{b}"), k * (16 * TPC))
                pool.tensor_copy(sidx_st[:, b, :], cellc[:, tc(c)]).then_inc(sem("map_idx"), 1)
                pool.tensor_copy(row_st[:, b, :], rowc[:, tc(c)]).then_inc(sem("map_idx"), 1)
                pool.wait_ge(sem("map_idx"), (c + 1) * 2)
                carry_waits()
                for s in range(TPC):
                    pool.indirect_dma_start(
                        xmap_cells, bass.IndirectOffsetOnAxis(ap=sidx_st[:, b, s:s + 1], axis=0),
                        row_st[:, b, s:s + 1], None,
                        bounds_check=last_cell, oob_is_err=False).then_inc(sem(f"map_st{b}"), 16)
            run_chunks(pool, map_scatter)
            pool.wait_ge(sem("map_st0"), 16 * TPC * (CH // 2 + 1))
            pool.wait_ge(sem("map_st1"), 16 * TPC * (CH // 2))

            pool.wait_ge(sem("p0_T"), upto("p0_T", CH))
            pool.wait_ge(sem("p0_rows0"), upto("p0_rows0", 16 * TPC * (CH // 2 + 1)))
            pool.wait_ge(sem("p0_rows1"), upto("p0_rows1", 16 * TPC * (CH // 2)))

            pool.wait_ge(sem("a_stored0"), 16 * (NB1 // 2 + 1))
            pool.wait_ge(sem("a_stored1"), 16 * (NB1 // 2))


            def l0(c, b, k):
                load_indices("l0", srcc, c, b, k)
                if some("l0_dense", c - 1):
                    pool.wait_ge(sem("l0_dense"), upto("l0_dense", c - 1))
                if some("l0_q", c - 1):
                    pool.wait_ge(sem("l0_q"), upto("l0_q", c - 1))
                carry_waits()
                gather("l0", xmap, last_node, XM, b)
            run_chunks(pool, l0)

            def layer_gather(stage, l, prev):
                pool.wait_ge(sem("l0_q"), upto("l0_q", CH))
                pool.wait_ge(sem(f"{prev}_rows0"), upto(f"{prev}_rows0", 16 * TPC * (CH // 2 + 1)))
                pool.wait_ge(sem(f"{prev}_rows1"), upto(f"{prev}_rows1", 16 * TPC * (CH // 2)))
                pool.wait_ge(sem(f"tab{l}_st0"), 16 * (CH // 2 + 1))
                pool.wait_ge(sem(f"tab{l}_st1"), 16 * (CH // 2))

            layer_gather("l1a", 1, "l0")

            def l1a(c, b, k):
                load_indices("l1a", qcol, c, b, k)
                pool.wait_ge(sem("l1a_copy"), upto("l1a_copy", c + 1))
                carry_waits()
                gather("l1a", dtab[0], last_row, XR, b)
            run_chunks(pool, l1a)
            layer_gather("l2", 2, "l1a")

            def l2(c, b, k):
                load_indices("l2", qcol, c, b, k)
                pool.wait_ge(sem("l2_copy"), upto("l2_copy", c + 1))
                carry_waits()
                gather("l2", dtab[1], last_row, XR, b)
            run_chunks(pool, l2)
            layer_gather("l3", 3, "l2")
            pool.wait_ge(sem("a_stored0"), 16 * (NB // 2))
            pool.wait_ge(sem("a_stored1"), 16 * (NB // 2))
            pool.wait_ge(sem("map_st0"), 16 * TPC * (CH // 2 + 1))

            def l3_front(c, b, k):
                load_indices("l3", qcol, c, b, k)
                pool.wait_ge(sem("l3_copy"), upto("l3_copy", c + 1))
                carry_waits()
                gather("l3", dtab[2], last_row, XR, b)

            def final_scatter(c, b, k):
                if some(f"final_st{b}", k * (16 * TPC)):
                    pool.wait_ge(sem(f"final_st{b}"), k * (16 * TPC))
                pool.tensor_copy(sidx_st[:, b, :], outc[:, tc(c)]).then_inc(sem("final_idx"), 1)
                pool.wait_ge(sem("final_idx"), c + 1)
                pool.wait_ge(sem("l3_D"), upto("l3_D", c + 1))
                carry_waits()
                for s in range(TPC):
                    pool.indirect_dma_start(
                        out[:, :], bass.IndirectOffsetOnAxis(ap=sidx_st[:, b, s:s + 1], axis=0),
                        dn[b][:, s * F:(s + 1) * F], None,
                        bounds_check=last_node, oob_is_err=False).then_inc(sem(f"final_st{b}"), 16)

            def l3(front, ahead, mid, back):
                if front:
                    l3_front(*front)
                if back:
                    final_scatter(*back)
            run_pipe(pool, l3, 4)

        @block.tensor
        def _(pe):
            pe.wait_ge(sem("weights_in"), 64)
            pe.wait_ge(sem("consts"), 6)
            pe.wait_ge(sem("eye_plus"), 2)
            fold = bank[6]
            pe.matmul(fold[:, 0:128], W("w_src"), W("w1aT"), start=True, stop=True)
            pe.matmul(fold[:, 128:256], W("w_tgt"), W("w1bT"), start=True, stop=True)
            pe.matmul(fold[:, 256:384], W("w_tgtI"), cen, start=True, stop=True)
            pe.matmul(fold[:, 384:512], W("res_wT"), cen, start=True, stop=True).then_inc(sem("fold"), 1)
            f2 = bank[7]
            pe.matmul(f2[:, 0:128], W("w_outT"), cen, start=True, stop=True)
            pe.matmul(f2[0:16, 128:256], W("w_edge", m=16), W("w1cT"), start=True, stop=True)
            pe.matmul(f2[:, 256:260], W("w_outT"), cols[:, COLS.index("attn1_0"):COLS.index("attn1_0") + 4],
                      start=True, stop=True)
            pe.matmul(f2[:, 260:261], W("w1aT"), col("b_src"), start=True, stop=False)
            pe.matmul(f2[:, 260:261], W("w1bT"), col("b_tgt"), start=False, stop=False)
            pe.matmul(f2[:, 260:261], W("w1cT"), col("b_edge"), start=False, stop=True)
            pe.matmul(f2[:, 261:262], W("app2"), col("msg_b"), start=True, stop=True)
            pe.matmul(f2[:, 262:263], W("attn_rep"), col("b_out"), start=True, stop=True).then_inc(sem("fold"), 1)
            f3 = bank[5]
            pe.matmul(f3[:, 0:128], col("b_tgt").broadcast_to([P, P]), cen, start=True, stop=True)
            pe.matmul(f3[:, 128:256], col("res_b").broadcast_to([P, P]), cen, start=True, stop=True)
            pe.matmul(f3[:, 256:384], col("b_out").broadcast_to([P, P]), cen, start=True, stop=True
                      ).then_inc(sem("fold"), 1)

            tls = [0]

            def two_level(loc, last, off, static=False):
                n = tls[0]
                tls[0] += 1
                pe.wait_ge(sem("tl_ends"), n + 1)
                row = bank[7][0:1, 0:TILES]
                for g in range(2):
                    mm = pe.matmul(bank[7][0:1, g * RP:(g + 1) * RP], loc[:, g, last:last + 1],
                                   eye[0:RP, 0:RP], start=True, stop=True)
                mm.then_inc(sem("tl_row"), 1)
                pe.wait_ge(sem("tl_carry"), n + 1)
                for g in range(2):
                    mm = pe.matmul(bank[7][0:RP, 256 + g:257 + g],
                                   rowbuf[0:1, 3, off + g * RP:off + (g + 1) * RP], one[:, :],
                                   start=True, stop=True)
                mm.then_inc(sem("tl_cin"), 1)

            def static_rows():
                pe.wait_ge(sem("ends_static"), 3)
                pe.wait_ge(sem("fold_used"), 7)
                for q in range(3):
                    if q:
                        if some("static_row", q):
                            pe.wait_ge(sem("static_row"), q)
                    for g in range(2):
                        mm = pe.matmul(bank[7][0:1, g * RP:(g + 1) * RP], ends[:, q, g:g + 1],
                                       eye[0:RP, 0:RP], start=True, stop=True)
                    mm.then_inc(sem("static_T"), 1)
                pe.wait_ge(sem("static_row"), 3)

            static_rows()
            two_level(rt(0), P - 1, 0)
            two_level(rt(2), 0, 2)

            def node_product(X, src, weight, bias, done):
                if bias is not None:
                    pe.matmul(X[:, :], ones_b[:, :], brow[:, bias, :], start=True, stop=True)
                for j in range(4):
                    mm = pe.matmul(X[:, j * P:(j + 1) * P], src[:, j * P:(j + 1) * P], weight,
                                   start=bias is None, stop=True, skip_group_check=True)
                mm.then_inc(sem(done), 1)

            def node_step(h, par, lo, hi):
                p0, p1, p2, p3 = node_phases(h, par, lo, hi)
                if p1:
                    i = p1[0]
                    pe.wait_ge(sem("a_x1"), i + 1)
                    if some("a_x1T", i):
                        pe.wait_ge(sem("a_x1T"), i)
                    for j in range(4):
                        mm = pe.transpose(bank[3][:, j * P:(j + 1) * P], node_x1[:, j * P:(j + 1) * P], eye)
                    mm.then_inc(sem("a_T1"), 1)
                if p2:
                    i, b, k = p2
                    pe.wait_ge(sem("a_x2"), i + 1)
                    if some("a_r", i):
                        pe.wait_ge(sem("a_r"), i)
                    for j in range(4):
                        mm = pe.transpose(bank[4][:, j * P:(j + 1) * P], node_x2[b][:, j * P:(j + 1) * P], eye)
                    mm.then_inc(sem("a_T2"), 1)
                if p3:
                    i = p3[0]
                    pe.wait_ge(sem("a_r"), i + 1)
                    if some("a_c2s", i):
                        pe.wait_ge(sem("a_c2s"), i)
                    node_product(bank[2], node_r, cen, None, "a_c2")
                if p0:
                    i, b, k = p0
                    pe.wait_ge(sem(f"a_in{b}"), (k + 1) * 16)
                    if some("a_x1", i):
                        pe.wait_ge(sem("a_x1"), i)
                    node_product(bank[0], node_in[b], M0, 0, "a_c0")
                if p2:
                    i = p2[0]
                    pe.wait_ge(sem("a_x2T"), i + 1)
                    pe.matmul(bank[4][:, :], W("app1"), node_x2T, start=True, stop=True).then_inc(sem("a_y"), 1)
                if p1:
                    i = p1[0]
                    pe.wait_ge(sem("a_x1T"), i + 1)
                    if some("a_x2", i):
                        pe.wait_ge(sem("a_x2"), i)
                    node_product(bank[1], node_x1T, M1, 1, "a_c1")

            pe.wait_ge(sem("fold_used"), 7)
            pe.wait_ge(sem("brow"), 3)

            def transpose_rows(stage, rows, dest):
                for j in range(4):
                    mm = pe.transpose(dest[:, j * P:(j + 1) * P],
                                      rows[:, 2 * j:2 * j + 2, :].rearrange("p s f -> p (s f)"), eye)
                mm.then_inc(sem(f"{stage}_T"), 1)

            def stage1(c, b, k):
                node_step(c, 0, 0, NB1)
                pe.wait_ge(sem(f"p0_rows{b}"), upto(f"p0_rows{b}", (k + 1) * ROWS))
                if some("p0_D", c - 1):
                    pe.wait_ge(sem("p0_D"), upto("p0_D", c - 1))
                transpose_rows("p0", XR[:, b, :, :], bank[5 + b])
                node_step(c, 1, 0, NB1)
            run_chunks(pe, stage1)
            run_nodes_alone(pe, node_step)

            def tile_product(dest, terms, bias, done):
                if bias is not None:
                    pe.matmul(dest[:, :], ones_b[:, :], brow[:, bias, :], start=True, stop=True)
                for j in range(4):
                    for t, (src, weight) in enumerate(terms):
                        mm = pe.matmul(dest[:, j * P:(j + 1) * P], src(j), weight,
                                       start=bias is None and t == 0, stop=True,
                                       skip_group_check=True)
                mm.then_inc(sem(done), 1)

            def fixed(t):
                return lambda j: t[:, j * P:(j + 1) * P]

            def transpose_dn(stage, c, b):
                pe.wait_ge(sem(f"{stage}_D"), upto(f"{stage}_D", c + 1))
                if some(f"{stage}_DT", c):
                    pe.wait_ge(sem(f"{stage}_DT"), upto(f"{stage}_DT", c))
                for j in range(4):
                    mm = pe.transpose(bank[2][:, j * P:(j + 1) * P], dn[b][:, j * P:(j + 1) * P], eye)
                mm.then_inc(sem(f"{stage}_T2"), 1)

            pe.wait_ge(sem("p0_D"), upto("p0_D", CH))
            pe.wait_ge(sem("a_c2s"), NB1)

            def l0(front, mid, back):
                if mid:
                    c, b, k = mid
                    pe.wait_ge(sem("l0_h1"), upto("l0_h1", c + 1))
                    if some("l0_z2b", c):
                        pe.wait_ge(sem("l0_z2b"), upto("l0_z2b", c))
                    pe.matmul(bank[6][0:64, :], W("w2T", m=64), h1, start=True, stop=True
                              ).then_inc(sem("l0_z2"), 1)
                if front:
                    c, b, k = front
                    pe.wait_ge(sem("l0_dense"), upto("l0_dense", c + 1))
                    if some("l0_xsT", c):
                        pe.wait_ge(sem("l0_xsT"), upto("l0_xsT", c))
                    transpose_rows("l0", XR[:, b, :, :], bank[4])
                if mid:
                    c, b, k = mid
                    if some("l0_msg", c):
                        pe.wait_ge(sem("l0_msg"), upto("l0_msg", c))
                    pe.matmul(bank[3][:, :], W("w_srcT"), xsT[b], start=True, stop=True
                              ).then_inc(sem("l0_xs"), 1)
                    pe.wait_ge(sem("l0_h2"), upto("l0_h2", c + 1))
                    if some("l0_eg", c):
                        pe.wait_ge(sem("l0_eg"), upto("l0_eg", c))
                    pe.matmul(bank[7][:, :], W("w3rep", k=64), h2[0:64, :], start=True, stop=True
                              ).then_inc(sem("l0_e"), 1)
                if front:
                    c, b, k = front
                    pe.wait_ge(sem(f"l0_attr{b}"), upto(f"l0_attr{b}", (k + 1) * 16))
                    pe.wait_ge(sem("l0_xsT"), upto("l0_xsT", c + 1))
                    if some("l0_z1b", c):
                        pe.wait_ge(sem("l0_z1b"), upto("l0_z1b", c))
                    pe.matmul(bank[5][:, :], B1, D[:, cs(c)], start=True, stop=False)
                    pe.matmul(bank[5][:, :], edge1[:, :], attr[:, b, :], start=False, stop=False)
                    pe.matmul(bank[5][:, :], A1, xsT[b], start=False, stop=True).then_inc(sem("l0_z1"), 1)
                if mid:
                    c, b, k = mid
                    if some("l0_S", c):
                        pe.wait_ge(sem("l0_S"), upto("l0_S", c))
                    tile_product(bank[1], [(fixed(xsT[b]), M0)], 0, "l0_cS")
                if back:
                    c, b, k = back
                    pe.wait_ge(sem(f"l0_stream{b}"), upto(f"l0_stream{b}", (k + 1) * 32))
                    pe.wait_ge(sem("l0_scan"), upto("l0_scan", c * 2 + 2))
                    if some("l0_D", c):
                        pe.wait_ge(sem("l0_D"), upto("l0_D", c))
                    tile_product(bank[0], [(fixed(dT[:, b, :]), M0), (fixed(agg), cen)], 0, "l0_cD")
                    transpose_dn("l0", c, b)
            run_pipe(pe, l0, 3)

            def l1a(c, b, k):
                pe.wait_ge(sem(f"l1a_rows{b}"), upto(f"l1a_rows{b}", (k + 1) * ROWS))
                if some("l1a_ST", c):
                    pe.wait_ge(sem("l1a_ST"), upto("l1a_ST", c))
                transpose_rows("l1a", XR[:, b, :, :], bank[5])
                nodes_beside(pe, node_step, c, b, k)
                pe.wait_ge(sem("l1a_ST"), upto("l1a_ST", c + 1))
                if some("l1a_sc", c):
                    pe.wait_ge(sem("l1a_sc"), upto("l1a_sc", c))
                pe.wait_ge(sem(f"l1a_stream{b}"), upto(f"l1a_stream{b}", (k + 1) * 16))
                for j in range(4):
                    pe.matmul(bank[6][:, 2 * j:2 * j + 2], xsT[b][:, j * P:(j + 1) * P], attn_w[:, 0:2],
                              start=True, stop=True)
                for j in range(4):
                    mm = pe.matmul(bank[6][:, 8 + 2 * j:10 + 2 * j], dT[:, b, j * P:(j + 1) * P],
                                   attn_w[:, 2:4], start=True, stop=True)
                mm.then_inc(sem("l1a_s"), 1)
            pe.wait_ge(sem("l0_DT"), upto("l0_DT", CH))
            run_chunks(pe, l1a)
            for i in range(NB, NB + 3):
                node_step(i // 2, i % 2, NB1, NB)

            pe.wait_ge(sem("l1_perm"), 2)
            pe.wait_ge(sem("l1a_ST"), upto("l1a_ST", CH))
            for q in range(2):
                for g in range(2):
                    mm = pe.transpose(bank[6][0:RP, (2 * q + g) * P:(2 * q + g + 1) * P],
                                      EB[:, 4 + q, g * RP:(g + 1) * RP], eye)
            mm.then_inc(sem("l1_run"), 1)
            two_level(rt(2), 0, 2)
            two_level(rt(0), P - 1, 0)
            two_level(rt(2), 0, 2)
            two_level(rt(0), P - 1, 0)
            two_level(rt(2), 0, 2)

            pe.wait_ge(sem("a_c2s"), NB)

            def l1b(front, back):
                if back:
                    c, b, k = back
                    pe.wait_ge(sem("l1b_scan"), upto("l1b_scan", c * 2 + 2))
                    if some("l1b_D", c):
                        pe.wait_ge(sem("l1b_D"), upto("l1b_D", c))
                    tile_product(bank[0], [(fixed(dT[:, b, :]), M1), (fixed(agg), WOC)], 2, "l1b_cD")
                if front:
                    c, b, k = front
                    pe.wait_ge(sem(f"l1b_stream{b}"), upto(f"l1b_stream{b}", (k + 1) * 64))
                    if some("l1b_S", c):
                        pe.wait_ge(sem("l1b_S"), upto("l1b_S", c))
                    tile_product(bank[1], [(fixed(xsT[b]), M1)], 1, "l1b_cS")
                if back:
                    transpose_dn("l1b", *back[:2])
            run_pipe(pe, l1b, 2)
            pe.wait_ge(sem("l1b_DT"), upto("l1b_DT", CH))

            def l2(front, mid, back):
                if back:
                    c, b, k = back
                    pe.wait_ge(sem(f"l2_dT{b}"), upto(f"l2_dT{b}", (k + 1) * 16))
                    pe.wait_ge(sem("l2_rD"), upto("l2_rD", c + 1))
                    if some("l2_D", c):
                        pe.wait_ge(sem("l2_D"), upto("l2_D", c))
                    tile_product(bank[0], [(fixed(dT[:, b, :]), cen), (fixed(rD), cen)], None, "l2_cD")
                if front:
                    c, b, k = front
                    pe.wait_ge(sem(f"l2_rows{b}"), upto(f"l2_rows{b}", (k + 1) * ROWS))
                    if some("l2_xsT", c):
                        pe.wait_ge(sem("l2_xsT"), upto("l2_xsT", c))
                    transpose_rows("l2", XR[:, b, :, :], bank[4])
                if mid:
                    c, b, k = mid
                    pe.wait_ge(sem("l2_scan"), upto("l2_scan", c * 2 + 2))
                    if some("l2_rD", c):
                        pe.wait_ge(sem("l2_rD"), upto("l2_rD", c))
                    pe.matmul(bank[7][:, :], W("app1"), D[:, cs(c)], start=True, stop=False)
                    pe.matmul(bank[7][:, :], W("app2"), agg, start=False, stop=True).then_inc(sem("l2_yD"), 1)
                if front:
                    c, b, k = front
                    pe.wait_ge(sem("l2_xsT"), upto("l2_xsT", c + 1))
                    if some("l2_rS", c):
                        pe.wait_ge(sem("l2_rS"), upto("l2_rS", c))
                    pe.matmul(bank[6][:, :], W("app1"), xsT[b], start=True, stop=True).then_inc(sem("l2_yS"), 1)
                    pe.wait_ge(sem(f"l2_stream{b}"), upto(f"l2_stream{b}", (k + 1) * 32))
                    if some("l2_msg", c):
                        pe.wait_ge(sem("l2_msg"), upto("l2_msg", c))
                    pe.matmul(bank[5][:, :], W("msg1"), xsT[b], start=True, stop=False)
                    pe.matmul(bank[5][:, :], W("msg2", k=64), stream2[b][0:F, :], start=False, stop=True
                              ).then_inc(sem("l2_m"), 1)
                    pe.wait_ge(sem("l2_rS"), upto("l2_rS", c + 1))
                    if some("l2_addS", c):
                        pe.wait_ge(sem("l2_addS"), upto("l2_addS", c))
                    tile_product(bank[1], [(fixed(rS), cen)], None, "l2_cS")
            run_pipe(pe, l2, 3)

            pe.wait_ge(sem("l2_D"), upto("l2_D", CH))

            def l3(front, mid, back, scattered):
                if mid:
                    c, b, k = mid
                    if some("l3_scan", (c - 1) * 2):
                        pe.wait_ge(sem("l3_scan"), upto("l3_scan", (c - 1) * 2))
                    for q in range(REL // 2):
                        pe.wait_ge(sem("l3_mask"), upto("l3_mask", c * REL + (2 * q + 2)))
                        for h in range(2):
                            mm = pe.matmul(bank[6 + b][h * F:(h + 1) * F, :], relw[:, q, :],
                                           NT[:, 4 * h + q % 4, :], start=q == 0, stop=q == REL // 2 - 1)
                        mm.then_inc(sem("l3_pair"), 1)
                        if q == 3 and back:
                            pe.wait_ge(sem("l3_rD"), upto("l3_rD", back[0] + 1))
                            if some("l3_addD", back[0]):
                                pe.wait_ge(sem("l3_addD"), upto("l3_addD", back[0]))
                            tile_product(bank[0], [(fixed(rD), cen)], None, "l3_cD")
                        if q == 5 and front:
                            l3_turn(*front)
                else:
                    if back:
                        pe.wait_ge(sem("l3_rD"), upto("l3_rD", back[0] + 1))
                        if some("l3_addD", back[0]):
                            pe.wait_ge(sem("l3_addD"), upto("l3_addD", back[0]))
                        tile_product(bank[0], [(fixed(rD), cen)], None, "l3_cD")
                    if front:
                        l3_turn(*front)

            def l3_turn(c, b, k):
                pe.wait_ge(sem("l3_xw"), upto("l3_xw", c + 1))
                if some("l3_xAB", c * 2):
                    pe.wait_ge(sem("l3_xAB"), upto("l3_xAB", c * 2))
                for h in range(2):
                    for j in range(4):
                        mm = pe.transpose(bank[4 + h][:, j * P:(j + 1) * P],
                                          xw2[:, (2 * j + h) * P:(2 * j + h + 1) * P], eye)
                    mm.then_inc(sem("l3_T"), 1)
            run_pipe(pe, l3, 4)

        @block.scalar
        def _(act):
            act.wait_ge(sem("consts"), 6)

            def deviation(dest, ss, final, p=P):
                scale = (1.0 + EPS) / F if final else 1.0 / F
                return act.activation(dest, ss, ACT.Sqrt, bias=epsc[:, 1:2] if final else epsc[:, 0:1],
                                      scale=scale)

            def node_square(p, layer):
                i, b, k = p
                act.wait_ge(sem(("a_c0", "a_c1", "a_c2s")[layer]), upto(("a_c0", "a_c1", "a_c2s")[layer], i + 1))
                if some(f"a_ss{layer}", i):
                    act.wait_ge(sem(f"a_ss{layer}"), i)
                act.activation(node_sq[layer], node_out[b] if layer == 2 else bank[layer][:, :], ACT.Square
                               ).then_inc(sem(f"a_sq{layer}"), 1)

            def node_deviation(p, layer):
                act.wait_ge(sem(f"a_ss{layer}"), p[0] + 1)
                if some(f"a_rs{layer}", p[0]):
                    act.wait_ge(sem(f"a_rs{layer}"), p[0])
                deviation(asmall[:, layer, 1, :], asmall[:, layer, 0, :], layer == 2
                          ).then_inc(sem(f"a_sd{layer}"), 1)

            def node_step(h, par, lo, hi):
                p0, p1, p2, p3 = node_phases(h, par, lo, hi)
                if p1:
                    act.wait_ge(sem("a_T1"), p1[0] + 1)
                    if some("a_c1", p1[0]):
                        act.wait_ge(sem("a_c1"), p1[0])
                    act.activation(node_x1T, bank[3][:, :], ACT.Copy).then_inc(sem("a_x1T"), 1)
                if p2:
                    act.wait_ge(sem("a_T2"), p2[0] + 1)
                    if some("a_y", p2[0]):
                        act.wait_ge(sem("a_y"), p2[0])
                    act.activation(node_x2T, bank[4][:, :], ACT.Copy).then_inc(sem("a_x2T"), 1)
                if p3:
                    node_square(p3, 2)
                if p0:
                    node_square(p0, 0)
                if p3:
                    node_deviation(p3, 2)
                if p2:
                    act.wait_ge(sem("a_y"), p2[0] + 1)
                    if some("a_c2", p2[0]):
                        act.wait_ge(sem("a_c2"), p2[0])
                    act.activation(node_r, bank[4][:, :], ACT.Relu, bias=col("app_b")).then_inc(sem("a_r"), 1)
                if p0:
                    node_deviation(p0, 0)
                if p1:
                    node_square(p1, 1)
                    node_deviation(p1, 1)

            act.wait_ge(sem("weights_in"), 64)

            def stage1(c, b, k):
                node_step(c, 0, 0, NB1)
                act.wait_ge(sem("p0_T"), upto("p0_T", c + 1))
                act.activation(D[:, cs(c)], bank[5 + b][:, :], ACT.Copy).then_inc(sem("p0_D"), 1)
                node_step(c, 1, 0, NB1)
            run_chunks(act, stage1)
            run_nodes_alone(act, node_step)

            def run_ahead(body, depth):
                def step(t):
                    body(*((t - p, (t - p) % 2, (t - p) // 2) if 0 <= t - p < CH else None for p in range(depth)))
                peeled = 2 * depth - 1
                for t in range(peeled):
                    step(t)
                with act.Fori(peeled // 2, CH // 2 - 1) as i:
                    for t in (1, 2):
                        body(*((i * 2 + (t - p), (t - p) % 2, i + (t - p) // 2) for p in range(depth)))
                for t in range(CH - 2, CH + depth - 1):
                    step(t)

            def ln_square(stage, who, src, dest, after, c):
                act.wait_ge(sem(after), upto(after, c + 1))
                if some(f"{stage}_ss{who}", c):
                    act.wait_ge(sem(f"{stage}_ss{who}"), upto(f"{stage}_ss{who}", c))
                act.activation(dest, src, ACT.Square).then_inc(sem(f"{stage}_sq{who}"), 1)

            def ln_dev(stage, who, c):
                act.wait_ge(sem(f"{stage}_ss{who}"), upto(f"{stage}_ss{who}", c + 1))
                if some(f"{stage}_rs{who}", c):
                    act.wait_ge(sem(f"{stage}_rs{who}"), upto(f"{stage}_rs{who}", c))
                i = "DS".index(who)
                deviation(small[:, i, 1, :], small[:, i, 0, :], False).then_inc(sem(f"{stage}_sd{who}"), 1)

            def store_tab(l, stage, c, b, k):
                act.wait_ge(sem(f"{stage}_D"), upto(f"{stage}_D", c + 1))
                act.dma_start(dtab[l - 1][bass.ds(c * 1024, 1024), :].rearrange("(p s) f -> p (s f)", p=P),
                              dn[b]).then_inc(sem(f"tab{l}_st{b}"), 16)

            def turn_D(stage, c):
                act.wait_ge(sem(f"{stage}_T2"), upto(f"{stage}_T2", c + 1))
                act.activation(D[:, cs(c)], bank[2][:, :], ACT.Copy).then_inc(sem(f"{stage}_DT"), 1)

            def densify(c, b, k):
                act.wait_ge(sem(f"l0_rows{b}"), upto(f"l0_rows{b}", (k + 1) * ROWS))
                if some("l0_T", c - 1):
                    act.wait_ge(sem("l0_T"), upto("l0_T", c - 1))
                act.activation(XR[:, b, :, :], XM[:, b, :, 0:F], ACT.Copy).then_inc(sem("l0_dense"), 1)

            def l0(front, mid, back):
                if front and isinstance(front[0], int) and front[0] == 0:
                    densify(*front)
                if mid:
                    c, b, k = mid
                    act.wait_ge(sem("l0_z2"), upto("l0_z2", c + 1))
                    if some("l0_h2", c):
                        act.wait_ge(sem("l0_h2"), upto("l0_h2", c))
                    act.activation(z2[0:64, :], bank[6][0:64, :], ACT.Identity, bias=col("b2", 64)
                                   ).then_inc(sem("l0_z2b"), 1)
                if front:
                    c, b, k = front
                    act.wait_ge(sem("l0_T"), upto("l0_T", c + 1))
                    if some("l0_cS", c - 1):
                        act.wait_ge(sem("l0_cS"), upto("l0_cS", c - 1))
                    act.activation(xsT[b], bank[4][:, :], ACT.Copy).then_inc(sem("l0_xsT"), 1)
                if mid:
                    c, b, k = mid
                    act.wait_ge(sem("l0_e"), upto("l0_e", c + 1))
                    act.activation(eg, bank[7][:, :], ACT.Relu, bias=col("b3")).then_inc(sem("l0_eg"), 1)
                if front:
                    c, b, k = front
                    act.wait_ge(sem("l0_z1"), upto("l0_z1", c + 1))
                    if some("l0_h1", c):
                        act.wait_ge(sem("l0_h1"), upto("l0_h1", c))
                    act.activation(z1, bank[5][:, :], ACT.Identity, bias=fcol[:, 0:1]).then_inc(sem("l0_z1b"), 1)
                if mid:
                    ln_square("l0", "S", bank[1][:, :], sqS, "l0_cS", mid[0])
                if front and not last(front[0]):
                    c, b, k = front
                    densify(c + 1, 1 - b, k + b)
                if mid:
                    ln_dev("l0", "S", mid[0])
                if back:
                    c, b, k = back
                    ln_square("l0", "D", bank[0][:, :], sqD, "l0_cD", c)
                    ln_dev("l0", "D", c)
                    store_tab(1, "l0", c, b, k)
                    turn_D("l0", c)

            def last(c):
                return isinstance(c, int) and c == CH - 1
            act.wait_ge(sem("fold_used"), 7)
            run_ahead(l0, 3)

            def copy_ring(stage, c, b):
                act.activation(XR[:, b, :, :], rows64(S[:, cs(c)]), ACT.Copy).then_inc(sem(f"{stage}_copy"), 1)

            def l1a(c, b, k):
                if not last(c):
                    if some("l1a_T", c):
                        act.wait_ge(sem("l1a_T"), upto("l1a_T", c))
                    copy_ring("l1a", c + 1, 1 - b)
                act.wait_ge(sem("l1a_T"), upto("l1a_T", c + 1))
                if some(f"l1a_stored{b}", k * 16):
                    act.wait_ge(sem(f"l1a_stored{b}"), upto(f"l1a_stored{b}", k * 16))
                if some("l1a_s", c - 1):
                    act.wait_ge(sem("l1a_s"), upto("l1a_s", c - 1))
                act.activation(xsT[b], bank[5][:, :], ACT.Copy).then_inc(sem("l1a_ST"), 1)
                nodes_beside(act, node_step, c, b, k)

            act.wait_ge(sem("l0_T"), upto("l0_T", CH))
            act.wait_ge(sem("l0_q"), upto("l0_q", CH))
            act.wait_ge(sem("l0_S"), upto("l0_S", CH))
            copy_ring("l1a", 0, 0)
            run_chunks(act, l1a, tail=2)
            for i in range(NB, NB + 3):
                node_step(i // 2, i % 2, NB1, NB)

            act.wait_ge(sem("l1_dve"), 1)
            act.activation(rt(3), rt(3), ACT.Gelu, bias=fcol[0:RP, 2:3]).then_inc(sem("l1_act"), 1)
            act.wait_ge(sem("l1_dve"), 2)
            act.activation(rt(3), rt(3), ACT.Exp).then_inc(sem("l1_act"), 1)

            def l1b(front, back):
                if back:
                    ln_square("l1b", "D", bank[0][:, :], sqD, "l1b_cD", back[0])
                if front:
                    ln_square("l1b", "S", bank[1][:, :], sqS, "l1b_cS", front[0])
                if back:
                    ln_dev("l1b", "D", back[0])
                if front:
                    ln_dev("l1b", "S", front[0])
                if back:
                    store_tab(2, "l1b", *back)
                    turn_D("l1b", back[0])
            run_pipe(act, l1b, 2)

            def l2(front, mid, back):
                if front and not last(front[0]):
                    c, b, k = front
                    if some("l2_T", c):
                        act.wait_ge(sem("l2_T"), upto("l2_T", c))
                    if some("l2_addS", c):
                        act.wait_ge(sem("l2_addS"), upto("l2_addS", c))
                    copy_ring("l2", c + 1, 1 - b)
                if mid:
                    ln_square("l2", "S", cadd, sqS, "l2_addS", mid[0])
                if back:
                    ln_square("l2", "D", bank[0][:, :], sqD, "l2_cD", back[0])
                if front:
                    c, b, k = front
                    act.wait_ge(sem("l2_T"), upto("l2_T", c + 1))
                    if some("l2_cS", c - 1):
                        act.wait_ge(sem("l2_cS"), upto("l2_cS", c - 1))
                    if some("l2_m", c - 1):
                        act.wait_ge(sem("l2_m"), upto("l2_m", c - 1))
                    act.activation(xsT[b], bank[4][:, :], ACT.Copy).then_inc(sem("l2_xsT"), 1)
                if mid:
                    ln_dev("l2", "S", mid[0])
                    act.wait_ge(sem("l2_yD"), upto("l2_yD", mid[0] + 1))
                    if some("l2_cD", mid[0]):
                        act.wait_ge(sem("l2_cD"), upto("l2_cD", mid[0]))
                    act.activation(rD, bank[7][:, :], ACT.Relu, bias=fcol[:, 1:2]).then_inc(sem("l2_rD"), 1)
                if front:
                    c, b, k = front
                    act.wait_ge(sem("l2_yS"), upto("l2_yS", c + 1))
                    if some("l2_cS", c):
                        act.wait_ge(sem("l2_cS"), upto("l2_cS", c))
                    act.activation(rS, bank[6][:, :], ACT.Relu, bias=col("app_b")).then_inc(sem("l2_rS"), 1)
                if back:
                    c, b, k = back
                    ln_dev("l2", "D", c)
                    store_tab(3, "l2", c, b, k)
                    act.wait_ge(sem(f"l2_dT{b}"), upto(f"l2_dT{b}", (k + 1) * 16))
                    act.activation(D[:, cs(c)], dn[b], ACT.Copy).then_inc(sem("l2_keepD"), 1)
            act.wait_ge(sem("l1b_S"), upto("l1b_S", CH))
            copy_ring("l2", 0, 0)
            run_ahead(l2, 3)

            def l3(front, mid, back, scattered):
                if front and not last(front[0]):
                    c, b, k = front
                    if some("l3_xw", c):
                        act.wait_ge(sem("l3_xw"), upto("l3_xw", c))
                    copy_ring("l3", c + 1, 1 - b)
                if back:
                    c, b, k = back
                    act.wait_ge(sem("l3_scan"), upto("l3_scan", c * 2 + 2))
                    if some("l3_cD", c):
                        act.wait_ge(sem("l3_cD"), upto("l3_cD", c))
                    act.activation(rD, agg, ACT.Relu).then_inc(sem("l3_rD"), 1)
                    ln_square("l3", "D", eg, sqD, "l3_addD", c)
                    ln_dev("l3", "D", c)
                if front:
                    c, b, k = front
                    for h in range(2):
                        act.wait_ge(sem("l3_T"), upto("l3_T", c * 2 + (h + 1)))
                        if some("l3_mask", c * REL):
                            act.wait_ge(sem("l3_mask"), upto("l3_mask", c * REL))
                        act.activation((z1, h1)[h], bank[4 + h][:, :], ACT.Copy).then_inc(sem("l3_xAB"), 1)
            act.wait_ge(sem("l2_S"), upto("l2_S", CH))
            act.wait_ge(sem("l2_T"), upto("l2_T", CH))
            copy_ring("l3", 0, 0)
            run_ahead(l3, 4)

        @block.vector
        def _(dve):
            dve.wait_ge(sem("weights_in"), 64)
            dve.tensor_tensor(W("w_tgtI"), W("w_tgt"), eye, ALU.add).then_inc(sem("eye_plus"), 1)
            dve.tensor_tensor(W("res_wT"), W("res_wT"), eye, ALU.add).then_inc(sem("eye_plus"), 1)
            fl = [sqD[:, 0:TILES], sqS[:, 0:TILES], dn[0][:, 0:TILES]]
            dve.wait_ge(sem("dstc_in"), 16)
            dve.wait_ge(sem("index_in"), 64)
            dve.tensor_tensor(fl[0], dstc[:, :], nxtc[:, :], ALU.is_equal).then_inc(sem("nm_flags"), 1)
            dve.wait_ge(sem("nm_flags"), 1)
            dve.scalar_tensor_tensor(fl[1], fl[0], float(NO_ROW), dstc[:, :], ALU.mult, ALU.add
                                     ).then_inc(sem("nm_flags"), 1)
            dve.wait_ge(sem("nm_flags"), 2)
            dve.tensor_copy(outc[:, :], fl[1]).then_inc(sem("nm_flags"), 1)
            dve.tensor_scalar(fl[2], dstc[:, :], float(F + 1), float(F), ALU.mult, ALU.add
                              ).then_inc(sem("nm_flags"), 1)
            dve.wait_ge(sem("nm_flags"), 4)
            dve.scalar_tensor_tensor(fl[2], fl[0], float(8 * NO_ROW), fl[2], ALU.mult, ALU.add
                                     ).then_inc(sem("nm_flags"), 1)
            dve.wait_ge(sem("nm_flags"), 5)
            dve.tensor_copy(cellc[:, :], fl[2]).then_inc(sem("cells"), 1)
            dve.wait_ge(sem("runs_in"), 48)
            keep, cont, rep, pen = (runs[:, i, :, :] for i in range(4))
            dve.tensor_tensor(keep, rt(1).bitcast(I32), rt(0).bitcast(I32), ALU.is_equal).then_inc(sem("keep_run"), 1)
            dve.tensor_tensor(cont, rt(1).bitcast(I32), rt(2).bitcast(I32), ALU.is_equal).then_inc(sem("flags"), 1)
            dve.wait_ge(sem("keep_run"), 1)
            dve.wait_ge(sem("flags"), 1)
            dve.tensor_scalar(rep, cont, -1.0, 1.0, ALU.mult, ALU.add).then_inc(sem("flags"), 1)
            dve.tensor_scalar(pen, keep, -NEG, NEG, ALU.mult, ALU.add).then_inc(sem("flags"), 1)
            dve.wait_ge(sem("flags"), 3)
            for q, a in enumerate((keep, cont, pen)):
                dve.tensor_reduce(ends[:, q, :], a, AX.X, ALU.min).then_inc(sem("ends_static"), 1)
            dve.wait_ge(sem("fold"), 3)
            dve.tensor_copy(folded[:, 0:4, :], bank[6][:, :].rearrange("p (n m) -> p n m", n=4)
                            ).then_inc(sem("fold_used"), 1)
            dve.tensor_copy(WOC, bank[7][:, 0:128]).then_inc(sem("fold_used"), 1)
            dve.tensor_copy(edge1[:, :], bank[7][0:16, 128:256]).then_inc(sem("fold_used"), 1)
            dve.tensor_copy(attn_w[:, :], bank[7][:, 256:260]).then_inc(sem("fold_used"), 1)
            dve.tensor_tensor(fcol[:, 0:1], bank[7][:, 260:261], col("b1"), ALU.add).then_inc(sem("fold_used"), 1)
            dve.tensor_tensor(fcol[:, 1:2], bank[7][:, 261:262], col("app_b"), ALU.add).then_inc(sem("fold_used"), 1)
            dve.tensor_copy(fcol[:, 2:3], bank[7][:, 262:263]).then_inc(sem("fold_used"), 1)
            full = msg[:, 0:3 * P].rearrange("p (n m) -> p n m", n=3)
            dve.wait_ge(sem("consts"), 6)
            dve.tensor_copy(full, bank[5][:, 0:3 * P].rearrange("p (n m) -> p n m", n=3)).then_inc(sem("bias_rows"), 1)
            dve.wait_ge(sem("bias_rows"), 1)
            dve.tensor_tensor(full[:, 2, :], full[:, 2, :], full[:, 1, :], ALU.add).then_inc(sem("bias_rows"), 1)
            for part in range(3):
                r0 = 32 * part
                dve.wait_ge(sem("bias_rows"), 2 + 2 * part)
                for rr in range(4):
                    dv = dve.tensor_copy(brow[r0:r0 + 1, :, rr * P:(rr + 1) * P], full[r0:r0 + 1, :, :])
                dv.then_inc(sem("brow"), 1)
                if part < 2:
                    dve.tensor_copy(parts_b := h2[:, 0:192].bitcast(BF16).rearrange("p (n m) -> p n m", n=3), full
                                    ).then_inc(sem("bias_rows"), 1)
                    dve.wait_ge(sem("bias_rows"), 3 + 2 * part)
                    dve.wait_ge(sem("brow"), part + 1)
                    dve.tensor_tensor(full, full, parts_b, ALU.subtract).then_inc(sem("bias_rows"), 1)

            for q in range(3):
                dve.wait_ge(sem("static_T"), q + 1)
                dve.tensor_copy(rowbuf[0:1, q, 0:TILES], bank[7][0:1, 0:TILES]).then_inc(sem("static_row"), 1)
            dve.wait_ge(sem("static_row"), 3)

            tls = [0]

            def two_level(a, d0, d1, op0, op1, start, coef, reverse):
                n = tls[0]
                tls[0] += 1

                def way(t):
                    return t[:, ::-1] if reverse else t[:, :]
                if n:
                    if some("tl_done", 2 * n):
                        dve.wait_ge(sem("tl_done"), 2 * n)
                dve.tensor_tensor_scan(way(a[:, 0, :]), way(d0[:, 0, :]), way(d1[:, 0, :]), start, op0, op1
                                       ).then_inc(sem("tl_loc"), 1)
                dve.tensor_tensor_scan(way(a[:, 1, :]), way(d0[:, 1, :]), way(d1[:, 1, :]), start, op0, op1
                                       ).then_inc(sem("tl_ends"), 1)
                dve.memset(rowbuf[0:1, 3, :], start).then_inc(sem("tl_init"), 1)
                dve.wait_ge(sem("tl_init"), n + 1)
                dve.wait_ge(sem("tl_row"), n + 1)
                dve.tensor_tensor_scan(way(rowbuf[0:1, 3, 1:TILES + 1]), way(rowbuf[0:1, coef, 0:TILES]),
                                       way(bank[7][0:1, 0:TILES]), start, op0, op1).then_inc(sem("tl_carry"), 1)
                dve.wait_ge(sem("tl_cin"), n + 1)
                dve.tensor_copy(ends[:, 3, :], bank[7][0:RP, 256:258]).then_inc(sem("tl_cin_sb"), 1)
                dve.wait_ge(sem("tl_cin_sb"), n + 1)
                for g in range(2):
                    dve.tensor_tensor_scan(way(a[:, g, :]), way(d0[:, g, :]), way(d1[:, g, :]),
                                           ends[:, 3, g:g + 1], op0, op1).then_inc(sem("tl_done"), 1)
                dve.wait_ge(sem("tl_done"), 2 * n + 2)

            lasts = [0]

            def last_to_run(dest, src, tmp):
                lasts[0] += 1
                dve.tensor_tensor(tmp, src, rep, ALU.mult).then_inc(sem("rep_only"), 1)
                if some("rep_only", lasts[0]):
                    dve.wait_ge(sem("rep_only"), lasts[0])
                two_level(dest, cont, tmp, ALU.mult, ALU.add, 0.0, 1, True)

            dve.memset(rt(1), 1.0).then_inc(sem("unit"), 1)
            dve.wait_ge(sem("unit"), 1)
            two_level(rt(0), keep, rt(1), ALU.mult, ALU.add, 0.0, 0, False)
            last_to_run(rt(2), rt(0), rt(1))
            dve.reciprocal(rt(3), rt(2)).then_inc(sem("inv_run"), 1)

            def ln_apply(dest, src, rs):
                return dve.tensor_tensor(rows64(dest), rows64(src), bcast8(rs), ALU.mult)

            def node_sum(p, layer):
                dve.wait_ge(sem(f"a_sq{layer}"), p[0] + 1)
                dve.tensor_reduce(asmall[:, layer, 0, :], rows64(node_sq[layer]), AX.X, ALU.add
                                  ).then_inc(sem(f"a_ss{layer}"), 1)

            def node_inverse(p, layer):
                dve.wait_ge(sem(f"a_sd{layer}"), p[0] + 1)
                dve.reciprocal(asmall[:, layer, 2, :], asmall[:, layer, 1, :]).then_inc(sem(f"a_rs{layer}"), 1)
                dve.wait_ge(sem(f"a_rs{layer}"), p[0] + 1)

            def node_step(h, par, lo, hi):
                p0, p1, p2, p3 = node_phases(h, par, lo, hi)
                if p3:
                    i, b, k = p3
                    dve.wait_ge(sem("a_c2"), i + 1)
                    if some(f"a_stored{b}", k * 16):
                        dve.wait_ge(sem(f"a_stored{b}"), k * 16)
                    dve.tensor_tensor(node_out[b], bank[2][:, :], node_x2[b], ALU.add).then_inc(sem("a_c2s"), 1)
                if p0:
                    node_sum(p0, 0)
                if p3:
                    node_sum(p3, 2)
                if p0:
                    node_inverse(p0, 0)
                    if some("a_T1", p0[0]):
                        dve.wait_ge(sem("a_T1"), p0[0])
                    ln_apply(node_x1, bank[0][:, :], asmall[:, 0, 2, :]).then_inc(sem("a_x1"), 1)
                if p3:
                    node_inverse(p3, 2)
                    ln_apply(node_out[p3[1]], node_out[p3[1]], asmall[:, 2, 2, :]).then_inc(sem("a_out"), 1)
                if p1:
                    i, b, k = p1
                    node_sum(p1, 1)
                    node_inverse(p1, 1)
                    if some("a_T2", i - 1):
                        dve.wait_ge(sem("a_T2"), i - 1)
                    ln_apply(node_x2[b], bank[1][:, :], asmall[:, 1, 2, :]).then_inc(sem("a_x2"), 1)

            def stage1(c, b, k):
                node_step(c, 0, 0, NB1)
                node_step(c, 1, 0, NB1)
            run_chunks(dve, stage1)
            run_nodes_alone(dve, node_step)

            def ln_reduce(stage, who, src, c):
                i = "DS".index(who)
                dve.wait_ge(sem(f"{stage}_sq{who}"), upto(f"{stage}_sq{who}", c + 1))
                dve.tensor_reduce(small[:, i, 0, :], rows64(src), AX.X, ALU.add).then_inc(sem(f"{stage}_ss{who}"), 1)

            def ln_inverse(stage, who, c):
                i = "DS".index(who)
                dve.wait_ge(sem(f"{stage}_sd{who}"), upto(f"{stage}_sd{who}", c + 1))
                dve.reciprocal(small[:, i, 2, :], small[:, i, 1, :]).then_inc(sem(f"{stage}_rs{who}"), 1)
                dve.wait_ge(sem(f"{stage}_rs{who}"), upto(f"{stage}_rs{who}", c + 1))

            def scan_half(stage, c, b, data, h):
                a, z, o = h * F, (h + 1) * F, (1 - h) * F
                dve.wait_ge(sem(f"{stage}_carry"), upto(f"{stage}_carry", c * 2 + h))
                dve.tensor_tensor_scan(agg[a:z, :], stream[a:z, 0, b, :], data[a:z, :],
                                       carry[a:z, :], ALU.mult, ALU.add).then_inc(sem(f"{stage}_scan"), 1)
                dve.wait_ge(sem(f"{stage}_scan"), upto(f"{stage}_scan", c * 2 + (h + 1)))
                dve.tensor_copy(carry[o:o + F, :], agg[a:z, CW - 1:CW]).then_inc(sem(f"{stage}_carry"), 1)

            def l0(front, mid, back):
                if front:
                    c, b, k = front
                    dve.wait_ge(sem(f"l0_rows{b}"), upto(f"l0_rows{b}", (k + 1) * ROWS))
                    dve.tensor_copy(qcol[:, tc(c)].rearrange("p (s o) -> p s o", o=1), XM[:, b, :, F:F + 1]
                                    ).then_inc(sem("l0_q"), 1)
                if back:
                    c, b, k = back
                    dve.wait_ge(sem("l0_msg"), upto("l0_msg", c + 1))
                    dve.wait_ge(sem(f"l0_stream{b}"), upto(f"l0_stream{b}", (k + 1) * 32))
                    if some("l0_cD", c):
                        dve.wait_ge(sem("l0_cD"), upto("l0_cD", c))
                    scan_half("l0", c, b, msg, 0)
                if mid:
                    c, b, k = mid
                    dve.wait_ge(sem("l0_z2b"), upto("l0_z2b", c + 1))
                    dve.scalar_tensor_tensor(h2[0:64, :], z2[0:64, :], SLOPE, z2[0:64, :], ALU.mult, ALU.max
                                             ).then_inc(sem("l0_h2"), 1)
                if back:
                    scan_half("l0", back[0], back[1], msg, 1)
                if mid:
                    c, b, k = mid
                    dve.wait_ge(sem("l0_eg"), upto("l0_eg", c + 1))
                    dve.wait_ge(sem("l0_xs"), upto("l0_xs", c + 1))
                    dve.scalar_tensor_tensor(msg, bank[3][:, :], col("b_src"), eg, ALU.add, ALU.mult
                                             ).then_inc(sem("l0_msg"), 1)
                if front:
                    c, b, k = front
                    dve.wait_ge(sem("l0_z1b"), upto("l0_z1b", c + 1))
                    if some("l0_z2", c):
                        dve.wait_ge(sem("l0_z2"), upto("l0_z2", c))
                    dve.scalar_tensor_tensor(h1, z1, SLOPE, z1, ALU.mult, ALU.max).then_inc(sem("l0_h1"), 1)
                if mid:
                    c, b, k = mid
                    ln_reduce("l0", "S", sqS, c)
                    ln_inverse("l0", "S", c)
                    ln_apply(S[:, cs(c)], bank[1][:, :], small[:, 1, 2, :]).then_inc(sem("l0_S"), 1)
                if back:
                    c, b, k = back
                    ln_reduce("l0", "D", sqD, c)
                    ln_inverse("l0", "D", c)
                    if some(f"tab1_st{b}", k * 16):
                        dve.wait_ge(sem(f"tab1_st{b}"), k * 16)
                    if some("l0_T2", c - 1):
                        dve.wait_ge(sem("l0_T2"), upto("l0_T2", c - 1))
                    ln_apply(dn[b], bank[0][:, :], small[:, 0, 2, :]).then_inc(sem("l0_D"), 1)
            run_pipe(dve, l0, 3)

            def l1a(c, b, k):
                nodes_beside(dve, node_step, c, b, k)
                dve.wait_ge(sem("l1a_s"), upto("l1a_s", c + 1))
                dve.tensor_copy(sc[:, :, tc(c)], bank[6][:, 0:16].rearrange("p (q s) -> p q s", q=2)
                                ).then_inc(sem("l1a_sc"), 1)
            run_chunks(dve, l1a)
            for i in range(NB, NB + 3):
                node_step(i // 2, i % 2, NB1, NB)

            dve.wait_ge(sem("l1a_sc"), upto("l1a_sc", CH))
            dve.wait_ge(sem("l0_e"), upto("l0_e", CH))
            for q in range(2):
                dve.tensor_copy(EB[:, 4 + q, 0:TILES].rearrange("p (c h j) -> p c h j", h=2, j=4),
                                sc[:, q, :].rearrange("p (c j h) -> p c h j", h=2, j=4)).then_inc(sem("l1_perm"), 1)
            dve.wait_ge(sem("l1_run"), 1)
            dve.wait_ge(sem("l1a_stored0"), upto("l1a_stored0", 16 * (CH // 2 + 1)))
            dve.wait_ge(sem("l1a_stored1"), upto("l1a_stored1", 16 * (CH // 2)))
            dve.wait_ge(sem("tab1_st0"), 16)
            s_src = bank[6][0:RP, 0:2 * P].rearrange("p (g n) -> p g n", g=2)
            s_dst = bank[6][0:RP, 2 * P:4 * P].rearrange("p (g n) -> p g n", g=2)
            last_to_run(rt(2), s_dst, rt(1))
            dve.tensor_tensor(rt(3), s_src, rt(2), ALU.add).then_inc(sem("l1_dve"), 1)
            dve.wait_ge(sem("l1_act"), 1)
            two_level(rt(0), pen, rt(3), ALU.add, ALU.max, NEG, 2, False)
            last_to_run(rt(2), rt(0), rt(1))
            dve.tensor_tensor(rt(3), rt(3), rt(2), ALU.subtract).then_inc(sem("l1_dve"), 1)
            dve.wait_ge(sem("l1_act"), 2)
            two_level(rt(0), keep, rt(3), ALU.mult, ALU.add, 0.0, 0, False)
            last_to_run(rt(2), rt(0), rt(1))
            dve.tensor_scalar(rt(2), rt(2), 1e-20, None, ALU.max).then_inc(sem("l1_den"), 1)
            dve.wait_ge(sem("l1_den"), 1)
            dve.reciprocal(rt(1), rt(2)).then_inc(sem("l1_den"), 1)
            dve.wait_ge(sem("l1_den"), 2)
            dve.tensor_tensor(rt(3), rt(3), rt(1), ALU.mult).then_inc(sem("attn_run"), 1)

            dve.wait_ge(sem("l0_carry"), upto("l0_carry", CH * 2))
            dve.memset(carry[:, :], 0.0).then_inc(sem("carry_clear"), 1)
            dve.wait_ge(sem("carry_clear"), 1)

            def l1b(front, back):
                if front:
                    c, b, k = front
                    dve.wait_ge(sem(f"l1b_stream{b}"), upto(f"l1b_stream{b}", (k + 1) * 64))
                    dve.tensor_tensor(msg, xsT[b], stream[:, 1, b, :], ALU.mult).then_inc(sem("l1b_msg"), 1)
                    dve.wait_ge(sem("l1b_msg"), upto("l1b_msg", c + 1))
                    if some("l1b_cD", c):
                        dve.wait_ge(sem("l1b_cD"), upto("l1b_cD", c))
                    scan_half("l1b", c, b, msg, 0)
                if back:
                    ln_reduce("l1b", "D", sqD, back[0])
                if front:
                    scan_half("l1b", c, b, msg, 1)
                if back:
                    c, b, k = back
                    ln_inverse("l1b", "D", c)
                    if some(f"tab2_st{b}", k * 16):
                        dve.wait_ge(sem(f"tab2_st{b}"), k * 16)
                    if some("l1b_T2", c - 1):
                        dve.wait_ge(sem("l1b_T2"), upto("l1b_T2", c - 1))
                    ln_apply(dn[b], bank[0][:, :], small[:, 0, 2, :]).then_inc(sem("l1b_D"), 1)
                if front:
                    c, b, k = front
                    ln_reduce("l1b", "S", sqS, c)
                    ln_inverse("l1b", "S", c)
                    ln_apply(S[:, cs(c)], bank[1][:, :], small[:, 1, 2, :]).then_inc(sem("l1b_S"), 1)
            dve.wait_ge(sem("attn_out"), 16)
            run_pipe(dve, l1b, 2)

            dve.wait_ge(sem("l1b_carry"), upto("l1b_carry", CH * 2))
            dve.memset(carry[:, :], 0.0).then_inc(sem("carry_clear"), 1)
            dve.wait_ge(sem("carry_clear"), 2)

            def l2(front, mid, back):
                if mid:
                    c, b, k = mid
                    dve.wait_ge(sem(f"l2_keep{b}"), upto(f"l2_keep{b}", (k + 1) * 16))
                    dve.wait_ge(sem("l2_msg"), upto("l2_msg", c + 1))
                    if some("l2_yD", c):
                        dve.wait_ge(sem("l2_yD"), upto("l2_yD", c))
                    scan_half("l2", c, b, msg, 0)
                    scan_half("l2", c, b, msg, 1)
                    ln_reduce("l2", "S", sqS, c)
                if back:
                    ln_reduce("l2", "D", sqD, back[0])
                if mid:
                    ln_inverse("l2", "S", c)
                    ln_apply(S[:, cs(c)], cadd, small[:, 1, 2, :]).then_inc(sem("l2_S"), 1)
                if front:
                    c, b, k = front
                    dve.wait_ge(sem("l2_m"), upto("l2_m", c + 1))
                    dve.wait_ge(sem(f"l2_stream{b}"), upto(f"l2_stream{b}", (k + 1) * 32))
                    dve.tensor_tensor(msg, bank[5][:, :], stream[:, 1, b, :], ALU.mult).then_inc(sem("l2_msg"), 1)
                if back:
                    c, b, k = back
                    ln_inverse("l2", "D", c)
                    if some(f"tab3_st{b}", k * 16):
                        dve.wait_ge(sem(f"tab3_st{b}"), k * 16)
                    if some("l2_keepD", c - 1):
                        dve.wait_ge(sem("l2_keepD"), upto("l2_keepD", c - 1))
                    ln_apply(dn[b], bank[0][:, :], small[:, 0, 2, :]).then_inc(sem("l2_D"), 1)
                if front:
                    c, b, k = front
                    dve.wait_ge(sem("l2_cS"), upto("l2_cS", c + 1))
                    if some("l2_S", c):
                        dve.wait_ge(sem("l2_S"), upto("l2_S", c))
                    dve.tensor_tensor(rows64(cadd), rows64(bank[1][:, :]), XR[:, b, :, :], ALU.add
                                      ).then_inc(sem("l2_addS"), 1)
            dve.wait_ge(sem("tab2_st0"), 16 * (CH // 2 + 1))
            dve.wait_ge(sem("tab2_st1"), 16 * (CH // 2))
            dve.wait_ge(sem("l1b_T2"), upto("l1b_T2", CH))
            run_pipe(dve, l2, 3)

            dve.wait_ge(sem("l2_carry"), upto("l2_carry", CH * 2))
            dve.memset(carry[:, :], 0.0).then_inc(sem("carry_clear"), 1)
            dve.wait_ge(sem("carry_clear"), 3)
            dve.wait_ge(sem("tab3_st0"), 16 * (CH // 2 + 1))
            dve.wait_ge(sem("tab3_st1"), 16 * (CH // 2))
            dve.wait_ge(sem("l2_keepD"), upto("l2_keepD", CH))

            def weigh(c, b, k):
                dve.wait_ge(sem(f"l3_rows{b}"), upto(f"l3_rows{b}", (k + 1) * ROWS))
                if some("l3_T", c * 2):
                    dve.wait_ge(sem("l3_T"), upto("l3_T", c * 2))
                dve.tensor_tensor(xw2.rearrange("p (s d f) -> p s d f", d=2, f=F),
                                  XR[:, b, :, :].rearrange("p s (o f) -> p s o f", o=1).broadcast_to([P, TPC, 2, F]),
                                  wcol[:, tc(c)].rearrange("p (s o d) -> p s o d", o=1, d=1
                                                           ).broadcast_to([P, TPC, 2, F]),
                                  ALU.mult).then_inc(sem("l3_xw"), 1)

            def mask(c, b, k, q):
                for h in range(2):
                    if q == 0:
                        dve.wait_ge(sem("l3_xAB"), upto("l3_xAB", c * 2 + (h + 1)))
                    if h == 0:
                        if some("l3_pair", c * (REL // 2) + (q - 3)):
                            dve.wait_ge(sem("l3_pair"), upto("l3_pair", c * (REL // 2) + (q - 3)))
                    dve.scalar_tensor_tensor(NT[:, 4 * h + q % 4, :],
                                             (stream[:, 1, b, :], stream2[b])[h].bitcast(I32),
                                             relid[:, q:q + 1], (z1, h1)[h], ALU.is_equal, ALU.mult
                                             ).then_inc(sem("l3_mask"), 1)

            def l3(front, mid, back, scattered):
                if mid:
                    dve.wait_ge(sem(f"l3_stream{mid[1]}"), upto(f"l3_stream{mid[1]}", (mid[2] + 1) * 32))
                    mask(*mid, 0)
                if back:
                    c, b, k = back
                    dve.wait_ge(sem(f"l3_keep{b}"), upto(f"l3_keep{b}", (k + 1) * 16))
                    dve.wait_ge(sem("l3_pair"), upto("l3_pair", (c + 1) * (REL // 2)))
                    if some("l3_rD", c):
                        dve.wait_ge(sem("l3_rD"), upto("l3_rD", c))
                    scan_half("l3", c, b, bank[6 + b], 0)
                    scan_half("l3", c, b, bank[6 + b], 1)
                if mid:
                    for q in range(1, 4):
                        mask(*mid, q)
                if front:
                    weigh(*front)
                if mid:
                    for q in range(4, 6):
                        mask(*mid, q)
                if back:
                    c, b, k = back
                    dve.wait_ge(sem("l3_cD"), upto("l3_cD", c + 1))
                    dve.tensor_tensor(eg, bank[0][:, :], D[:, cs(c)], ALU.add).then_inc(sem("l3_addD"), 1)
                if mid:
                    mask(*mid, 6)
                if back:
                    ln_reduce("l3", "D", sqD, c)
                if mid:
                    mask(*mid, 7)
                if back:
                    ln_inverse("l3", "D", c)
                    if some(f"final_st{b}", k * ROWS):
                        dve.wait_ge(sem(f"final_st{b}"), k * ROWS)
                    ln_apply(dn[b], eg, small[:, 0, 2, :]).then_inc(sem("l3_D"), 1)
            dve.wait_ge(sem("a_stored0"), 16 * (NB // 2))
            dve.wait_ge(sem("a_stored1"), 16 * (NB // 2))
            run_pipe(dve, l3, 4)


def kernel(**inputs):
    import numpy as np
    import concourse.bacc as bacc
    from concourse import mybir as mb
    from concourse.bass_utils import run_bass_kernel_spmd as run

    g = {k: np.asarray(v) for k, v in inputs.items()}
    x, src, dst = g["x"], g["src"], g["dst"]
    H = F

    def pad_slots(a, fill):
        o = np.full((SLOTS,) + a.shape[1:], fill, a.dtype)
        o[:E] = a
        return o

    def node_cols(a):
        return np.ascontiguousarray(a.reshape(CH, 2, 4, P).transpose(3, 0, 2, 1).reshape(P, TILES))

    def feature_major(a):
        f = a.shape[1]
        return np.ascontiguousarray(a.reshape(CH, 2, CW, f).transpose(1, 3, 0, 2).reshape(2 * f, CH * CW))

    dst_p = pad_slots(dst, N)
    nxt = np.append(dst_p[1:], np.array([-1], dst.dtype))
    run_ = np.concatenate([np.array([-1], dst.dtype), dst_p, np.array([-1], dst.dtype)])
    rows = node_cols(np.arange(SLOTS)) * 0 + (
        (np.arange(CH)[None, :, None] * P + np.arange(P)[:, None, None]) * TPC
        + np.arange(TPC)[None, None, :]).reshape(P, TILES)
    xp = np.zeros((NPAD, F), x.dtype)
    xp[:N] = x
    xT = np.ascontiguousarray(xp.reshape(NB, P, 4, 2, F).transpose(3, 4, 0, 2, 1).reshape(P, NB * CW))

    def bd(a):
        k, m = a.shape
        o = np.zeros((P, P), np.float32)
        o[:k, :m] = a
        o[k:2 * k, m:2 * m] = a
        return o

    W1 = g["L0_gnn_W1"]
    aw = g["L1_gnn_attn_w"]
    Wm, Wa = g["L2_gnn_W_msg_w"], g["L2_gnn_W_apply_w"]
    w3 = np.zeros((P, P), np.float32)
    w3[0:32, 0:64] = g["L0_gnn_W3"].T
    w3[32:64, 64:128] = g["L0_gnn_W3"].T
    attn_rep = np.concatenate([np.repeat(aw[:64, None], P, 1), np.repeat(aw[64:, None], P, 1)])
    piece = {
        "eye": np.eye(P, dtype=np.float32),
        "cen": bd(np.eye(F, dtype=np.float32) - np.float32(1.0 / F)),
        "w_src": bd(g["L0_gnn_W_src"]), "w_tgt": bd(g["L0_gnn_W_tgt"]),
        "w_srcT": bd(g["L0_gnn_W_src"].T),
        "w1aT": bd(W1[:, :64].T), "w1bT": bd(W1[:, 64:128].T), "w1cT": bd(W1[:, 128:].T),
        "w2T": bd(g["L0_gnn_W2"].T), "w3rep": w3,
        "res_wT": bd(g["L1_gnn_res_W"].T), "w_outT": bd(g["L1_gnn_W_out"].T),
        "w_tgtI": np.zeros((P, P), np.float32), "attn_rep": attn_rep,
        "msg1": bd(Wm[:64]), "msg2": bd(Wm[64:]), "app1": bd(Wa[:64]), "app2": bd(Wa[64:]),
        "w_edge": bd(g["L0_gnn_W_edge"]),
    }
    wpack = np.concatenate([piece[n] for n in PIECES], 1)

    def st(v):
        o = np.zeros((P,), np.float32)
        o[:2 * len(v)] = np.concatenate([v, v])
        return o
    z = np.zeros(64, np.float32)
    column = {
        "b_src": st(g["L0_gnn_b_src"]), "b_tgt": st(g["L0_gnn_b_tgt"]), "b_edge": st(g["L0_gnn_b_edge"]),
        "b1": st(g["L0_gnn_b1"]), "b2": st(g["L0_gnn_b2"]), "b3": np.repeat(g["L0_gnn_b3"], P),
        "res_b": st(g["L1_gnn_res_b"]), "b_out": st(g["L1_gnn_b_out"]), "msg_b": st(g["L2_gnn_W_msg_b"]),
        "app_b": st(g["L2_gnn_W_apply_b"]),
        "attn1_0": np.concatenate([aw[:64], z]), "attn1_1": np.concatenate([z, aw[:64]]),
        "attn2_0": np.concatenate([aw[64:], z]), "attn2_1": np.concatenate([z, aw[64:]]),
    }
    cpack = np.ascontiguousarray(np.stack([column[n] for n in COLS], 1))
    rw = g["L3_gnn_weight"].reshape(REL // 2, 2 * F, F).transpose(1, 0, 2).reshape(P, -1)
    relid = (2 * np.arange(REL // 2)[None, :] + (np.arange(P)[:, None] >= F)).astype(np.float32)
    arrays = {
        "x": x,
        "xmap_in": np.concatenate([x, np.full((N, 1), NO_ROW, x.dtype)], 1),
        "xT": xT,
        "dst_col": node_cols(dst_p), "nxt_col": node_cols(nxt), "src_col": node_cols(pad_slots(src, 0)),
        "row_col": rows.astype(np.float32), "dst_run": run_,
        "attr8T": feature_major(pad_slots(g["edge_attr_8"], 0)),
        "attr32T": feature_major(pad_slots(g["edge_attr_32"], 0)),
        "rel_flat": pad_slots(g["edge_type_16"], 0),
        "weight_col": node_cols(pad_slots(g["edge_weight1"][:, 0], 0)),
        "wpack": wpack, "cpack": cpack, "relpack": np.concatenate([rw, relid], 1),
    }
    arrays = {k: np.ascontiguousarray(v) for k, v in arrays.items()}

    nc = bacc.Bacc("TRN2", target_bir_lowering=False, num_devices=1)
    aps = [nc.dram_tensor(f"in_{k}", v.shape, mb.dt.from_np(v.dtype), kind="ExternalInput").ap()
           for k, v in arrays.items()]
    o = nc.dram_tensor("out_0", (NPAD, F), F32, kind="ExternalOutput").ap()
    build(nc, *aps, o)
    r = run(nc, [{f"in_{k}": v for k, v in arrays.items()}], core_ids=[0])
    return r.results[0]["out_0"][:N]
```

```python
from contextlib import ExitStack

import concourse.bass as bass
from concourse import mybir

F32 = mybir.dt.float32
BF16 = mybir.dt.bfloat16
I32 = mybir.dt.int32
ALU = mybir.AluOpType
ACT = mybir.ActivationFunctionType
AX = mybir.AxisListType

N, E, F, P = 100000, 25000, 64, 128
REL = 16
CW = 512
CH = -(-E // (2 * CW))
SLOTS = CH * 2 * CW
TILES = SLOTS // P
TPC = TILES // CH
RP = TILES // 2
NB = 4 * CH
NPAD = NB * 2 * CW
EPS = 1e-5
SLOPE = 0.01
NO_ROW = 1 << 20
NEG = -1.0e30
NB1 = 2 * CH + 6
CUT = NB - NB1 - CH
assert NPAD >= N and CH % 2 == 1 and NB1 % 2 == 0 and 8 <= CUT < CH - 4

PIECES = ["eye", "cen", "w_src", "w_tgt", "w_srcT", "w1aT", "w1bT", "w1cT", "w2T", "w3rep",
          "res_wT", "w_outT", "w_tgtI", "attn_rep", "msg1", "app1", "app2", "w_edge", "msg2"]
COLS = ["b_src", "b_tgt", "b_edge", "b1", "b2", "b3", "res_b", "b_out", "msg_b", "app_b",
        "attn1_0", "attn1_1", "attn2_0", "attn2_1"]


ROWS = 16 * TPC
LN = {f"{what}{who}": 1 for what in ("sq", "ss", "sd", "rs") for who in "DS"}
BOTH = {"scan": 2, "carry": 2, "msg": 1, "cD": 1, "cS": 1, "D": 1, "S": 1, **LN}
STAGES = ["p0", "l0", "l1a", "l1b", "l2", "l3"]
PER_CHUNK = {
    "p0": {"rows0": ROWS, "rows1": ROWS, "idx": 1, "turn": 1, "T": 1},
    "l0": {"rows0": ROWS, "rows1": ROWS, "idx": 1, "turn": 1, "T": 1, "stream0": 32, "stream1": 32, "xsT": 1,
           "T2": 1, "DT": 1, **BOTH},
    "l1a": {"rows0": ROWS, "rows1": ROWS, "idx": 1, "turn": 1, "T": 1, "stream0": 16, "stream1": 16, "copy": 1},
    "l1b": {"stream0": 64, "stream1": 64, "T2": 1, "DT": 1, **BOTH},
    "l2": {"rows0": ROWS, "rows1": ROWS, "idx": 1, "turn": 1, "T": 1, "stream0": 32, "stream1": 32, "copy": 1,
           "keep0": 16, "keep1": 16, "xsT": 1, "rD": 1, **BOTH},
    "l3": {"rows0": ROWS, "rows1": ROWS, "idx": 1, "turn": 1, "T": 2, "stream0": 32, "stream1": 32, "copy": 1,
           "keep0": 16, "keep1": 16,
           "rD": 1, "scan": 2, "carry": 2, "cD": 1, "D": 1, "sqD": 1, "ssD": 1, "sdD": 1, "rsD": 1},
}


def run_chunks(eng, body, head=3, tail=0):
    for c in range(head):
        body(c, c % 2, c // 2)
    with eng.Fori(head // 2, (CH - tail) // 2) as i:
        body(i * 2 + 1, 1, i)
        body(i * 2 + 2, 0, i + 1)
    for c in range(CH - tail, CH):
        body(c, c % 2, c // 2)


def run_pipe(eng, body, depth):
    def step(t):
        body(*((t - p, (t - p) % 2, (t - p) // 2) if 0 <= t - p < CH else None for p in range(depth)))

    def loop_step(i, t):
        body(*((i * 2 + (t - p), (t - p) % 2, i + (t - p) // 2) for p in range(depth)))
    peeled = 2 * depth - 1
    for t in range(peeled):
        step(t)
    with eng.Fori(peeled // 2, CH // 2) as i:
        loop_step(i, 1)
        loop_step(i, 2)
    for t in range(CH, CH + depth - 1):
        step(t)


def run_ahead(eng, body, depth):
    def step(t):
        body(*((t - p, (t - p) % 2, (t - p) // 2) if 0 <= t - p < CH else None for p in range(depth)))
    peeled = 2 * depth - 1
    for t in range(peeled):
        step(t)
    with eng.Fori(peeled // 2, CH // 2 - 1) as i:
        for t in (1, 2):
            body(*((i * 2 + (t - p), (t - p) % 2, i + (t - p) // 2) for p in range(depth)))
    for t in range(CH - 2, CH + depth - 1):
        step(t)


def run_cut(eng, body, alone, depth, cut, back_on):
    def step(t):
        body(*((t - p, (t - p) % 2, (t - p) // 2) if 0 <= t - p < CH else None for p in range(depth)))

    def pair(i, what):
        for t in (1, 2):
            what(*((i * 2 + (t - p), (t - p) % 2, i + (t - p) // 2) for p in range(depth)))
    peeled = 5
    for t in range(peeled):
        step(t)
    with eng.Fori(peeled // 2, cut // 2) as i:
        pair(i, body)
    for t in range(cut, back_on):
        step(t)
    with eng.Fori(back_on // 2, CH // 2) as i:
        pair(i, alone)
    for t in range(CH, CH + depth - 1):
        step(t)


def node_phases(h, par, lo, hi):
    out = []
    for p in range(4):
        d = par - p
        blk, b, k = h * 2 + d, d % 2, h + d // 2
        out.append((blk, b, k) if not isinstance(h, int) or lo <= blk < hi else None)
    return out


def run_nodes_alone(eng, step):
    step(CH // 2, 1, 0, NB1)
    with eng.Fori(CH // 2 + 1, NB1 // 2 - 1) as h:
        step(h, 0, 0, NB1)
        step(h, 1, 0, NB1)
    for i in range(NB1 - 2, NB1 + 3):
        step(i // 2, i % 2, 0, NB1)


def nodes_beside(step, b, k, first):
    step(k + (first + b) // 2, (first + b) % 2, NB1, NB)


def build(nc, x, xmap_in, xT, dst_col, nxt_col, src_col, row_col, dst_run, attr8T, attr32T,
          rel_flat, weight_col, wpack, cpack, relpack, out):
    with ExitStack() as ctx:
        def sb(name, shape, dt=F32):
            return ctx.enter_context(nc.sbuf_tensor(name, shape, dt))

        sems = {}

        def signal_of(name):
            stage, _, what = name.partition("_")
            if stage not in STAGES or what not in PER_CHUNK[stage]:
                return name, 0
            chunks = {"0": CH // 2 + 1, "1": CH // 2}.get(what[-1], CH)
            return what, sum(PER_CHUNK[s].get(what, 0) * chunks for s in STAGES[:STAGES.index(stage)])

        def sem(name):
            name = signal_of(name)[0]
            if name not in sems:
                sems[name] = ctx.enter_context(nc.semaphore(name))
            return sems[name]

        def upto(name, value):
            first = signal_of(name)[1]
            return max(value, 0) + first if isinstance(value, int) else value + first

        def some(name, value):
            at = upto(name, value)
            return not isinstance(at, int) or at > 0

        xmap = nc.dram_tensor("xmap", (N, F + 1), F32, kind="Internal").ap()
        dtab = [nc.dram_tensor(f"dtab{l}", (SLOTS, F), F32, kind="Internal").ap() for l in (1, 2, 3)]
        keep_flat = nc.dram_tensor("keep_flat", (SLOTS,), F32, kind="Internal").ap()
        inv_flat = nc.dram_tensor("inv_flat", (SLOTS,), F32, kind="Internal").ap()
        attn_flat = nc.dram_tensor("attn_flat", (SLOTS,), F32, kind="Internal").ap()
        xmap_cells = xmap.rearrange("n (f o) -> (n f) o", o=1)

        S = sb("S", [P, CH * CW])
        D = sb("D", [P, CH * CW])
        XR = sb("XR", [P, 2, TPC, F])
        idx_st = sb("idx_st", [P, 2, TPC], I32)
        row_st = sb("row_st", [P, 2, TPC])
        sidx_st = sb("sidx_st", [P, 2, TPC], I32)
        dstc = sb("dstc", [P, TILES], I32)
        srcc = sb("srcc", [P, TILES], I32)
        nxtc = sb("nxtc", [P, TILES], I32)
        rowc = sb("rowc", [P, TILES])
        qcol = sb("qcol", [P, TILES], I32)
        outc = sb("outc", [P, TILES], I32)
        cellc = sb("cellc", [P, TILES], I32)
        wcol = sb("wcol", [P, TILES])
        sc = sb("sc", [P, 2, TILES])
        stream = sb("stream", [P, 2, 2, CW])
        attr = sb("attr", [16, 2, CW])
        w = sb("w", [P, len(PIECES), P])
        cols = sb("cols", [P, len(COLS)])
        relw = sb("relw", [P, REL // 2, F])
        relid = sb("relid", [P, REL // 2])
        folded = sb("folded", [P, 5, P])
        edge1 = sb("edge1", [16, P])
        attn_w = sb("attn_w", [P, 4])
        fcol = sb("fcol", [P, 3])
        ones_b = sb("ones_b", [P, P], BF16)
        one = sb("one", [1, 1])
        epsc = sb("epsc", [P, 2])
        brow = sb("brow", [P, 3, CW], BF16)
        NT = sb("NT", [P, 13, CW])
        dT = sb("dT", [P, 2, CW])
        EB = sb("EB", [P, 12, CW])
        small = sb("small", [P, 2, 3, 8])
        asmall = sb("asmall", [P, 3, 3, 8])
        token = sb("token", [1, 4])
        carry = sb("carry", [P, 1])
        runs = sb("runs", [RP, 4, 2, P])
        rowbuf = sb("rowbuf", [1, 4, TILES + 2])
        ends = sb("ends", [RP, 4, 2])

        bank = [ctx.enter_context(nc.psum_tensor(f"bank{i}", [P, CW], F32)) for i in range(8)]

        def W(name, k=P, m=P):
            return w[0:k, PIECES.index(name), 0:m]

        def col(name, m=P):
            return cols[0:m, COLS.index(name):COLS.index(name) + 1]

        A1, B1, M0, M1, WOC = (folded[:, i, :] for i in range(5))
        eye = W("eye")
        cen = W("cen")

        def rows64(t):
            return t.rearrange("p (s f) -> p s f", f=F)

        def bcast8(t):
            return t.rearrange("p (s o) -> p s o", o=1).broadcast_to([P, 8, F])

        def cs(c):
            return bass.ds(c * CW, CW)

        def tc(c):
            return bass.ds(c * TPC, TPC)

        def half_stream(flat, c):
            v = flat[bass.ds(c * 2 * CW, 2 * CW)].rearrange("(h o n) -> h o n", h=2, o=1)
            return v.broadcast_to([2, F, CW])

        node_in = [NT[:, 0, :], NT[:, 1, :]]
        node_sq = [NT[:, 2, :], NT[:, 3, :], NT[:, 4, :]]
        node_x1, node_x1T = NT[:, 5, :], NT[:, 6, :]
        node_x2, node_x2T = [NT[:, 7, :], NT[:, 8, :]], NT[:, 9, :]
        node_r, node_out = NT[:, 10, :], [NT[:, 11, :], NT[:, 12, :]]

        xsT, z1, h1 = [EB[:, i, :] for i in (0, 1)], EB[:, 2, :], EB[:, 3, :]
        h2, eg, msg = EB[:, 4, :], EB[:, 4, :], EB[:, 5, :]
        agg = EB[:, 6, :]
        sqD, sqS = EB[:, 7, :], EB[:, 8, :]
        dn = [EB[:, 9, :], EB[:, 10, :]]
        z2 = EB[:, 11, :]
        stream2 = [NT[:, 8, :], NT[:, 9, :]]
        rD, rS, cadd = NT[:, 10, :], NT[:, 11, :], NT[:, 12, :]
        xw2 = NT[:, 11:13, :].rearrange("p a n -> p (a n)")
        XM = NT[:, 0:3, :].rearrange("p a n -> p (a n)")[:, 0:2 * TPC * (F + 1)].rearrange(
            "p (b s f) -> p b s f", b=2, s=TPC)

        def rt(i):
            return EB[0:RP, i, 0:2 * P].rearrange("p (g n) -> p g n", g=2)

        block = ctx.enter_context(nc.Block())

        @block.sync
        def _(sp):
            sp.dma_start(dstc[:, :], dst_col).then_inc(sem("dstc_in"), 16)
            sp.dma_start(w[:, :, :], wpack.rearrange("p (n m) -> p n m", m=P)).then_inc(sem("weights_in"), 16)
            sp.dma_start(cols[:, :], cpack).then_inc(sem("weights_in"), 16)
            sp.dma_start(relw[:, :, :], relpack[:, 0:REL // 2 * F].rearrange("p (k m) -> p k m", m=F)
                         ).then_inc(sem("weights_in"), 16)
            sp.dma_start(relid[:, :], relpack[:, REL // 2 * F:]).then_inc(sem("weights_in"), 16)
            sp.dma_start(nxtc[:, :], nxt_col).then_inc(sem("index_in"), 16)
            sp.dma_start(srcc[:, :], src_col).then_inc(sem("index_in"), 16)
            sp.dma_start(rowc[:, :], row_col).then_inc(sem("index_in"), 16)
            sp.dma_start(wcol[:, :], weight_col).then_inc(sem("index_in"), 16)
            for i in range(3):
                sp.dma_start(rt(i).bitcast(I32),
                             dst_run[i:i + SLOTS].rearrange("(g p n) -> p g n", g=2, n=P)
                             ).then_inc(sem("runs_in"), 16)

            def node_load(blk, b, k):
                if not isinstance(blk, int) or blk > 1:
                    if some("a_c0", blk - 1):
                        sp.wait_ge(sem("a_c0"), blk - 1)
                sp.dma_start(node_in[b], xT[:, cs(blk)]).then_inc(sem(f"a_in{b}"), 16)

            def node_store(blk, b, k):
                sp.wait_ge(sem("a_out"), blk + 1)
                sp.dma_start(out[bass.ds(blk * 1024, 1024), :].rearrange("(p s) f -> p (s f)", p=P),
                             node_out[b]).then_inc(sem(f"a_stored{b}"), 16)

            def node_io(h, par, lo, hi):
                nxt = h * 2 + (par + 1)
                if not isinstance(h, int) or nxt < hi:
                    node_load(nxt, (par + 1) % 2, None)
                last = node_phases(h, par, lo, hi)[3]
                if last:
                    node_store(*last)

            node_load(0, 0, 0)
            sp.wait_ge(sem("keep_run"), 1)
            sp.dma_start(keep_flat.rearrange("(g p n) -> p g n", g=2, n=P), runs[:, 0, :, :]
                         ).then_inc(sem("flat_out"), 16)

            def stage1(c, b, k):
                sp.dma_start(xmap[bass.ds(c * (N // CH), N // CH), :].rearrange("(a n) f -> a (n f)", a=16),
                             xmap_in[bass.ds(c * (N // CH), N // CH), :].rearrange("(a n) f -> a (n f)", a=16)
                             ).then_inc(sem("xmap_init"), 16)
                node_io(k, b, 0, NB1)
            run_chunks(sp, stage1, head=5)
            run_nodes_alone(sp, node_io)

            sp.wait_ge(sem("flat_out"), 16)
            sp.wait_ge(sem("p0_D"), upto("p0_D", CH))


            def l0(front, mid, back):
                if front:
                    c, b, k = front
                    if some("l0_z1", c - 1):
                        sp.wait_ge(sem("l0_z1"), upto("l0_z1", c - 1))
                    sp.dma_start(attr[:, b, :], attr8T[:, cs(c)]).then_inc(sem(f"l0_attr{b}"), 16)
                if mid:
                    c, b, k = mid
                    sp.wait_ge(sem("ring_clear"), 1)
                    if some("l0_cD", c - 1):
                        sp.wait_ge(sem("l0_cD"), upto("l0_cD", c - 1))
                    sp.dma_start(dT[:, b, :], D[:, cs(c)]).then_inc(sem(f"l0_stream{b}"), 16)
                    sp.dma_start(stream[:, 0, b, :], half_stream(keep_flat, c)).then_inc(sem(f"l0_stream{b}"), 16)
            run_pipe(sp, l0, 3)


            def l1a_D(c, b):
                if some("l1a_s", c - 1):
                    sp.wait_ge(sem("l1a_s"), upto("l1a_s", c - 1))
                sp.dma_start(dT[:, b, :], D[:, cs(c)]).then_inc(sem(f"l1a_stream{b}"), 16)

            def l1a(c, b, k):
                if not (isinstance(c, int) and c == CH - 1):
                    l1a_D(c + 1, 1 - b)
                sp.wait_ge(sem("ring_clear"), 1)
                sp.wait_ge(sem("l1a_ST"), upto("l1a_ST", c + 1))
                sp.dma_start(S[:, cs(c)], xsT[b]).then_inc(sem(f"l1a_stored{b}"), 16)
                nodes_beside(node_io, b, k, NB1)

            sp.wait_ge(sem("l0_DT"), upto("l0_DT", CH))
            node_load(NB1, NB1 % 2, None)
            l1a_D(0, 0)
            run_chunks(sp, l1a, head=5, tail=2)
            sp.wait_ge(sem("l1a_stored0"), upto("l1a_stored0", 16 * (CH // 2 + 1)))
            sp.wait_ge(sem("l1a_stored1"), upto("l1a_stored1", 16 * (CH // 2)))
            sp.wait_ge(sem("inv_run"), 1)
            sp.dma_start(inv_flat.rearrange("(g p n) -> p g n", g=2, n=P), rt(7)
                         ).then_inc(sem("flat_out"), 16)
            sp.wait_ge(sem("flat_out"), 32)

            sp.wait_ge(sem("attn_run"), 1)
            sp.dma_start(attn_flat.rearrange("(g p n) -> p g n", g=2, n=P), rt(3)
                         ).then_inc(sem("attn_out"), 16)
            sp.wait_ge(sem("attn_out"), 16)

            def l1b(front, back, tail, nodes=True):
                if not front:
                    return
                c, b, k = front
                sp.wait_ge(sem("ring_clear"), 1)
                if some("l1b_cD", c - 1):
                    sp.wait_ge(sem("l1b_cD"), upto("l1b_cD", c - 1))
                sp.dma_start(dT[:, b, :], D[:, cs(c)]).then_inc(sem(f"l1b_stream{b}"), 16)
                sp.dma_start(xsT[b], S[:, cs(c)]).then_inc(sem(f"l1b_stream{b}"), 16)
                sp.dma_start(stream[:, 1, b, :], half_stream(attn_flat, c)).then_inc(sem(f"l1b_stream{b}"), 16)
                sp.dma_start(stream[:, 0, b, :], half_stream(keep_flat, c)).then_inc(sem(f"l1b_stream{b}"), 16)
                if nodes:
                    nodes_beside(node_io, b, k, NB1 + CH)

            def l1b_alone(front, back, tail):
                l1b(front, back, tail, nodes=False)
            run_cut(sp, l1b, l1b_alone, 3, CUT - 2, CUT + 4)

            sp.wait_ge(sem("l1b_DT"), upto("l1b_DT", CH))
            sp.wait_ge(sem("a_stored0"), 16 * (NB // 2))
            sp.wait_ge(sem("a_stored1"), 16 * (NB // 2))

            def l2(front, mid, back):
                if front:
                    c, b, k = front
                    if some("l2_msg", c - 1):
                        sp.wait_ge(sem("l2_msg"), upto("l2_msg", c - 1))
                    sp.dma_start(stream2[b][0:F, :], attr32T[:, cs(c)]).then_inc(sem(f"l2_stream{b}"), 16)
                    sp.dma_start(stream[:, 1, b, :], half_stream(inv_flat, c)).then_inc(sem(f"l2_stream{b}"), 16)
                    if some("l2_scan", (c - 1) * 2):
                        sp.wait_ge(sem("l2_scan"), upto("l2_scan", (c - 1) * 2))
                    sp.dma_start(stream[:, 0, b, :], half_stream(keep_flat, c)).then_inc(sem(f"l2_keep{b}"), 16)
                if mid:
                    c, b, k = mid
                    sp.wait_ge(sem("ring_clear"), 1)
                    if some("l2_cD", c - 1):
                        sp.wait_ge(sem("l2_cD"), upto("l2_cD", c - 1))
                    sp.dma_start(dT[:, b, :], D[:, cs(c)]).then_inc(sem(f"l2_dT{b}"), 16)
            run_pipe(sp, l2, 3)

            def rel_half(c, h):
                v = rel_flat[bass.ds(c * 2 * CW + h * CW, CW)].rearrange("(o n) -> o n", o=1)
                return v.broadcast_to([P, CW])

            sp.wait_ge(sem("l2_msg"), upto("l2_msg", CH))
            sp.wait_ge(sem("l2_scan"), upto("l2_scan", CH * 2))

            def l3(c, b, k):
                if some("l3_mask", (c - 1) * REL):
                    sp.wait_ge(sem("l3_mask"), upto("l3_mask", (c - 1) * REL))
                sp.dma_start(stream[:, 1, b, :].bitcast(I32), rel_half(c, 0)).then_inc(sem(f"l3_stream{b}"), 16)
                sp.dma_start(stream2[b].bitcast(I32), rel_half(c, 1)).then_inc(sem(f"l3_stream{b}"), 16)
                if some("l3_scan", (c - 1) * 2):
                    sp.wait_ge(sem("l3_scan"), upto("l3_scan", (c - 1) * 2))
                sp.dma_start(stream[:, 0, b, :], half_stream(keep_flat, c)).then_inc(sem(f"l3_keep{b}"), 16)
            run_chunks(sp, l3)
            sp.wait_ge(sem("a_stored0"), 16 * (NB // 2))
            sp.wait_ge(sem("a_stored1"), 16 * (NB // 2))
            sp.wait_ge(sem("final_st0"), 16 * TPC * (CH // 2 + 1))
            sp.wait_ge(sem("final_st1"), 16 * TPC * (CH // 2))

        @block.gpsimd
        def _(pool):
            last_node, last_row, last_cell = (pool.to_reg(v) for v in (N - 1, SLOTS - 1, N * (F + 1) - 1))
            pool.memset(token[:, :], 0.0).then_inc(sem("token"), 1)
            pool.wait_ge(sem("token"), 1)
            pool.memset(XR[:, :, :, :], 0.0).then_inc(sem("ring_clear"), 1)
            pool.memset(ones_b[:, :], 1.0).then_inc(sem("consts"), 1)
            pool.memset(one[:, :], 1.0).then_inc(sem("consts"), 1)
            pool.memset(epsc[:, 0:1], EPS).then_inc(sem("consts"), 1)
            pool.memset(epsc[:, 1:2], EPS * EPS).then_inc(sem("consts"), 1)
            pool.memset(brow[:, :, :], 0.0).then_inc(sem("consts"), 1)
            pool.memset(carry[:, :], 0.0).then_inc(sem("consts"), 1)

            def gather(stage, table, bound, ring, b):
                for s in range(TPC):
                    pool.indirect_dma_start(
                        ring[:, b, s, :], None, table,
                        bass.IndirectOffsetOnAxis(ap=idx_st[:, b, s:s + 1], axis=0),
                        bounds_check=bound, oob_is_err=False).then_inc(sem(f"{stage}_rows{b}"), 16)

            def carry_waits(stage, c, cell=0):
                if some(f"{stage}_turn", c):
                    pool.wait_ge(sem(f"{stage}_turn"), upto(f"{stage}_turn", c))
                pool.tensor_tensor(token[:, cell:cell + 1], token[:, 1:2], token[:, 2:3], ALU.add
                                   ).then_inc(sem(f"{stage}_turn"), 1)

            pool.wait_ge(sem("ring_clear"), 1)

            def p0(c, b, k):
                pool.wait_ge(sem("p0_idx"), upto("p0_idx", c + 1))
                if some("p0_T", c - 1):
                    pool.wait_ge(sem("p0_T"), upto("p0_T", c - 1))
                carry_waits("p0", c)
                gather("p0", x, last_node, XR, b)
            run_chunks(pool, p0)

            pool.wait_ge(sem("xmap_init"), 16 * CH)
            pool.wait_ge(sem("cells"), 1)
            pool.wait_ge(sem("index_in"), 64)

            def map_scatter(c, b, k):
                if some(f"map_st{b}", k * (16 * TPC)):
                    pool.wait_ge(sem(f"map_st{b}"), k * (16 * TPC))
                pool.tensor_copy(sidx_st[:, b, :], cellc[:, tc(c)]).then_inc(sem("map_idx"), 1)
                pool.tensor_copy(row_st[:, b, :], rowc[:, tc(c)]).then_inc(sem("map_idx"), 1)
                pool.wait_ge(sem("map_idx"), (c + 1) * 2)
                carry_waits("map", c, 3)
                for s in range(TPC):
                    pool.indirect_dma_start(
                        xmap_cells, bass.IndirectOffsetOnAxis(ap=sidx_st[:, b, s:s + 1], axis=0),
                        row_st[:, b, s:s + 1], None,
                        bounds_check=last_cell, oob_is_err=False).then_inc(sem(f"map_st{b}"), 16)
            run_chunks(pool, map_scatter)
            pool.wait_ge(sem("map_st0"), 16 * TPC * (CH // 2 + 1))
            pool.wait_ge(sem("map_st1"), 16 * TPC * (CH // 2))

            pool.wait_ge(sem("p0_T"), upto("p0_T", CH))
            pool.wait_ge(sem("p0_rows0"), upto("p0_rows0", 16 * TPC * (CH // 2 + 1)))
            pool.wait_ge(sem("p0_rows1"), upto("p0_rows1", 16 * TPC * (CH // 2)))

            pool.wait_ge(sem("a_stored0"), 16 * (NB1 // 2))
            pool.wait_ge(sem("a_stored1"), 16 * (NB1 // 2))


            def l0(c, b, k):
                pool.wait_ge(sem("l0_idx"), upto("l0_idx", c + 1))
                if some("l0_dense", c - 1):
                    pool.wait_ge(sem("l0_dense"), upto("l0_dense", c - 1))
                if some("l0_q", c - 1):
                    pool.wait_ge(sem("l0_q"), upto("l0_q", c - 1))
                carry_waits("l0", c)
                gather("l0", xmap, last_node, XM, b)
            run_chunks(pool, l0)

            def layer_gather(stage, l, prev):
                pool.wait_ge(sem("l0_q"), upto("l0_q", CH))
                pool.wait_ge(sem(f"{prev}_rows0"), upto(f"{prev}_rows0", 16 * TPC * (CH // 2 + 1)))
                pool.wait_ge(sem(f"{prev}_rows1"), upto(f"{prev}_rows1", 16 * TPC * (CH // 2)))
                pool.wait_ge(sem(f"tab{l}_st0"), 16 * (CH // 2 + 1))
                pool.wait_ge(sem(f"tab{l}_st1"), 16 * (CH // 2))

            layer_gather("l1a", 1, "l0")

            def l1a(c, b, k):
                pool.wait_ge(sem("l1a_idx"), upto("l1a_idx", c + 1))
                pool.wait_ge(sem("l1a_copy"), upto("l1a_copy", c + 1))
                carry_waits("l1a", c)
                gather("l1a", dtab[0], last_row, XR, b)
            run_chunks(pool, l1a)

            def node_scale(h, par, lo, hi):
                last = node_phases(h, par, lo, hi)[3]
                if last:
                    i, b, k = last
                    pool.wait_ge(sem("a_rs2"), i + 1)
                    if some("a_out", i):
                        pool.wait_ge(sem("a_out"), i)
                    pool.tensor_tensor(rows64(node_out[b]), rows64(node_out[b]), bcast8(asmall[:, 2, 2, :]),
                                       ALU.mult).then_inc(sem("a_out"), 1)

            def l1b_alone(front):
                c, b, k = front
                pool.wait_ge(sem(f"l1b_stream{b}"), upto(f"l1b_stream{b}", (k + 1) * 64))
                if some("l1b_scan", c * 2):
                    pool.wait_ge(sem("l1b_scan"), upto("l1b_scan", c * 2))
                pool.tensor_tensor(msg, xsT[b], stream[:, 1, b, :], ALU.mult).then_inc(sem("l1b_msg"), 1)

            def l1b(front):
                l1b_alone(front)
                nodes_beside(node_scale, front[1], front[2], NB1 + CH)
            pool.wait_ge(sem("l0_scan"), upto("l0_scan", CH * 2))
            run_cut(pool, l1b, l1b_alone, 1, CUT, CUT + 4)
            layer_gather("l2", 2, "l1a")

            def l2(c, b, k):
                pool.wait_ge(sem("l2_idx"), upto("l2_idx", c + 1))
                pool.wait_ge(sem("l2_copy"), upto("l2_copy", c + 1))
                carry_waits("l2", c)
                gather("l2", dtab[1], last_row, XR, b)
            run_chunks(pool, l2)
            layer_gather("l3", 3, "l2")
            pool.wait_ge(sem("a_stored0"), 16 * (NB // 2))
            pool.wait_ge(sem("a_stored1"), 16 * (NB // 2))
            pool.wait_ge(sem("map_st0"), 16 * TPC * (CH // 2 + 1))

            def l3_front(c, b, k):
                pool.wait_ge(sem("l3_idx"), upto("l3_idx", c + 1))
                pool.wait_ge(sem("l3_copy"), upto("l3_copy", c + 1))
                carry_waits("l3", c)
                gather("l3", dtab[2], last_row, XR, b)

            def final_scatter(c, b, k):
                pool.wait_ge(sem("final_idx"), c + 1)
                pool.wait_ge(sem("l3_D"), upto("l3_D", c + 1))
                carry_waits("final", c, 3)
                for s in range(TPC):
                    pool.indirect_dma_start(
                        out[:, :], bass.IndirectOffsetOnAxis(ap=sidx_st[:, b, s:s + 1], axis=0),
                        dn[b][:, s * F:(s + 1) * F], None,
                        bounds_check=last_node, oob_is_err=False).then_inc(sem(f"final_st{b}"), 16)

            def l3(front, ahead, mid, back):
                if front:
                    l3_front(*front)
                if back:
                    final_scatter(*back)
            run_pipe(pool, l3, 4)

        @block.tensor
        def _(pe):
            pe.wait_ge(sem("weights_in"), 64)
            pe.wait_ge(sem("consts"), 6)
            pe.wait_ge(sem("eye_plus"), 2)
            fold = bank[6]
            pe.matmul(fold[:, 0:128], W("w_src"), W("w1aT"), start=True, stop=True)
            pe.matmul(fold[:, 128:256], W("w_tgt"), W("w1bT"), start=True, stop=True)
            pe.matmul(fold[:, 256:384], W("w_tgtI"), cen, start=True, stop=True)
            pe.matmul(fold[:, 384:512], W("res_wT"), cen, start=True, stop=True).then_inc(sem("fold"), 1)
            f2 = bank[7]
            pe.matmul(f2[:, 0:128], W("w_outT"), cen, start=True, stop=True)
            pe.matmul(f2[0:16, 128:256], W("w_edge", m=16), W("w1cT"), start=True, stop=True)
            pe.matmul(f2[:, 256:260], W("w_outT"), cols[:, COLS.index("attn1_0"):COLS.index("attn1_0") + 4],
                      start=True, stop=True)
            pe.matmul(f2[:, 260:261], W("w1aT"), col("b_src"), start=True, stop=False)
            pe.matmul(f2[:, 260:261], W("w1bT"), col("b_tgt"), start=False, stop=False)
            pe.matmul(f2[:, 260:261], W("w1cT"), col("b_edge"), start=False, stop=True)
            pe.matmul(f2[:, 261:262], W("app2"), col("msg_b"), start=True, stop=True)
            pe.matmul(f2[:, 262:263], W("attn_rep"), col("b_out"), start=True, stop=True).then_inc(sem("fold"), 1)
            f3 = bank[5]
            pe.matmul(f3[:, 0:128], col("b_tgt").broadcast_to([P, P]), cen, start=True, stop=True)
            pe.matmul(f3[:, 128:256], col("res_b").broadcast_to([P, P]), cen, start=True, stop=True)
            pe.matmul(f3[:, 256:384], col("b_out").broadcast_to([P, P]), cen, start=True, stop=True
                      ).then_inc(sem("fold"), 1)

            tls = [0]

            def two_level(loc, last, off, static=False):
                n = tls[0]
                tls[0] += 1
                pe.wait_ge(sem("tl_ends"), n + 1)
                row = bank[7][0:1, 0:TILES]
                for g in range(2):
                    mm = pe.matmul(bank[7][0:1, g * RP:(g + 1) * RP], loc[:, g, last:last + 1],
                                   eye[0:RP, 0:RP], start=True, stop=True)
                mm.then_inc(sem("tl_row"), 1)
                pe.wait_ge(sem("tl_carry"), n + 1)
                for g in range(2):
                    mm = pe.matmul(bank[7][0:RP, 256 + g:257 + g],
                                   rowbuf[0:1, 3, off + g * RP:off + (g + 1) * RP], one[:, :],
                                   start=True, stop=True)
                mm.then_inc(sem("tl_cin"), 1)

            def static_rows():
                pe.wait_ge(sem("ends_static"), 3)
                pe.wait_ge(sem("fold_used"), 7)
                for q in range(3):
                    if q:
                        if some("static_row", q):
                            pe.wait_ge(sem("static_row"), q)
                    for g in range(2):
                        mm = pe.matmul(bank[7][0:1, g * RP:(g + 1) * RP], ends[:, q, g:g + 1],
                                       eye[0:RP, 0:RP], start=True, stop=True)
                    mm.then_inc(sem("static_T"), 1)
                pe.wait_ge(sem("static_row"), 3)

            def node_product(X, src, weight, bias, done):
                if bias is not None:
                    pe.matmul(X[:, :], ones_b[:, :], brow[:, bias, :], start=True, stop=True)
                for j in range(4):
                    mm = pe.matmul(X[:, j * P:(j + 1) * P], src[:, j * P:(j + 1) * P], weight,
                                   start=bias is None, stop=True, skip_group_check=True)
                mm.then_inc(sem(done), 1)

            def node_step(h, par, lo, hi):
                p0, p1, p2, p3 = node_phases(h, par, lo, hi)
                if p3:
                    i = p3[0]
                    pe.wait_ge(sem("a_r"), i + 1)
                    if some("a_c2s", i):
                        pe.wait_ge(sem("a_c2s"), i)
                    node_product(bank[2], node_r, cen, None, "a_c2")
                if p1:
                    i = p1[0]
                    pe.wait_ge(sem("a_x1"), i + 1)
                    if some("a_x1T", i):
                        pe.wait_ge(sem("a_x1T"), i)
                    for j in range(4):
                        mm = pe.transpose(bank[3][:, j * P:(j + 1) * P], node_x1[:, j * P:(j + 1) * P], eye)
                    mm.then_inc(sem("a_T1"), 1)
                if p2:
                    i, b, k = p2
                    pe.wait_ge(sem("a_x2"), i + 1)
                    if some("a_r", i):
                        pe.wait_ge(sem("a_r"), i)
                    for j in range(4):
                        mm = pe.transpose(bank[4][:, j * P:(j + 1) * P], node_x2[b][:, j * P:(j + 1) * P], eye)
                    mm.then_inc(sem("a_T2"), 1)
                if p0:
                    i, b, k = p0
                    pe.wait_ge(sem(f"a_in{b}"), (k + 1) * 16)
                    if some("a_x1", i):
                        pe.wait_ge(sem("a_x1"), i)
                    node_product(bank[0], node_in[b], M0, 0, "a_c0")
                if p1:
                    i = p1[0]
                    pe.wait_ge(sem("a_x1T"), i + 1)
                    if some("a_x2", i):
                        pe.wait_ge(sem("a_x2"), i)
                    node_product(bank[1], node_x1T, M1, 1, "a_c1")
                if p2:
                    i = p2[0]
                    pe.wait_ge(sem("a_x2T"), i + 1)
                    pe.matmul(bank[4][:, :], W("app1"), node_x2T, start=True, stop=True).then_inc(sem("a_y"), 1)

            pe.wait_ge(sem("fold_used"), 7)

            def transpose_rows(stage, rows, dest):
                for j in range(4):
                    mm = pe.transpose(dest[:, j * P:(j + 1) * P],
                                      rows[:, 2 * j:2 * j + 2, :].rearrange("p s f -> p (s f)"), eye)
                mm.then_inc(sem(f"{stage}_T"), 1)

            def turn_D0(c, b, k):
                pe.wait_ge(sem(f"p0_rows{b}"), upto(f"p0_rows{b}", (k + 1) * ROWS))
                if some("p0_D", c - 1):
                    pe.wait_ge(sem("p0_D"), upto("p0_D", c - 1))
                transpose_rows("p0", XR[:, b, :, :], bank[5 + b])

            def stage1(c, b, k):
                node_step(k, b, 0, NB1)
                if not isinstance(c, int) or c > 1:
                    turn_D0(c, b, k)
            pe.wait_ge(sem("bias_rows"), 1)
            turn_D0(0, 0, 0)
            turn_D0(1, 1, 0)
            pe.wait_ge(sem("brow"), 3)
            run_chunks(pe, stage1, head=5)
            run_nodes_alone(pe, node_step)

            def tile_product(dest, terms, bias, done):
                if bias is not None:
                    pe.matmul(dest[:, :], ones_b[:, :], brow[:, bias, :], start=True, stop=True)
                for j in range(4):
                    for t, (src, weight) in enumerate(terms):
                        mm = pe.matmul(dest[:, j * P:(j + 1) * P], src(j), weight,
                                       start=bias is None and t == 0, stop=True,
                                       skip_group_check=True)
                mm.then_inc(sem(done), 1)

            def fixed(t):
                return lambda j: t[:, j * P:(j + 1) * P]

            def transpose_dn(stage, c, b, dest):
                pe.wait_ge(sem(f"{stage}_D"), upto(f"{stage}_D", c + 1))
                if some(f"{stage}_DT", c):
                    pe.wait_ge(sem(f"{stage}_DT"), upto(f"{stage}_DT", c))
                for j in range(4):
                    mm = pe.transpose(dest[:, j * P:(j + 1) * P], dn[b][:, j * P:(j + 1) * P], eye)
                mm.then_inc(sem(f"{stage}_T2"), 1)

            pe.wait_ge(sem("p0_D"), upto("p0_D", CH))
            pe.wait_ge(sem("a_c2s"), NB1)

            def l0(front, mid, back, tail):
                if mid:
                    c, b, k = mid
                    pe.wait_ge(sem("l0_h1"), upto("l0_h1", c + 1))
                    if some("l0_z2b", c):
                        pe.wait_ge(sem("l0_z2b"), upto("l0_z2b", c))
                    pe.matmul(bank[6][0:64, :], W("w2T", m=64), h1, start=True, stop=True
                              ).then_inc(sem("l0_z2"), 1)
                if front:
                    c, b, k = front
                    pe.wait_ge(sem("l0_dense"), upto("l0_dense", c + 1))
                    if some("l0_xsT", c):
                        pe.wait_ge(sem("l0_xsT"), upto("l0_xsT", c))
                    transpose_rows("l0", XR[:, b, :, :], bank[4])
                if mid:
                    c, b, k = mid
                    if some("l0_msg", c):
                        pe.wait_ge(sem("l0_msg"), upto("l0_msg", c))
                    pe.matmul(bank[3][:, :], W("w_srcT"), xsT[b], start=True, stop=True
                              ).then_inc(sem("l0_xs"), 1)
                    pe.wait_ge(sem("l0_h2"), upto("l0_h2", c + 1))
                    if some("l0_eg", c):
                        pe.wait_ge(sem("l0_eg"), upto("l0_eg", c))
                    pe.matmul(bank[7][:, :], W("w3rep", k=64), h2[0:64, :], start=True, stop=True
                              ).then_inc(sem("l0_e"), 1)
                if front:
                    c, b, k = front
                    pe.wait_ge(sem(f"l0_attr{b}"), upto(f"l0_attr{b}", (k + 1) * 16))
                    pe.wait_ge(sem("l0_xsT"), upto("l0_xsT", c + 1))
                    if some("l0_z1b", c):
                        pe.wait_ge(sem("l0_z1b"), upto("l0_z1b", c))
                    pe.matmul(bank[5][:, :], B1, D[:, cs(c)], start=True, stop=False)
                    pe.matmul(bank[5][:, :], edge1[:, :], attr[:, b, :], start=False, stop=False)
                    pe.matmul(bank[5][:, :], A1, xsT[b], start=False, stop=True).then_inc(sem("l0_z1"), 1)
                if mid:
                    c, b, k = mid
                    if some("l0_S", c):
                        pe.wait_ge(sem("l0_S"), upto("l0_S", c))
                    tile_product(bank[1], [(fixed(xsT[b]), M0)], 0, "l0_cS")
                if tail:
                    transpose_dn("l0", tail[0], tail[1], bank[2])
                if back:
                    c, b, k = back
                    pe.wait_ge(sem(f"l0_stream{b}"), upto(f"l0_stream{b}", (k + 1) * 32))
                    pe.wait_ge(sem("l0_scan"), upto("l0_scan", c * 2 + 2))
                    if some("l0_D", c):
                        pe.wait_ge(sem("l0_D"), upto("l0_D", c))
                    tile_product(bank[0], [(fixed(dT[:, b, :]), M0), (fixed(agg), cen)], 0, "l0_cD")
            run_pipe(pe, l0, 4)
            pe.wait_ge(sem("l0_eg"), upto("l0_eg", CH))
            static_rows()
            two_level(rt(4), P - 1, 0)
            two_level(rt(6), 0, 2)

            def l1a(c, b, k):
                pe.wait_ge(sem(f"l1a_rows{b}"), upto(f"l1a_rows{b}", (k + 1) * ROWS))
                if some("l1a_ST", c):
                    pe.wait_ge(sem("l1a_ST"), upto("l1a_ST", c))
                transpose_rows("l1a", XR[:, b, :, :], bank[5])
                nodes_beside(node_step, b, k, NB1)
                pe.wait_ge(sem("l1a_ST"), upto("l1a_ST", c + 1))
                if some("l1a_sc", c):
                    pe.wait_ge(sem("l1a_sc"), upto("l1a_sc", c))
                pe.wait_ge(sem(f"l1a_stream{b}"), upto(f"l1a_stream{b}", (k + 1) * 16))
                for j in range(4):
                    pe.matmul(bank[6][:, 2 * j:2 * j + 2], xsT[b][:, j * P:(j + 1) * P], attn_w[:, 0:2],
                              start=True, stop=True)
                for j in range(4):
                    mm = pe.matmul(bank[6][:, 8 + 2 * j:10 + 2 * j], dT[:, b, j * P:(j + 1) * P],
                                   attn_w[:, 2:4], start=True, stop=True)
                mm.then_inc(sem("l1a_s"), 1)
            pe.wait_ge(sem("l0_DT"), upto("l0_DT", CH))
            run_chunks(pe, l1a, head=5)

            pe.wait_ge(sem("l1_perm"), 2)
            pe.wait_ge(sem("l1a_ST"), upto("l1a_ST", CH))
            for q in range(2):
                for g in range(2):
                    mm = pe.transpose(bank[6][0:RP, (2 * q + g) * P:(2 * q + g + 1) * P],
                                      EB[:, 4 + q, g * RP:(g + 1) * RP], eye)
            mm.then_inc(sem("l1_run"), 1)
            two_level(rt(2), 0, 2)
            two_level(rt(0), P - 1, 0)
            two_level(rt(2), 0, 2)
            two_level(rt(0), P - 1, 0)
            two_level(rt(2), 0, 2)


            def l1b(front, back, tail, nodes=True):
                if front and nodes:
                    nodes_beside(node_step, front[1], front[2], NB1 + CH)
                if tail:
                    transpose_dn("l1b", tail[0], tail[1], bank[7])
                if back:
                    c, b, k = back
                    pe.wait_ge(sem("l1b_scan"), upto("l1b_scan", c * 2 + 2))
                    if some("l1b_D", c):
                        pe.wait_ge(sem("l1b_D"), upto("l1b_D", c))
                    tile_product(bank[6], [(fixed(dT[:, b, :]), M1), (fixed(agg), WOC)], 2, "l1b_cD")
                if front:
                    c, b, k = front
                    pe.wait_ge(sem(f"l1b_stream{b}"), upto(f"l1b_stream{b}", (k + 1) * 64))
                    if some("l1b_S", c):
                        pe.wait_ge(sem("l1b_S"), upto("l1b_S", c))
                    tile_product(bank[5], [(fixed(xsT[b]), M1)], 1, "l1b_cS")

            def l1b_alone(front, back, tail):
                l1b(front, back, tail, nodes=False)
            run_cut(pe, l1b, l1b_alone, 3, CUT, CUT + 4)
            pe.wait_ge(sem("l1b_DT"), upto("l1b_DT", CH))
            pe.wait_ge(sem("a_c2s"), NB)
            pe.wait_ge(sem("a_x2T"), NB)

            def l2(front, mid, back):
                if back:
                    c, b, k = back
                    pe.wait_ge(sem(f"l2_dT{b}"), upto(f"l2_dT{b}", (k + 1) * 16))
                    pe.wait_ge(sem("l2_rD"), upto("l2_rD", c + 1))
                    if some("l2_D", c):
                        pe.wait_ge(sem("l2_D"), upto("l2_D", c))
                    tile_product(bank[0], [(fixed(dT[:, b, :]), cen), (fixed(rD), cen)], None, "l2_cD")
                if front:
                    c, b, k = front
                    pe.wait_ge(sem(f"l2_rows{b}"), upto(f"l2_rows{b}", (k + 1) * ROWS))
                    if some("l2_xsT", c):
                        pe.wait_ge(sem("l2_xsT"), upto("l2_xsT", c))
                    transpose_rows("l2", XR[:, b, :, :], bank[4])
                if mid:
                    c, b, k = mid
                    pe.wait_ge(sem("l2_scan"), upto("l2_scan", c * 2 + 2))
                    if some("l2_rD", c):
                        pe.wait_ge(sem("l2_rD"), upto("l2_rD", c))
                    pe.matmul(bank[7][:, :], W("app1"), D[:, cs(c)], start=True, stop=False)
                    pe.matmul(bank[7][:, :], W("app2"), agg, start=False, stop=True).then_inc(sem("l2_yD"), 1)
                if front:
                    c, b, k = front
                    pe.wait_ge(sem("l2_xsT"), upto("l2_xsT", c + 1))
                    if some("l2_rS", c):
                        pe.wait_ge(sem("l2_rS"), upto("l2_rS", c))
                    pe.matmul(bank[6][:, :], W("app1"), xsT[b], start=True, stop=True).then_inc(sem("l2_yS"), 1)
                    pe.wait_ge(sem(f"l2_stream{b}"), upto(f"l2_stream{b}", (k + 1) * 32))
                    if some("l2_msg", c):
                        pe.wait_ge(sem("l2_msg"), upto("l2_msg", c))
                    pe.matmul(bank[5][:, :], W("msg1"), xsT[b], start=True, stop=False)
                    pe.matmul(bank[5][:, :], W("msg2", k=64), stream2[b][0:F, :], start=False, stop=True
                              ).then_inc(sem("l2_m"), 1)
                    pe.wait_ge(sem("l2_rS"), upto("l2_rS", c + 1))
                    if some("l2_addS", c):
                        pe.wait_ge(sem("l2_addS"), upto("l2_addS", c))
                    tile_product(bank[1], [(fixed(rS), cen)], None, "l2_cS")
            run_pipe(pe, l2, 3)

            pe.wait_ge(sem("l2_D"), upto("l2_D", CH))

            def l3(front, mid, back, scattered):
                if mid:
                    c, b, k = mid
                    if some("l3_scan", (c - 1) * 2):
                        pe.wait_ge(sem("l3_scan"), upto("l3_scan", (c - 1) * 2))
                    for q in range(REL // 2):
                        pe.wait_ge(sem("l3_mask"), upto("l3_mask", c * REL + (2 * q + 2)))
                        for h in range(2):
                            mm = pe.matmul(bank[6 + b][h * F:(h + 1) * F, :], relw[:, q, :],
                                           NT[:, 4 * h + q % 4, :], start=q == 0, stop=q == REL // 2 - 1)
                        mm.then_inc(sem("l3_pair"), 1)
                        if q == 3 and back:
                            pe.wait_ge(sem("l3_rD"), upto("l3_rD", back[0] + 1))
                            if some("l3_addD", back[0]):
                                pe.wait_ge(sem("l3_addD"), upto("l3_addD", back[0]))
                            tile_product(bank[0], [(fixed(rD), cen)], None, "l3_cD")
                        if q == 5 and front:
                            l3_turn(*front)
                else:
                    if back:
                        pe.wait_ge(sem("l3_rD"), upto("l3_rD", back[0] + 1))
                        if some("l3_addD", back[0]):
                            pe.wait_ge(sem("l3_addD"), upto("l3_addD", back[0]))
                        tile_product(bank[0], [(fixed(rD), cen)], None, "l3_cD")
                    if front:
                        l3_turn(*front)

            def l3_turn(c, b, k):
                pe.wait_ge(sem("l3_xw"), upto("l3_xw", c + 1))
                if some("l3_xAB", c * 2):
                    pe.wait_ge(sem("l3_xAB"), upto("l3_xAB", c * 2))
                for h in range(2):
                    for j in range(4):
                        mm = pe.transpose(bank[4 + h][:, j * P:(j + 1) * P],
                                          xw2[:, (2 * j + h) * P:(2 * j + h + 1) * P], eye)
                    mm.then_inc(sem("l3_T"), 1)
            run_pipe(pe, l3, 4)

        @block.scalar
        def _(act):
            act.wait_ge(sem("consts"), 6)

            def deviation(dest, ss, final, p=P):
                scale = (1.0 + EPS) / F if final else 1.0 / F
                return act.activation(dest, ss, ACT.Sqrt, bias=epsc[:, 1:2] if final else epsc[:, 0:1],
                                      scale=scale)

            def node_square(p, layer):
                i, b, k = p
                act.wait_ge(sem(("a_c0", "a_c1", "a_c2s")[layer]), upto(("a_c0", "a_c1", "a_c2s")[layer], i + 1))
                if some(f"a_ss{layer}", i):
                    act.wait_ge(sem(f"a_ss{layer}"), i)
                act.activation(node_sq[layer], node_out[b] if layer == 2 else bank[layer][:, :], ACT.Square
                               ).then_inc(sem(f"a_sq{layer}"), 1)

            def node_deviation(p, layer):
                act.wait_ge(sem(f"a_ss{layer}"), p[0] + 1)
                if some(f"a_rs{layer}", p[0]):
                    act.wait_ge(sem(f"a_rs{layer}"), p[0])
                deviation(asmall[:, layer, 1, :], asmall[:, layer, 0, :], layer == 2
                          ).then_inc(sem(f"a_sd{layer}"), 1)

            def node_turned(h, par, lo, hi):
                p0, p1, p2, p3 = node_phases(h, par, lo, hi)
                if p1:
                    act.wait_ge(sem("a_T1"), p1[0] + 1)
                    if some("a_c1", p1[0]):
                        act.wait_ge(sem("a_c1"), p1[0])
                    act.activation(node_x1T, bank[3][:, :], ACT.Copy).then_inc(sem("a_x1T"), 1)
                if p2:
                    act.wait_ge(sem("a_T2"), p2[0] + 1)
                    if some("a_y", p2[0]):
                        act.wait_ge(sem("a_y"), p2[0])
                    act.activation(node_x2T, bank[4][:, :], ACT.Copy).then_inc(sem("a_x2T"), 1)

            def node_rest(h, par, lo, hi):
                p0, p1, p2, p3 = node_phases(h, par, lo, hi)
                if p3:
                    node_square(p3, 2)
                if p0:
                    node_square(p0, 0)
                if p3:
                    node_deviation(p3, 2)
                if p1:
                    node_square(p1, 1)
                if p0:
                    node_deviation(p0, 0)
                if p1:
                    node_deviation(p1, 1)
                if p2:
                    act.wait_ge(sem("a_y"), p2[0] + 1)
                    if some("a_c2", p2[0]):
                        act.wait_ge(sem("a_c2"), p2[0])
                    act.activation(node_r, bank[4][:, :], ACT.Relu, bias=col("app_b")).then_inc(sem("a_r"), 1)

            def node_step(h, par, lo, hi):
                node_turned(h, par, lo, hi)
                node_rest(h, par, lo, hi)

            act.wait_ge(sem("weights_in"), 64)

            def stage1(c, b, k):
                node_step(k, b, 0, NB1)
                act.wait_ge(sem("p0_T"), upto("p0_T", c + 1))
                act.activation(D[:, cs(c)], bank[5 + b][:, :], ACT.Copy).then_inc(sem("p0_D"), 1)
            run_chunks(act, stage1, head=5)
            run_nodes_alone(act, node_step)

            def ln_square(stage, who, src, dest, after, c):
                act.wait_ge(sem(after), upto(after, c + 1))
                if some(f"{stage}_ss{who}", c):
                    act.wait_ge(sem(f"{stage}_ss{who}"), upto(f"{stage}_ss{who}", c))
                act.activation(dest, src, ACT.Square).then_inc(sem(f"{stage}_sq{who}"), 1)

            def ln_dev(stage, who, c):
                act.wait_ge(sem(f"{stage}_ss{who}"), upto(f"{stage}_ss{who}", c + 1))
                if some(f"{stage}_rs{who}", c):
                    act.wait_ge(sem(f"{stage}_rs{who}"), upto(f"{stage}_rs{who}", c))
                i = "DS".index(who)
                deviation(small[:, i, 1, :], small[:, i, 0, :], False).then_inc(sem(f"{stage}_sd{who}"), 1)

            def store_tab(l, stage, c, b, k):
                act.wait_ge(sem(f"{stage}_D"), upto(f"{stage}_D", c + 1))
                act.dma_start(dtab[l - 1][bass.ds(c * 1024, 1024), :].rearrange("(p s) f -> p (s f)", p=P),
                              dn[b]).then_inc(sem(f"tab{l}_st{b}"), 16)

            def turn_D(stage, c, turned):
                act.wait_ge(sem(f"{stage}_T2"), upto(f"{stage}_T2", c + 1))
                act.activation(D[:, cs(c)], turned[:, :], ACT.Copy).then_inc(sem(f"{stage}_DT"), 1)

            def densify(c, b, k):
                act.wait_ge(sem(f"l0_rows{b}"), upto(f"l0_rows{b}", (k + 1) * ROWS))
                if some("l0_T", c - 1):
                    act.wait_ge(sem("l0_T"), upto("l0_T", c - 1))
                act.activation(XR[:, b, :, :], XM[:, b, :, 0:F], ACT.Copy).then_inc(sem("l0_dense"), 1)

            def l0(front, mid, back, tail):
                if front and isinstance(front[0], int) and front[0] == 0:
                    densify(*front)
                if mid:
                    c, b, k = mid
                    act.wait_ge(sem("l0_z2"), upto("l0_z2", c + 1))
                    if some("l0_h2", c):
                        act.wait_ge(sem("l0_h2"), upto("l0_h2", c))
                    act.activation(z2[0:64, :], bank[6][0:64, :], ACT.Identity, bias=col("b2", 64)
                                   ).then_inc(sem("l0_z2b"), 1)
                if tail:
                    ln_square("l0", "D", bank[0][:, :], sqD, "l0_cD", tail[0])
                if front:
                    c, b, k = front
                    act.wait_ge(sem("l0_T"), upto("l0_T", c + 1))
                    if some("l0_cS", c - 1):
                        act.wait_ge(sem("l0_cS"), upto("l0_cS", c - 1))
                    act.activation(xsT[b], bank[4][:, :], ACT.Copy).then_inc(sem("l0_xsT"), 1)
                if tail:
                    ln_dev("l0", "D", tail[0])
                if mid:
                    c, b, k = mid
                    act.wait_ge(sem("l0_e"), upto("l0_e", c + 1))
                    act.activation(eg, bank[7][:, :], ACT.Relu, bias=col("b3")).then_inc(sem("l0_eg"), 1)
                if front:
                    c, b, k = front
                    act.wait_ge(sem("l0_z1"), upto("l0_z1", c + 1))
                    if some("l0_h1", c):
                        act.wait_ge(sem("l0_h1"), upto("l0_h1", c))
                    act.activation(z1, bank[5][:, :], ACT.Identity, bias=fcol[:, 0:1]).then_inc(sem("l0_z1b"), 1)
                if mid:
                    ln_square("l0", "S", bank[1][:, :], sqS, "l0_cS", mid[0])
                if front and not last(front[0]):
                    c, b, k = front
                    densify(c + 1, 1 - b, k + b)
                if mid:
                    ln_dev("l0", "S", mid[0])
                if tail:
                    store_tab(1, "l0", *tail)
                    turn_D("l0", tail[0], bank[2])

            def last(c):
                return isinstance(c, int) and c == CH - 1
            act.wait_ge(sem("fold_used"), 7)
            run_ahead(act, l0, 4)

            def copy_ring(stage, c, b):
                act.activation(XR[:, b, :, :], rows64(S[:, cs(c)]), ACT.Copy).then_inc(sem(f"{stage}_copy"), 1)

            def l1a(c, b, k):
                act.wait_ge(sem("l1a_T"), upto("l1a_T", c + 1))
                if some(f"l1a_stored{b}", k * 16):
                    act.wait_ge(sem(f"l1a_stored{b}"), upto(f"l1a_stored{b}", k * 16))
                if some("l1a_s", c - 1):
                    act.wait_ge(sem("l1a_s"), upto("l1a_s", c - 1))
                act.activation(xsT[b], bank[5][:, :], ACT.Copy).then_inc(sem("l1a_ST"), 1)
                if not (isinstance(c, int) and c >= CH - 2):
                    copy_ring("l1a", c + 2, b)
                nodes_beside(node_step, b, k, NB1)

            act.wait_ge(sem("l0_T"), upto("l0_T", CH))
            act.wait_ge(sem("l0_q"), upto("l0_q", CH))
            act.wait_ge(sem("l0_S"), upto("l0_S", CH))
            copy_ring("l1a", 0, 0)
            copy_ring("l1a", 1, 1)
            run_chunks(act, l1a, head=5, tail=2)

            act.wait_ge(sem("l1_dve"), 1)
            act.activation(rt(3), rt(3), ACT.Gelu, bias=fcol[0:RP, 2:3]).then_inc(sem("l1_act"), 1)
            act.wait_ge(sem("l1_dve"), 2)
            act.activation(rt(3), rt(3), ACT.Exp).then_inc(sem("l1_act"), 1)

            def l1b(front, back, tail, nodes=True):
                if tail:
                    ln_square("l1b", "D", bank[6][:, :], sqD, "l1b_cD", tail[0])
                if back:
                    ln_square("l1b", "S", bank[5][:, :], sqS, "l1b_cS", back[0])
                if front and nodes:
                    nodes_beside(node_turned, front[1], front[2], NB1 + CH)
                if tail:
                    ln_dev("l1b", "D", tail[0])
                if back:
                    ln_dev("l1b", "S", back[0])
                if front and nodes:
                    nodes_beside(node_rest, front[1], front[2], NB1 + CH)
                if tail:
                    store_tab(2, "l1b", *tail)
                    turn_D("l1b", tail[0], bank[7])

            def l1b_alone(front, back, tail):
                l1b(front, back, tail, nodes=False)
            run_cut(act, l1b, l1b_alone, 3, CUT, CUT + 4)
            act.wait_ge(sem("a_stored0"), 16 * (NB // 2))
            act.wait_ge(sem("a_stored1"), 16 * (NB // 2))

            def l2(front, mid, back):
                if front and not last(front[0]):
                    c, b, k = front
                    if some("l2_T", c):
                        act.wait_ge(sem("l2_T"), upto("l2_T", c))
                    if some("l2_addS", c):
                        act.wait_ge(sem("l2_addS"), upto("l2_addS", c))
                    copy_ring("l2", c + 1, 1 - b)
                if mid:
                    ln_square("l2", "S", cadd, sqS, "l2_addS", mid[0])
                if back:
                    ln_square("l2", "D", bank[0][:, :], sqD, "l2_cD", back[0])
                if front:
                    c, b, k = front
                    act.wait_ge(sem("l2_T"), upto("l2_T", c + 1))
                    if some("l2_cS", c - 1):
                        act.wait_ge(sem("l2_cS"), upto("l2_cS", c - 1))
                    if some("l2_m", c - 1):
                        act.wait_ge(sem("l2_m"), upto("l2_m", c - 1))
                    act.activation(xsT[b], bank[4][:, :], ACT.Copy).then_inc(sem("l2_xsT"), 1)
                if mid:
                    ln_dev("l2", "S", mid[0])
                if back:
                    ln_dev("l2", "D", back[0])
                if mid:
                    act.wait_ge(sem("l2_yD"), upto("l2_yD", mid[0] + 1))
                    if some("l2_cD", mid[0]):
                        act.wait_ge(sem("l2_cD"), upto("l2_cD", mid[0]))
                    act.activation(rD, bank[7][:, :], ACT.Relu, bias=fcol[:, 1:2]).then_inc(sem("l2_rD"), 1)
                if front:
                    c, b, k = front
                    act.wait_ge(sem("l2_yS"), upto("l2_yS", c + 1))
                    if some("l2_cS", c):
                        act.wait_ge(sem("l2_cS"), upto("l2_cS", c))
                    act.activation(rS, bank[6][:, :], ACT.Relu, bias=col("app_b")).then_inc(sem("l2_rS"), 1)
                if back:
                    c, b, k = back
                    store_tab(3, "l2", c, b, k)
                    act.wait_ge(sem(f"l2_dT{b}"), upto(f"l2_dT{b}", (k + 1) * 16))
                    act.activation(D[:, cs(c)], dn[b], ACT.Copy).then_inc(sem("l2_keepD"), 1)
            act.wait_ge(sem("l1b_S"), upto("l1b_S", CH))
            copy_ring("l2", 0, 0)
            run_ahead(act, l2, 3)

            def l3(front, mid, back, scattered):
                if front and not last(front[0]):
                    c, b, k = front
                    if some("l3_xw", c):
                        act.wait_ge(sem("l3_xw"), upto("l3_xw", c))
                    copy_ring("l3", c + 1, 1 - b)
                if back:
                    c, b, k = back
                    act.wait_ge(sem("l3_scan"), upto("l3_scan", c * 2 + 2))
                    if some("l3_cD", c):
                        act.wait_ge(sem("l3_cD"), upto("l3_cD", c))
                    act.activation(rD, agg, ACT.Relu).then_inc(sem("l3_rD"), 1)
                    ln_square("l3", "D", eg, sqD, "l3_addD", c)
                    ln_dev("l3", "D", c)
                if front:
                    c, b, k = front
                    for h in range(2):
                        act.wait_ge(sem("l3_T"), upto("l3_T", c * 2 + (h + 1)))
                        if some("l3_mask", c * REL):
                            act.wait_ge(sem("l3_mask"), upto("l3_mask", c * REL))
                        act.activation((z1, h1)[h], bank[4 + h][:, :], ACT.Copy).then_inc(sem("l3_xAB"), 1)
            act.wait_ge(sem("l2_S"), upto("l2_S", CH))
            act.wait_ge(sem("l2_T"), upto("l2_T", CH))
            copy_ring("l3", 0, 0)
            run_ahead(act, l3, 4)

        @block.vector
        def _(dve):
            def put_indices(stage, index, c, b):
                dve.tensor_copy(idx_st[:, b, :], index[:, tc(c)]).then_inc(sem(f"{stage}_idx"), 1)

            def put_first_indices(stage, index, prev=None):
                for b in range(2):
                    if prev:
                        if some(f"{prev}_rows{b}", ROWS * (CH // 2 + 1 - b)):
                            dve.wait_ge(sem(f"{prev}_rows{b}"), upto(f"{prev}_rows{b}", ROWS * (CH // 2 + 1 - b)))
                    put_indices(stage, index, b, b)

            def put_next_indices(stage, index, c, b, k):
                if not (isinstance(c, int) and c >= CH - 2):
                    dve.wait_ge(sem(f"{stage}_rows{b}"), upto(f"{stage}_rows{b}", (k + 1) * ROWS))
                    put_indices(stage, index, c + 2, b)

            dve.wait_ge(sem("dstc_in"), 16)
            put_first_indices("p0", dstc)
            dve.wait_ge(sem("weights_in"), 64)
            dve.tensor_tensor(W("w_tgtI"), W("w_tgt"), eye, ALU.add).then_inc(sem("eye_plus"), 1)
            dve.tensor_tensor(W("res_wT"), W("res_wT"), eye, ALU.add).then_inc(sem("eye_plus"), 1)
            fl = [sqD[:, 0:TILES], sqS[:, 0:TILES], dn[0][:, 0:TILES]]
            dve.wait_ge(sem("dstc_in"), 16)
            dve.wait_ge(sem("index_in"), 64)
            dve.tensor_tensor(fl[0], dstc[:, :], nxtc[:, :], ALU.is_equal).then_inc(sem("nm_flags"), 1)
            dve.wait_ge(sem("nm_flags"), 1)
            dve.scalar_tensor_tensor(fl[1], fl[0], float(NO_ROW), dstc[:, :], ALU.mult, ALU.add
                                     ).then_inc(sem("nm_flags"), 1)
            dve.wait_ge(sem("nm_flags"), 2)
            dve.tensor_copy(outc[:, :], fl[1]).then_inc(sem("nm_flags"), 1)
            dve.tensor_scalar(fl[2], dstc[:, :], float(F + 1), float(F), ALU.mult, ALU.add
                              ).then_inc(sem("nm_flags"), 1)
            dve.wait_ge(sem("nm_flags"), 4)
            dve.scalar_tensor_tensor(fl[2], fl[0], float(8 * NO_ROW), fl[2], ALU.mult, ALU.add
                                     ).then_inc(sem("nm_flags"), 1)
            dve.wait_ge(sem("nm_flags"), 5)
            dve.tensor_copy(cellc[:, :], fl[2]).then_inc(sem("cells"), 1)
            dve.wait_ge(sem("runs_in"), 48)
            keep, cont, rep, pen = (runs[:, i, :, :] for i in range(4))
            dve.tensor_tensor(keep, rt(1).bitcast(I32), rt(0).bitcast(I32), ALU.is_equal).then_inc(sem("keep_run"), 1)
            dve.tensor_tensor(cont, rt(1).bitcast(I32), rt(2).bitcast(I32), ALU.is_equal).then_inc(sem("flags"), 1)
            dve.wait_ge(sem("keep_run"), 1)
            dve.wait_ge(sem("flags"), 1)
            dve.tensor_scalar(rep, cont, -1.0, 1.0, ALU.mult, ALU.add).then_inc(sem("flags"), 1)
            dve.tensor_scalar(pen, keep, -NEG, NEG, ALU.mult, ALU.add).then_inc(sem("flags"), 1)
            dve.wait_ge(sem("flags"), 3)
            for q, a in enumerate((keep, cont, pen)):
                dve.tensor_reduce(ends[:, q, :], a, AX.X, ALU.min).then_inc(sem("ends_static"), 1)
            dve.wait_ge(sem("fold"), 3)
            dve.tensor_copy(folded[:, 0:4, :], bank[6][:, :].rearrange("p (n m) -> p n m", n=4)
                            ).then_inc(sem("fold_used"), 1)
            dve.tensor_copy(WOC, bank[7][:, 0:128]).then_inc(sem("fold_used"), 1)
            dve.tensor_copy(edge1[:, :], bank[7][0:16, 128:256]).then_inc(sem("fold_used"), 1)
            dve.tensor_copy(attn_w[:, :], bank[7][:, 256:260]).then_inc(sem("fold_used"), 1)
            dve.tensor_tensor(fcol[:, 0:1], bank[7][:, 260:261], col("b1"), ALU.add).then_inc(sem("fold_used"), 1)
            dve.tensor_tensor(fcol[:, 1:2], bank[7][:, 261:262], col("app_b"), ALU.add).then_inc(sem("fold_used"), 1)
            dve.tensor_copy(fcol[:, 2:3], bank[7][:, 262:263]).then_inc(sem("fold_used"), 1)
            put_next_indices("p0", dstc, 0, 0, 0)
            full = msg[:, 0:3 * P].rearrange("p (n m) -> p n m", n=3)
            dve.wait_ge(sem("consts"), 6)
            dve.tensor_copy(full, bank[5][:, 0:3 * P].rearrange("p (n m) -> p n m", n=3)).then_inc(sem("bias_rows"), 1)
            dve.wait_ge(sem("bias_rows"), 1)
            dve.tensor_tensor(full[:, 2, :], full[:, 2, :], full[:, 1, :], ALU.add).then_inc(sem("bias_rows"), 1)
            for part in range(3):
                r0 = 32 * part
                dve.wait_ge(sem("bias_rows"), 2 + 2 * part)
                for rr in range(4):
                    dv = dve.tensor_copy(brow[r0:r0 + 1, :, rr * P:(rr + 1) * P], full[r0:r0 + 1, :, :])
                dv.then_inc(sem("brow"), 1)
                if part < 2:
                    dve.tensor_copy(parts_b := h2[:, 0:192].bitcast(BF16).rearrange("p (n m) -> p n m", n=3), full
                                    ).then_inc(sem("bias_rows"), 1)
                    dve.wait_ge(sem("bias_rows"), 3 + 2 * part)
                    dve.wait_ge(sem("brow"), part + 1)
                    dve.tensor_tensor(full, full, parts_b, ALU.subtract).then_inc(sem("bias_rows"), 1)

            tls = [0]

            def two_level(a, d0, d1, op0, op1, start, coef, reverse):
                n = tls[0]
                tls[0] += 1

                def way(t):
                    return t[:, ::-1] if reverse else t[:, :]
                if n:
                    if some("tl_done", 2 * n):
                        dve.wait_ge(sem("tl_done"), 2 * n)
                dve.tensor_tensor_scan(way(a[:, 0, :]), way(d0[:, 0, :]), way(d1[:, 0, :]), start, op0, op1
                                       ).then_inc(sem("tl_loc"), 1)
                dve.tensor_tensor_scan(way(a[:, 1, :]), way(d0[:, 1, :]), way(d1[:, 1, :]), start, op0, op1
                                       ).then_inc(sem("tl_ends"), 1)
                dve.memset(rowbuf[0:1, 3, :], start).then_inc(sem("tl_init"), 1)
                dve.wait_ge(sem("tl_init"), n + 1)
                dve.wait_ge(sem("tl_row"), n + 1)
                dve.tensor_tensor_scan(way(rowbuf[0:1, 3, 1:TILES + 1]), way(rowbuf[0:1, coef, 0:TILES]),
                                       way(bank[7][0:1, 0:TILES]), start, op0, op1).then_inc(sem("tl_carry"), 1)
                dve.wait_ge(sem("tl_cin"), n + 1)
                dve.tensor_copy(ends[:, 3, :], bank[7][0:RP, 256:258]).then_inc(sem("tl_cin_sb"), 1)
                dve.wait_ge(sem("tl_cin_sb"), n + 1)
                for g in range(2):
                    dve.tensor_tensor_scan(way(a[:, g, :]), way(d0[:, g, :]), way(d1[:, g, :]),
                                           ends[:, 3, g:g + 1], op0, op1).then_inc(sem("tl_done"), 1)
                dve.wait_ge(sem("tl_done"), 2 * n + 2)

            lasts = [0]

            def last_to_run(dest, src, tmp):
                lasts[0] += 1
                dve.tensor_tensor(tmp, src, rep, ALU.mult).then_inc(sem("rep_only"), 1)
                if some("rep_only", lasts[0]):
                    dve.wait_ge(sem("rep_only"), lasts[0])
                two_level(dest, cont, tmp, ALU.mult, ALU.add, 0.0, 1, True)

            def ln_apply(dest, src, rs):
                return dve.tensor_tensor(rows64(dest), rows64(src), bcast8(rs), ALU.mult)

            def node_sum(p, layer):
                dve.wait_ge(sem(f"a_sq{layer}"), p[0] + 1)
                dve.tensor_reduce(asmall[:, layer, 0, :], rows64(node_sq[layer]), AX.X, ALU.add
                                  ).then_inc(sem(f"a_ss{layer}"), 1)

            def node_inverse(p, layer):
                dve.wait_ge(sem(f"a_sd{layer}"), p[0] + 1)
                dve.reciprocal(asmall[:, layer, 2, :], asmall[:, layer, 1, :]).then_inc(sem(f"a_rs{layer}"), 1)
                dve.wait_ge(sem(f"a_rs{layer}"), p[0] + 1)

            def node_added(h, par, lo, hi):
                p0, p1, p2, p3 = node_phases(h, par, lo, hi)
                if p3:
                    i, b, k = p3
                    dve.wait_ge(sem("a_c2"), i + 1)
                    if some(f"a_stored{b}", k * 16):
                        dve.wait_ge(sem(f"a_stored{b}"), k * 16)
                    dve.tensor_tensor(node_out[b], bank[2][:, :], node_x2[b], ALU.add).then_inc(sem("a_c2s"), 1)

            def node_rest(h, par, lo, hi, last_product=True):
                p0, p1, p2, p3 = node_phases(h, par, lo, hi)
                if p3:
                    node_sum(p3, 2)
                if p0:
                    node_sum(p0, 0)
                if p3:
                    if not last_product:
                        if some("a_out", p3[0]):
                            dve.wait_ge(sem("a_out"), p3[0])
                    node_inverse(p3, 2)
                if p1:
                    node_sum(p1, 1)
                if p0:
                    node_inverse(p0, 0)
                    if some("a_T1", p0[0]):
                        dve.wait_ge(sem("a_T1"), p0[0])
                    ln_apply(node_x1, bank[0][:, :], asmall[:, 0, 2, :]).then_inc(sem("a_x1"), 1)
                if p1:
                    i, b, k = p1
                    node_inverse(p1, 1)
                    if some("a_T2", i - 1):
                        dve.wait_ge(sem("a_T2"), i - 1)
                    ln_apply(node_x2[b], bank[1][:, :], asmall[:, 1, 2, :]).then_inc(sem("a_x2"), 1)
                if p3 and last_product:
                    ln_apply(node_out[p3[1]], node_out[p3[1]], asmall[:, 2, 2, :]).then_inc(sem("a_out"), 1)

            def node_rest_beside(h, par, lo, hi):
                node_rest(h, par, lo, hi, last_product=False)

            def node_step(h, par, lo, hi):
                node_added(h, par, lo, hi)
                node_rest(h, par, lo, hi)

            def count_edges():
                for q in range(3):
                    dve.wait_ge(sem("static_T"), q + 1)
                    dve.tensor_copy(rowbuf[0:1, q, 0:TILES], bank[7][0:1, 0:TILES]).then_inc(sem("static_row"), 1)
                dve.wait_ge(sem("static_row"), 3)

                dve.memset(rt(5), 1.0).then_inc(sem("unit"), 1)
                dve.wait_ge(sem("unit"), 1)
                two_level(rt(4), keep, rt(5), ALU.mult, ALU.add, 0.0, 0, False)
                last_to_run(rt(6), rt(4), rt(5))
                dve.reciprocal(rt(7), rt(6)).then_inc(sem("inv_run"), 1)

            def stage1(c, b, k):
                node_step(k, b, 0, NB1)
                if not isinstance(c, int) or c > 1:
                    put_next_indices("p0", dstc, c, b, k)
            put_next_indices("p0", dstc, 1, 1, 0)
            run_chunks(dve, stage1, head=5, tail=2)
            dve.wait_ge(sem("index_in"), 64)
            put_first_indices("l0", srcc, "p0")
            run_nodes_alone(dve, node_step)

            def ln_reduce(stage, who, src, c):
                i = "DS".index(who)
                dve.wait_ge(sem(f"{stage}_sq{who}"), upto(f"{stage}_sq{who}", c + 1))
                dve.tensor_reduce(small[:, i, 0, :], rows64(src), AX.X, ALU.add).then_inc(sem(f"{stage}_ss{who}"), 1)

            def ln_inverse(stage, who, c):
                i = "DS".index(who)
                dve.wait_ge(sem(f"{stage}_sd{who}"), upto(f"{stage}_sd{who}", c + 1))
                dve.reciprocal(small[:, i, 2, :], small[:, i, 1, :]).then_inc(sem(f"{stage}_rs{who}"), 1)
                dve.wait_ge(sem(f"{stage}_rs{who}"), upto(f"{stage}_rs{who}", c + 1))

            def scan_half(stage, c, b, data, h):
                a, z, o = h * F, (h + 1) * F, (1 - h) * F
                dve.wait_ge(sem(f"{stage}_carry"), upto(f"{stage}_carry", c * 2 + h))
                dve.tensor_tensor_scan(agg[a:z, :], stream[a:z, 0, b, :], data[a:z, :],
                                       carry[a:z, :], ALU.mult, ALU.add).then_inc(sem(f"{stage}_scan"), 1)
                dve.wait_ge(sem(f"{stage}_scan"), upto(f"{stage}_scan", c * 2 + (h + 1)))
                dve.tensor_copy(carry[o:o + F, :], agg[a:z, CW - 1:CW]).then_inc(sem(f"{stage}_carry"), 1)

            def l0(front, mid, back, tail):
                if front:
                    c, b, k = front
                    dve.wait_ge(sem(f"l0_rows{b}"), upto(f"l0_rows{b}", (k + 1) * ROWS))
                    dve.tensor_copy(qcol[:, tc(c)].rearrange("p (s o) -> p s o", o=1), XM[:, b, :, F:F + 1]
                                    ).then_inc(sem("l0_q"), 1)
                    put_next_indices("l0", srcc, c, b, k)
                if back:
                    c, b, k = back
                    dve.wait_ge(sem("l0_msg"), upto("l0_msg", c + 1))
                    dve.wait_ge(sem(f"l0_stream{b}"), upto(f"l0_stream{b}", (k + 1) * 32))
                    if some("l0_cD", c):
                        dve.wait_ge(sem("l0_cD"), upto("l0_cD", c))
                    scan_half("l0", c, b, msg, 0)
                if mid:
                    c, b, k = mid
                    dve.wait_ge(sem("l0_z2b"), upto("l0_z2b", c + 1))
                    dve.scalar_tensor_tensor(h2[0:64, :], z2[0:64, :], SLOPE, z2[0:64, :], ALU.mult, ALU.max
                                             ).then_inc(sem("l0_h2"), 1)
                if back:
                    scan_half("l0", back[0], back[1], msg, 1)
                if tail:
                    ln_reduce("l0", "D", sqD, tail[0])
                if mid:
                    c, b, k = mid
                    dve.wait_ge(sem("l0_eg"), upto("l0_eg", c + 1))
                    dve.wait_ge(sem("l0_xs"), upto("l0_xs", c + 1))
                    dve.scalar_tensor_tensor(msg, bank[3][:, :], col("b_src"), eg, ALU.add, ALU.mult
                                             ).then_inc(sem("l0_msg"), 1)
                if tail:
                    c, b, k = tail
                    ln_inverse("l0", "D", c)
                    if some(f"tab1_st{b}", k * 16):
                        dve.wait_ge(sem(f"tab1_st{b}"), k * 16)
                    if some("l0_T2", c - 1):
                        dve.wait_ge(sem("l0_T2"), upto("l0_T2", c - 1))
                    ln_apply(dn[b], bank[0][:, :], small[:, 0, 2, :]).then_inc(sem("l0_D"), 1)
                if front:
                    c, b, k = front
                    dve.wait_ge(sem("l0_z1b"), upto("l0_z1b", c + 1))
                    if some("l0_z2", c):
                        dve.wait_ge(sem("l0_z2"), upto("l0_z2", c))
                    dve.scalar_tensor_tensor(h1, z1, SLOPE, z1, ALU.mult, ALU.max).then_inc(sem("l0_h1"), 1)
                if mid:
                    c, b, k = mid
                    ln_reduce("l0", "S", sqS, c)
                    ln_inverse("l0", "S", c)
                    ln_apply(S[:, cs(c)], bank[1][:, :], small[:, 1, 2, :]).then_inc(sem("l0_S"), 1)
            run_ahead(dve, l0, 4)
            dve.wait_ge(sem("l0_q"), upto("l0_q", CH))
            put_first_indices("l1a", qcol, "l0")
            count_edges()

            def l1a(c, b, k):
                put_next_indices("l1a", qcol, c, b, k)
                nodes_beside(node_step, b, k, NB1)
                dve.wait_ge(sem("l1a_s"), upto("l1a_s", c + 1))
                dve.tensor_copy(sc[:, :, tc(c)], bank[6][:, 0:16].rearrange("p (q s) -> p q s", q=2)
                                ).then_inc(sem("l1a_sc"), 1)
            run_chunks(dve, l1a, head=5, tail=2)
            put_first_indices("l2", qcol, "l1a")

            dve.wait_ge(sem("l1a_sc"), upto("l1a_sc", CH))
            dve.wait_ge(sem("l0_e"), upto("l0_e", CH))
            for q in range(2):
                dve.tensor_copy(EB[:, 4 + q, 0:TILES].rearrange("p (c h j) -> p c h j", h=2, j=4),
                                sc[:, q, :].rearrange("p (c j h) -> p c h j", h=2, j=4)).then_inc(sem("l1_perm"), 1)
            dve.wait_ge(sem("l1_run"), 1)
            dve.wait_ge(sem("l1a_stored0"), upto("l1a_stored0", 16 * (CH // 2 + 1)))
            dve.wait_ge(sem("l1a_stored1"), upto("l1a_stored1", 16 * (CH // 2)))
            dve.wait_ge(sem("tab1_st0"), 16)
            s_src = bank[6][0:RP, 0:2 * P].rearrange("p (g n) -> p g n", g=2)
            s_dst = bank[6][0:RP, 2 * P:4 * P].rearrange("p (g n) -> p g n", g=2)
            last_to_run(rt(2), s_dst, rt(1))
            dve.tensor_tensor(rt(3), s_src, rt(2), ALU.add).then_inc(sem("l1_dve"), 1)
            dve.wait_ge(sem("l1_act"), 1)
            two_level(rt(0), pen, rt(3), ALU.add, ALU.max, NEG, 2, False)
            last_to_run(rt(2), rt(0), rt(1))
            dve.tensor_tensor(rt(3), rt(3), rt(2), ALU.subtract).then_inc(sem("l1_dve"), 1)
            dve.wait_ge(sem("l1_act"), 2)
            two_level(rt(0), keep, rt(3), ALU.mult, ALU.add, 0.0, 0, False)
            last_to_run(rt(2), rt(0), rt(1))
            dve.tensor_scalar(rt(2), rt(2), 1e-20, None, ALU.max).then_inc(sem("l1_den"), 1)
            dve.wait_ge(sem("l1_den"), 1)
            dve.reciprocal(rt(1), rt(2)).then_inc(sem("l1_den"), 1)
            dve.wait_ge(sem("l1_den"), 2)
            dve.tensor_tensor(rt(3), rt(3), rt(1), ALU.mult).then_inc(sem("attn_run"), 1)

            dve.wait_ge(sem("l0_carry"), upto("l0_carry", CH * 2))
            dve.memset(carry[:, :], 0.0).then_inc(sem("carry_clear"), 1)
            dve.wait_ge(sem("carry_clear"), 1)

            def l1b(front, back, tail, nodes=True):
                if tail:
                    ln_reduce("l1b", "D", sqD, tail[0])
                if back:
                    ln_reduce("l1b", "S", sqS, back[0])
                if tail:
                    c, b, k = tail
                    ln_inverse("l1b", "D", c)
                    if some(f"tab2_st{b}", k * 16):
                        dve.wait_ge(sem(f"tab2_st{b}"), k * 16)
                    if some("l1b_T2", c - 1):
                        dve.wait_ge(sem("l1b_T2"), upto("l1b_T2", c - 1))
                    ln_apply(dn[b], bank[6][:, :], small[:, 0, 2, :]).then_inc(sem("l1b_D"), 1)
                if front and nodes:
                    nodes_beside(node_added, front[1], front[2], NB1 + CH)
                if back:
                    c, b, k = back
                    ln_inverse("l1b", "S", c)
                    ln_apply(S[:, cs(c)], bank[5][:, :], small[:, 1, 2, :]).then_inc(sem("l1b_S"), 1)
                if front:
                    c, b, k = front
                    if nodes:
                        nodes_beside(node_rest_beside, b, k, NB1 + CH)
                    dve.wait_ge(sem(f"l1b_stream{b}"), upto(f"l1b_stream{b}", (k + 1) * 64))
                    dve.wait_ge(sem("l1b_msg"), upto("l1b_msg", c + 1))
                    if some("l1b_cD", c):
                        dve.wait_ge(sem("l1b_cD"), upto("l1b_cD", c))
                    scan_half("l1b", c, b, msg, 0)
                    scan_half("l1b", c, b, msg, 1)
            dve.wait_ge(sem("attn_out"), 16)

            def l1b_alone(front, back, tail):
                l1b(front, back, tail, nodes=False)
            run_cut(dve, l1b, l1b_alone, 3, CUT, CUT + 4)
            dve.wait_ge(sem("a_stored0"), 16 * (NB // 2))
            dve.wait_ge(sem("a_stored1"), 16 * (NB // 2))

            dve.wait_ge(sem("l1b_carry"), upto("l1b_carry", CH * 2))
            dve.memset(carry[:, :], 0.0).then_inc(sem("carry_clear"), 1)
            dve.wait_ge(sem("carry_clear"), 2)

            def l2(front, mid, back):
                if mid:
                    c, b, k = mid
                    dve.wait_ge(sem(f"l2_keep{b}"), upto(f"l2_keep{b}", (k + 1) * 16))
                    dve.wait_ge(sem("l2_msg"), upto("l2_msg", c + 1))
                    if some("l2_yD", c):
                        dve.wait_ge(sem("l2_yD"), upto("l2_yD", c))
                    scan_half("l2", c, b, msg, 0)
                    scan_half("l2", c, b, msg, 1)
                    ln_reduce("l2", "S", sqS, c)
                if back:
                    ln_reduce("l2", "D", sqD, back[0])
                if mid:
                    ln_inverse("l2", "S", c)
                    ln_apply(S[:, cs(c)], cadd, small[:, 1, 2, :]).then_inc(sem("l2_S"), 1)
                if back:
                    c, b, k = back
                    ln_inverse("l2", "D", c)
                    if some(f"tab3_st{b}", k * 16):
                        dve.wait_ge(sem(f"tab3_st{b}"), k * 16)
                    if some("l2_keepD", c - 1):
                        dve.wait_ge(sem("l2_keepD"), upto("l2_keepD", c - 1))
                    ln_apply(dn[b], bank[0][:, :], small[:, 0, 2, :]).then_inc(sem("l2_D"), 1)
                if front:
                    c, b, k = front
                    put_next_indices("l2", qcol, c, b, k)
                    dve.wait_ge(sem("l2_m"), upto("l2_m", c + 1))
                    dve.wait_ge(sem(f"l2_stream{b}"), upto(f"l2_stream{b}", (k + 1) * 32))
                    dve.tensor_tensor(msg, bank[5][:, :], stream[:, 1, b, :], ALU.mult).then_inc(sem("l2_msg"), 1)
                if front:
                    c, b, k = front
                    dve.wait_ge(sem("l2_cS"), upto("l2_cS", c + 1))
                    if some("l2_S", c):
                        dve.wait_ge(sem("l2_S"), upto("l2_S", c))
                    dve.tensor_tensor(rows64(cadd), rows64(bank[1][:, :]), XR[:, b, :, :], ALU.add
                                      ).then_inc(sem("l2_addS"), 1)
            dve.wait_ge(sem("tab2_st0"), 16 * (CH // 2 + 1))
            dve.wait_ge(sem("tab2_st1"), 16 * (CH // 2))
            dve.wait_ge(sem("l1b_T2"), upto("l1b_T2", CH))
            run_ahead(dve, l2, 3)
            put_first_indices("l3", qcol, "l2")

            dve.wait_ge(sem("l2_carry"), upto("l2_carry", CH * 2))
            dve.memset(carry[:, :], 0.0).then_inc(sem("carry_clear"), 1)
            dve.wait_ge(sem("carry_clear"), 3)
            dve.wait_ge(sem("tab3_st0"), 16 * (CH // 2 + 1))
            dve.wait_ge(sem("tab3_st1"), 16 * (CH // 2))
            dve.wait_ge(sem("l2_keepD"), upto("l2_keepD", CH))

            def weigh(c, b, k):
                dve.wait_ge(sem(f"l3_rows{b}"), upto(f"l3_rows{b}", (k + 1) * ROWS))
                if some("l3_T", c * 2):
                    dve.wait_ge(sem("l3_T"), upto("l3_T", c * 2))
                dve.tensor_tensor(xw2.rearrange("p (s d f) -> p s d f", d=2, f=F),
                                  XR[:, b, :, :].rearrange("p s (o f) -> p s o f", o=1).broadcast_to([P, TPC, 2, F]),
                                  wcol[:, tc(c)].rearrange("p (s o d) -> p s o d", o=1, d=1
                                                           ).broadcast_to([P, TPC, 2, F]),
                                  ALU.mult).then_inc(sem("l3_xw"), 1)

            def mask(c, b, k, q):
                for h in range(2):
                    if q == 0:
                        dve.wait_ge(sem("l3_xAB"), upto("l3_xAB", c * 2 + (h + 1)))
                    if h == 0:
                        if some("l3_pair", c * (REL // 2) + (q - 3)):
                            dve.wait_ge(sem("l3_pair"), upto("l3_pair", c * (REL // 2) + (q - 3)))
                    dve.scalar_tensor_tensor(NT[:, 4 * h + q % 4, :],
                                             (stream[:, 1, b, :], stream2[b])[h].bitcast(I32),
                                             relid[:, q:q + 1], (z1, h1)[h], ALU.is_equal, ALU.mult
                                             ).then_inc(sem("l3_mask"), 1)

            def l3(front, mid, back, scattered):
                if mid:
                    dve.wait_ge(sem(f"l3_stream{mid[1]}"), upto(f"l3_stream{mid[1]}", (mid[2] + 1) * 32))
                    mask(*mid, 0)
                if back:
                    c, b, k = back
                    dve.wait_ge(sem(f"l3_keep{b}"), upto(f"l3_keep{b}", (k + 1) * 16))
                    dve.wait_ge(sem("l3_pair"), upto("l3_pair", (c + 1) * (REL // 2)))
                    if some("l3_rD", c):
                        dve.wait_ge(sem("l3_rD"), upto("l3_rD", c))
                    scan_half("l3", c, b, bank[6 + b], 0)
                    scan_half("l3", c, b, bank[6 + b], 1)
                if mid:
                    for q in range(1, 4):
                        mask(*mid, q)
                if front:
                    weigh(*front)
                    put_next_indices("l3", qcol, *front)
                if mid:
                    for q in range(4, 6):
                        mask(*mid, q)
                if back:
                    c, b, k = back
                    dve.wait_ge(sem("l3_cD"), upto("l3_cD", c + 1))
                    dve.tensor_tensor(eg, bank[0][:, :], D[:, cs(c)], ALU.add).then_inc(sem("l3_addD"), 1)
                if mid:
                    mask(*mid, 6)
                if back:
                    ln_reduce("l3", "D", sqD, c)
                if mid:
                    mask(*mid, 7)
                if back:
                    ln_inverse("l3", "D", c)
                    if some(f"final_st{b}", k * ROWS):
                        dve.wait_ge(sem(f"final_st{b}"), k * ROWS)
                    dve.tensor_copy(sidx_st[:, b, :], outc[:, tc(c)]).then_inc(sem("final_idx"), 1)
                    ln_apply(dn[b], eg, small[:, 0, 2, :]).then_inc(sem("l3_D"), 1)
            dve.wait_ge(sem("a_stored0"), 16 * (NB // 2))
            dve.wait_ge(sem("a_stored1"), 16 * (NB // 2))
            dve.wait_ge(sem("map_st0"), ROWS * (CH // 2 + 1))
            dve.wait_ge(sem("map_st1"), ROWS * (CH // 2))
            run_ahead(dve, l3, 4)


def kernel(**inputs):
    import numpy as np
    import concourse.bacc as bacc
    from concourse import mybir as mb
    from concourse.bass_utils import run_bass_kernel_spmd as run

    g = {k: np.asarray(v) for k, v in inputs.items()}
    x, src, dst = g["x"], g["src"], g["dst"]
    H = F

    def pad_slots(a, fill):
        o = np.full((SLOTS,) + a.shape[1:], fill, a.dtype)
        o[:E] = a
        return o

    def node_cols(a):
        return np.ascontiguousarray(a.reshape(CH, 2, 4, P).transpose(3, 0, 2, 1).reshape(P, TILES))

    def feature_major(a):
        f = a.shape[1]
        return np.ascontiguousarray(a.reshape(CH, 2, CW, f).transpose(1, 3, 0, 2).reshape(2 * f, CH * CW))

    dst_p = pad_slots(dst, N)
    nxt = np.append(dst_p[1:], np.array([-1], dst.dtype))
    run_ = np.concatenate([np.array([-1], dst.dtype), dst_p, np.array([-1], dst.dtype)])
    rows = node_cols(np.arange(SLOTS)) * 0 + (
        (np.arange(CH)[None, :, None] * P + np.arange(P)[:, None, None]) * TPC
        + np.arange(TPC)[None, None, :]).reshape(P, TILES)
    xp = np.zeros((NPAD, F), x.dtype)
    xp[:N] = x
    xT = np.ascontiguousarray(xp.reshape(NB, P, 4, 2, F).transpose(3, 4, 0, 2, 1).reshape(P, NB * CW))

    def bd(a):
        k, m = a.shape
        o = np.zeros((P, P), np.float32)
        o[:k, :m] = a
        o[k:2 * k, m:2 * m] = a
        return o

    W1 = g["L0_gnn_W1"]
    aw = g["L1_gnn_attn_w"]
    Wm, Wa = g["L2_gnn_W_msg_w"], g["L2_gnn_W_apply_w"]
    w3 = np.zeros((P, P), np.float32)
    w3[0:32, 0:64] = g["L0_gnn_W3"].T
    w3[32:64, 64:128] = g["L0_gnn_W3"].T
    attn_rep = np.concatenate([np.repeat(aw[:64, None], P, 1), np.repeat(aw[64:, None], P, 1)])
    piece = {
        "eye": np.eye(P, dtype=np.float32),
        "cen": bd(np.eye(F, dtype=np.float32) - np.float32(1.0 / F)),
        "w_src": bd(g["L0_gnn_W_src"]), "w_tgt": bd(g["L0_gnn_W_tgt"]),
        "w_srcT": bd(g["L0_gnn_W_src"].T),
        "w1aT": bd(W1[:, :64].T), "w1bT": bd(W1[:, 64:128].T), "w1cT": bd(W1[:, 128:].T),
        "w2T": bd(g["L0_gnn_W2"].T), "w3rep": w3,
        "res_wT": bd(g["L1_gnn_res_W"].T), "w_outT": bd(g["L1_gnn_W_out"].T),
        "w_tgtI": np.zeros((P, P), np.float32), "attn_rep": attn_rep,
        "msg1": bd(Wm[:64]), "msg2": bd(Wm[64:]), "app1": bd(Wa[:64]), "app2": bd(Wa[64:]),
        "w_edge": bd(g["L0_gnn_W_edge"]),
    }
    wpack = np.concatenate([piece[n] for n in PIECES], 1)

    def st(v):
        o = np.zeros((P,), np.float32)
        o[:2 * len(v)] = np.concatenate([v, v])
        return o
    z = np.zeros(64, np.float32)
    column = {
        "b_src": st(g["L0_gnn_b_src"]), "b_tgt": st(g["L0_gnn_b_tgt"]), "b_edge": st(g["L0_gnn_b_edge"]),
        "b1": st(g["L0_gnn_b1"]), "b2": st(g["L0_gnn_b2"]), "b3": np.repeat(g["L0_gnn_b3"], P),
        "res_b": st(g["L1_gnn_res_b"]), "b_out": st(g["L1_gnn_b_out"]), "msg_b": st(g["L2_gnn_W_msg_b"]),
        "app_b": st(g["L2_gnn_W_apply_b"]),
        "attn1_0": np.concatenate([aw[:64], z]), "attn1_1": np.concatenate([z, aw[:64]]),
        "attn2_0": np.concatenate([aw[64:], z]), "attn2_1": np.concatenate([z, aw[64:]]),
    }
    cpack = np.ascontiguousarray(np.stack([column[n] for n in COLS], 1))
    rw = g["L3_gnn_weight"].reshape(REL // 2, 2 * F, F).transpose(1, 0, 2).reshape(P, -1)
    relid = (2 * np.arange(REL // 2)[None, :] + (np.arange(P)[:, None] >= F)).astype(np.float32)
    arrays = {
        "x": x,
        "xmap_in": np.concatenate([x, np.full((N, 1), NO_ROW, x.dtype)], 1),
        "xT": xT,
        "dst_col": node_cols(dst_p), "nxt_col": node_cols(nxt), "src_col": node_cols(pad_slots(src, 0)),
        "row_col": rows.astype(np.float32), "dst_run": run_,
        "attr8T": feature_major(pad_slots(g["edge_attr_8"], 0)),
        "attr32T": feature_major(pad_slots(g["edge_attr_32"], 0)),
        "rel_flat": pad_slots(g["edge_type_16"], 0),
        "weight_col": node_cols(pad_slots(g["edge_weight1"][:, 0], 0)),
        "wpack": wpack, "cpack": cpack, "relpack": np.concatenate([rw, relid], 1),
    }
    arrays = {k: np.ascontiguousarray(v) for k, v in arrays.items()}

    nc = bacc.Bacc("TRN2", target_bir_lowering=False, num_devices=1)
    aps = [nc.dram_tensor(f"in_{k}", v.shape, mb.dt.from_np(v.dtype), kind="ExternalInput").ap()
           for k, v in arrays.items()]
    o = nc.dram_tensor("out_0", (NPAD, F), F32, kind="ExternalOutput").ap()
    build(nc, *aps, o)
    r = run(nc, [{f"in_{k}": v for k, v in arrays.items()}], core_ids=[0])
    return r.results[0]["out_0"][:N]
```
